# Optimizing a Trainium2 kernel written in Bass

```python
import numpy as np
import jax
import jax.numpy as jnp

def _softmax(x, axis=-1):
    return jax.nn.softmax(x, axis=axis)

def _gelu(x):
    return jax.nn.gelu(x, approximate=True)

def _silu(x):
    return jax.nn.silu(x)

def _sigmoid(x):
    return jax.nn.sigmoid(x)

def _layernorm(x, axis=-1, eps=1e-05):
    m = jnp.mean(x, axis=axis, keepdims=True)
    v = jnp.var(x, axis=axis, keepdims=True)
    return (x - m) / jnp.sqrt(v + eps)

def _scatter_add(tgt, idx, src, axis=0):
    return tgt.at[idx].add(src)

def _segment_sum(src, seg, n):
    return jax.ops.segment_sum(src, seg, n)
kernel_name = 'mk_macaron_d1_jaxref_r8_b11166'

def setup_inputs(seed: int=0):
    np.random.seed(seed)
    _w = jnp.asarray

    def _L0_attn_setup():
        import jax, jax.numpy as jnp
        import numpy as np
        NUM_HEADS = 16
        CLIP = 16
        key = jax.random.key(seed)
        ks = jax.random.split(key, 7)
        d = 128
        return {'x': jax.random.normal(ks[0], (2, 256, d), dtype=jnp.float32), 'Wq': jax.random.normal(ks[1], (d, d), dtype=jnp.float32) / np.sqrt(d), 'Wk': jax.random.normal(ks[2], (d, d), dtype=jnp.float32) / np.sqrt(d), 'Wv': jax.random.normal(ks[3], (d, d), dtype=jnp.float32) / np.sqrt(d), 'Wo': jax.random.normal(ks[4], (d, d), dtype=jnp.float32) / np.sqrt(d), 'bo': jax.random.normal(ks[5], (d,), dtype=jnp.float32) * 0.01, 'rel_emb': jax.random.normal(ks[6], (CLIP + 1,), dtype=jnp.float32)}
    _L0_attn_in = _L0_attn_setup()

    def _L0_ffn_setup():
        import jax, jax.numpy as jnp
        import numpy as np
        D_IN, D_H, D_OUT = (128, 128, 128)
        D_MOE = 512
        N_EXPERTS = 8
        TOP_K = 2
        key = jax.random.key(seed)
        ks = jax.random.split(key, 10)
        s = lambda d: 1.0 / np.sqrt(d)
        x = jax.random.normal(ks[0], (2, 256, D_IN), dtype=jnp.float32)
        W_in = jax.random.normal(ks[1], (D_IN, D_H), dtype=jnp.float32) * s(D_IN)
        b_in = jnp.zeros((D_H,), jnp.float32)
        W_gate = jax.random.normal(ks[2], (D_H, N_EXPERTS), dtype=jnp.float32) * s(D_H)
        b_gate = jnp.zeros((N_EXPERTS,), jnp.float32)
        W1 = jax.random.normal(ks[3], (N_EXPERTS, D_H, D_MOE), dtype=jnp.float32) * s(D_H)
        b1 = jnp.zeros((N_EXPERTS, D_MOE), jnp.float32)
        W2 = jax.random.normal(ks[4], (N_EXPERTS, D_MOE, D_H), dtype=jnp.float32) * s(D_MOE)
        b2 = jnp.zeros((N_EXPERTS, D_H), jnp.float32)
        W_out = jax.random.normal(ks[5], (D_H, D_OUT), dtype=jnp.float32) * s(D_H)
        b_out = jnp.zeros((D_OUT,), jnp.float32)
        return {'x': x, 'W_in': W_in, 'b_in': b_in, 'W_gate': W_gate, 'b_gate': b_gate, 'W1': W1, 'b1': b1, 'W2': W2, 'b2': b2, 'W_out': W_out, 'b_out': b_out}
    _L0_ffn_in = _L0_ffn_setup()
    _d = {'L0_attn_x': _L0_attn_in['x'], 'L0_attn_Wq': _L0_attn_in['Wq'], 'L0_attn_Wk': _L0_attn_in['Wk'], 'L0_attn_Wv': _L0_attn_in['Wv'], 'L0_attn_Wo': _L0_attn_in['Wo'], 'L0_attn_bo': _L0_attn_in['bo'], 'L0_attn_rel_emb': _L0_attn_in['rel_emb'], 'L0_ffn_W_in': _L0_ffn_in['W_in'], 'L0_ffn_b_in': _L0_ffn_in['b_in'], 'L0_ffn_W_gate': _L0_ffn_in['W_gate'], 'L0_ffn_b_gate': _L0_ffn_in['b_gate'], 'L0_ffn_W1': _L0_ffn_in['W1'], 'L0_ffn_b1': _L0_ffn_in['b1'], 'L0_ffn_W2': _L0_ffn_in['W2'], 'L0_ffn_b2': _L0_ffn_in['b2'], 'L0_ffn_W_out': _L0_ffn_in['W_out'], 'L0_ffn_b_out': _L0_ffn_in['b_out']}
    _x0 = _d['L0_attn_x']
    _d['L0_attn_x'] = jax.random.normal(jax.random.fold_in(jax.random.key(seed), 1), (4, 1024, 128), dtype=_x0.dtype)
    del _x0
    return _d

def reference(L0_attn_x, L0_attn_Wq, L0_attn_Wk, L0_attn_Wv, L0_attn_Wo, L0_attn_bo, L0_attn_rel_emb, L0_ffn_W_in, L0_ffn_b_in, L0_ffn_W_gate, L0_ffn_b_gate, L0_ffn_W1, L0_ffn_b1, L0_ffn_W2, L0_ffn_b2, L0_ffn_W_out, L0_ffn_b_out):

    def _L0_attn_ref(x, Wq, Wk, Wv, Wo, bo, rel_emb):
        import jax, jax.numpy as jnp
        import numpy as np
        NUM_HEADS = 16
        CLIP = 16
        b, s, d_in = x.shape
        h, hd = (NUM_HEADS, x.shape[-1] // NUM_HEADS)
        q = (x @ Wq).reshape(b, s, h, hd).transpose(0, 2, 1, 3)
        k = (x @ Wk).reshape(b, s, h, hd).transpose(0, 2, 1, 3)
        v = (x @ Wv).reshape(b, s, h, hd).transpose(0, 2, 1, 3)
        r = jnp.arange(s)
        dist = jnp.clip(jnp.abs(r[None, :] - r[:, None]), 0, CLIP)
        a_k = rel_emb[dist]
        scores = jnp.einsum('bhqd,bhkd->bhqk', q, k) * a_k
        causal = jnp.triu(jnp.ones((s, s), dtype=bool), k=1)
        scores = jnp.where(causal, -jnp.inf, scores)
        attn = jax.nn.softmax(scores / np.sqrt(hd), axis=-1)
        ctx = jnp.einsum('bhqk,bhkd->bhqd', attn, v)
        ctx = ctx.transpose(0, 2, 1, 3).reshape(b, s, h * hd)
        return ctx @ Wo + bo

    def _L0_ffn_ref(x, W_in, b_in, W_gate, b_gate, W1, b1, W2, b2, W_out, b_out):
        import jax, jax.numpy as jnp
        import numpy as np
        D_IN, D_H, D_OUT = (128, 128, 128)
        D_MOE = 512
        N_EXPERTS = 8
        TOP_K = 2
        B, S, _ = x.shape
        h = x @ W_in + b_in
        t = h.reshape(B * S, -1)
        logits = t @ W_gate + b_gate
        probs = jax.nn.softmax(logits, axis=-1)
        topv, topi = jax.lax.top_k(probs, TOP_K)
        topv = topv / jnp.sum(topv, axis=-1, keepdims=True)
        route = jnp.zeros_like(probs).at[jnp.arange(t.shape[0])[:, None], topi].set(topv)
        mid = jax.nn.relu(jnp.einsum('nd,edh->neh', t, W1) + b1)
        eout = jnp.einsum('neh,ehd->ned', mid, W2) + b2
        moe_out = jnp.einsum('ne,ned->nd', route, eout)
        out = moe_out.reshape(B, S, -1) @ W_out + b_out
        return out
    x = L0_attn_x
    x = x + 0.5 * _L0_ffn_ref(_layernorm(x, axis=-1), L0_ffn_W_in, L0_ffn_b_in, L0_ffn_W_gate, L0_ffn_b_gate, L0_ffn_W1, L0_ffn_b1, L0_ffn_W2, L0_ffn_b2, L0_ffn_W_out, L0_ffn_b_out)
    x = x + _L0_attn_ref(_layernorm(x, axis=-1), L0_attn_Wq, L0_attn_Wk, L0_attn_Wv, L0_attn_Wo, L0_attn_bo, L0_attn_rel_emb)
    x = x + 0.5 * _L0_ffn_ref(_layernorm(x, axis=-1), L0_ffn_W_in, L0_ffn_b_in, L0_ffn_W_gate, L0_ffn_b_gate, L0_ffn_W1, L0_ffn_b1, L0_ffn_W2, L0_ffn_b2, L0_ffn_W_out, L0_ffn_b_out)
    return x

_drawn_inputs = setup_inputs


def setup_inputs(seed=0):
    import zlib

    import numpy as np

    out = dict(_drawn_inputs(seed))
    spreads = {'L0_ffn_b_in': (0.0, 0.1),
     'L0_ffn_b_gate': (0.0, 0.1),
     'L0_ffn_b1': (0.0, 0.1),
     'L0_ffn_b2': (0.0, 0.1),
     'L0_ffn_b_out': (0.0, 0.1)}
    factors = {'L0_attn_bo': 3.357}
    for name, (base, spread) in spreads.items():
        noise = np.random.default_rng([zlib.crc32(name.encode()), seed]).standard_normal(out[name].shape)
        drawn = base * np.exp(spread * noise) if base else spread * noise
        out[name] = jnp.asarray(drawn.astype(out[name].dtype))
    for name, factor in factors.items():
        out[name] = (out[name] * factor).astype(out[name].dtype)
    return out
```

```python
from contextlib import ExitStack

import concourse.bass as bass
from concourse import mybir

F32 = mybir.dt.float32
BF16 = mybir.dt.bfloat16
ALU = mybir.AluOpType
ACT = mybir.ActivationFunctionType
AXX = mybir.AxisListType.X

P = 128
BATCH = 4
SEQ = 1024
TOKENS = BATCH * SEQ
TILES = TOKENS // P
CHUNK = 512
CHUNKS = TOKENS // CHUNK
TPC = CHUNK // P
EXPERTS = 8
HID = 512
HT = HID // P
HEADS = 16
HD = 8
CLIP = 16
GROUPS = HEADS // 4
QT = SEQ // P
BAND = P + CLIP
LN_EPS = 1e-5
MASKED = -1e30
LOWEST = -3e38
SCALE = float(HD) ** -0.5
C_ID, C_SHIFT, C_NEG, C_SEL, C_QLO, C_KLO, C_ONE = 0, 128, 448, 576, 704, 705, 706
C_ALL = 707


def consts():
    import numpy as np
    c = np.zeros((P, C_ALL), np.float32)
    p = np.arange(P)
    c[p, C_ID + p] = 1.0
    c[p, C_SHIFT + 160 + p] = 1.0
    c[:, C_NEG:C_NEG + P] = np.where(np.arange(P)[None, :] > p[:, None], MASKED, 0.0)
    c[32 * (p // 32) + HD, C_SEL + p] = 1.0
    r = p % 32
    c[:, C_QLO] = (r >= 8) & (r < 16)
    c[:, C_KLO] = (r >= 16) & (r < 24)
    c[:, C_ONE] = np.where((r == 24) | (r == 25), -1.0, 0.0)
    return c


def build(nc, x, Wq, Wk, Wv, Wo, bo, rel_emb, W_in, b_in, W_gate, b_gate, W1, b1, W2, b2,
          W_out, b_out, cst, out, phases=("f1", "at", "f2")):
    ctx = ExitStack()
    with ctx:
        def sb(name, shape, dt=F32):
            return ctx.enter_context(nc.sbuf_tensor(name, shape, dt))

        def sem(name):
            return ctx.enter_context(nc.semaphore(name))

        PS = ctx.enter_context(nc.psum_tensor("PS", [P, 8, CHUNK], F32))
        bank = [PS[:, i, :] for i in range(8)]

        X = sb("X", [P, TILES, P])
        C = sb("C", [P, C_ALL])
        ident = C[:, C_ID:C_ID + P]
        ident_bf = sb("ident_bf", [P, P], BF16)
        neg_bf = sb("neg_bf", [P, P], BF16)
        w1_hi, w1_lo = (sb(n, [P, EXPERTS, HID], BF16) for n in ("w1_hi", "w1_lo"))
        w2_hi, w2_lo = (sb(n, [P, EXPERTS, HT, P], BF16) for n in ("w2_hi", "w2_lo"))
        w_in, w_out = sb("w_in", [P, P]), sb("w_out", [P, P])
        w_gate = sb("w_gate", [P, EXPERTS])
        b_in_col = sb("b_in_col", [P, 1])
        b_gate_bc = sb("b_gate_bc", [P, EXPERTS])
        b1_rows = sb("b1_rows", [EXPERTS * HT, P])
        b1_cols = sb("b1_cols", [P, EXPERTS * HT])
        b2_rows = sb("b2_rows", [EXPERTS, P])
        half_b_out = sb("half_b_out", [P, P])
        bo_bc = sb("bo_bc", [P, P])
        rel_bc = sb("rel_bc", [P, CLIP + 1])
        t_hi, t_lo = sb("t_hi", [P, TOKENS], BF16), sb("t_lo", [P, TOKENS], BF16)
        order = sb("order", [P, EXPERTS])
        bn = sb("bn", [P, TILES, 6])
        mean, var, rstd, tmp0, tmp1 = (sb(n, [P, TILES]) for n in ("mean", "var", "rstd", "tmp0", "tmp1"))
        xn = sb("xn", [P, 2, TPC, P])
        big = sb("big", [P, 33000])

        def carve():
            at = [0]

            def take(shape, dt=F32, parts=P):
                n = 1
                for s in shape:
                    n *= s
                words = n if dt == F32 else (n + 1) // 2
                v = big[0:parts, at[0]:at[0] + words]
                at[0] += words
                assert at[0] <= 33000, at[0]
                if dt != F32:
                    v = v.bitcast(dt)
                names = " ".join(f"a{i}" for i in range(len(shape)))
                if len(shape) > 1:
                    v = v.rearrange(f"p ({names}) -> p {names}", **{f"a{i}": s for i, s in enumerate(shape)})
                return v
            return take

        take = carve()
        stage = take([4096])
        xnT, h32 = take([2, CHUNK]), take([2, CHUNK])
        mid32 = take([HT, CHUNK])
        mid_hi, mid_lo = take([2, HT, CHUNK], BF16), take([2, HT, CHUNK], BF16)
        acc = take([TPC, P])
        moT = take([CHUNK])
        routeT = take([CHUNK], parts=EXPERTS)
        route_c = take([TPC, EXPERTS])
        logits, oh1, oh2, rtmp, route = (take([TILES, EXPERTS]) for _ in range(5))
        top1, top2, rt1, rt2 = (take([TILES]) for _ in range(4))

        take = carve()
        wq_hi, wq_lo, wk_hi, wk_lo = (take([GROUPS, P], BF16) for _ in range(4))
        wv_hi, wv_lo = take([P], BF16), take([P], BF16)
        wo_rep = take([GROUPS, P])
        A = take([BAND])
        D = take([CLIP])
        sq_far, sq_band = take([1]), take([1])
        pr32 = take([2, CHUNK])
        part_far, part_band = take([2, CHUNK], BF16), take([2, CHUNK], BF16)
        QF, QB = take([2, SEQ], BF16), take([2, SEQ], BF16)
        Kfull = take([2, CHUNK], BF16)
        KM = take([2, 4, SEQ], BF16)
        T = take([QT, 4, BAND])
        TD = take([QT, 4, P])
        E = take([2, QT, 4, 32], parts=CLIP)
        mxp = take([QT, 4, 3])
        nmax, nmr = take([QT, 4]), take([QT, 4])
        M4 = take([QT, P], BF16)
        PT = take([2, 4, CHUNK])
        vaug = take([QT, HEADS, 32])
        cs = take([CHUNK])
        crec = take([CHUNK])
        ctxn = take([2, CHUNK])
        ptw = PT.rearrange("p a b c -> p (a b c)")
        xT32 = ptw[:, 0:2 * CHUNK].rearrange("p (s c) -> p s c", s=2)
        wqkv = ptw[:, 1024:1024 + 3 * P].rearrange("p (w n) -> p w n", w=3)
        wq_rep = ptw[:, 1536:2048].rearrange("p (h r) -> p h r", h=HEADS)
        wk_rep = ptw[:, 2048:2560].rearrange("p (h r) -> p h r", h=HEADS)

        s_x = sem("x_loaded")
        s_w = sem("weights_loaded")
        s_stage = sem("expert_weights_staged")
        s_hi = sem("expert_hi_ready")
        s_lo = sem("expert_lo_ready")
        s_vc = sem("vector_chain")
        s_cst = sem("constants_ready")
        s_b1T = sem("b1_transposed")
        s_b1 = sem("b1_cols_ready")
        s_out = sem("stored")
        s_in_done = sem("phase_done")

        block = ctx.enter_context(nc.Block())

        chain = [0]

        def link(dve, ins):
            chain[0] += 1
            ins.then_inc(s_vc, 1)
            dve.wait_ge(s_vc, chain[0])

        def ffn_semaphores(n):
            return {s: sem(f"ffn{n}_{s}") for s in (
                "stats", "sd", "xn_ready", "tr_full", "xnT_ready", "h_full", "h32_ready", "lg_full", "lg_ready",
                "hi_ready", "lo_ready", "rt_d", "rt_e", "route_ready", "up_full", "mid32_ready", "hi_act", "hi_dve",
                "lo_done", "dn_full", "acc_chain", "rc_ready", "rT_full", "rT_ready", "fa_full", "fa_ready",
                "fb_full", "x_done", "fa_chain")}

        F = {1: ffn_semaphores(1), 2: ffn_semaphores(2)}

        def dve_stats(dve, stats_sem, sd_sem):
            for t in range(TILES):
                ins = dve.bn_stats(bn[:, t, :], X[:, t, :])
            link(dve, ins)
            m_e, v_e, m_o, v_o = bn[:, :, 1], bn[:, :, 2], bn[:, :, 4], bn[:, :, 5]
            dve.tensor_tensor(mean[:], m_e, m_o, ALU.add)
            dve.tensor_tensor(tmp0[:], m_e, m_o, ALU.subtract)
            link(dve, dve.tensor_tensor(var[:], v_e, v_o, ALU.add))
            dve.tensor_scalar(mean[:], mean[:], 0.5, None, ALU.mult)
            dve.tensor_tensor(tmp1[:], tmp0[:], tmp0[:], ALU.mult)
            link(dve, dve.tensor_scalar(var[:], var[:], 1.0 / P, LN_EPS, ALU.mult, ALU.add))
            link(dve, dve.scalar_tensor_tensor(out=var[:], in0=tmp1[:], scalar=0.25, in1=var[:],
                                               op0=ALU.mult, op1=ALU.add))
            dve.sem_inc(stats_sem, 1)
            dve.wait_ge(sd_sem, 1)
            link(dve, dve.reciprocal(rstd[:], tmp0[:]))
            link(dve, dve.tensor_tensor(tmp1[:], rstd[:], rstd[:], ALU.mult))
            link(dve, dve.tensor_tensor(tmp1[:], tmp1[:], var[:], ALU.mult))
            link(dve, dve.tensor_scalar(tmp1[:], tmp1[:], -0.5, 1.5, ALU.mult, ALU.add))
            link(dve, dve.tensor_tensor(rstd[:], rstd[:], tmp1[:], ALU.mult))

        def dve_normalise(dve, xn_ready, tr_full):
            with dve.Fori(0, CHUNKS // 2) as c2:
                for u in range(2):
                    dve.wait_ge(tr_full, c2 * 2 + (u + 1))
                    for k in range(TPC):
                        t = bass.ds(c2 * (2 * TPC) + (u * TPC + k), 1)
                        ins = dve.tensor_scalar(xn[:, u, k, :], X[:, t, :].rearrange("p a d -> p (a d)"), mean[:, t], rstd[:, t],
                                                ALU.subtract, ALU.mult)
                    ins.then_inc(xn_ready, 1)

        B_UNITS = [(i, u) for i in range(QT) for u in range(2)]

        def b_steps(i):
            far = max(P * i - CLIP, 0)
            if far + BAND <= CHUNK:
                return [(0, far, True)]
            cut = min(far, CHUNK)
            return [(0, cut, False), (cut, far, True)]

        B_COUNT = []
        n = 0
        for i in range(QT):
            B_COUNT.append(n)
            n += len(b_steps(i))
        B_PER = n
        C_UNITS = [(c, k) for c in range(SEQ // CHUNK) for k in range(TPC * (c + 1))]
        CU = len(C_UNITS)

        def slot_plan(g, lead):
            ev = []
            pieces = [("A", g, p) for p in range(4)] if g == 0 else []
            cs_ = {}
            if lead:
                ev.append(("M",))
            if g == 0:
                for p in range(4):
                    ev.append(pieces[p])
                    if p:
                        ev.append(("AD", g, p - 1))
                    if lead and p == 0:
                        ev.append(("M2",))
                    if lead and p:
                        ev.append(("C", p - 1))
                ev.append(("AD", g, 3))
                nxt = 3
            else:
                nxt = 0
            for k, (i, u) in enumerate(B_UNITS):
                ev.append(("B", i, u))
                if g > 0 and k == 0:
                    ev.append(("M2",))
                if lead and nxt <= CU and (g == 0 or k > 0):
                    ev.append(("C", nxt))
                    if nxt == 6:
                        ev.append(("N", 0))
                    if nxt == 7:
                        ev.append(("O", 0))
                    nxt += 1
                elif lead and nxt == CU + 1:
                    ev.append(("N", 1))
                    nxt += 1
                elif lead and nxt == CU + 2:
                    ev.append(("O", 1))
                    nxt += 1
                if g < GROUPS - 1 and k >= 12:
                    ev.append(("A", g + 1, k - 12))
                    if k > 12:
                        ev.append(("AD", g + 1, k - 13))
            while lead and nxt <= CU + 2:
                ev.append([("C", CU), ("N", 1), ("O", 1)][nxt - CU])
                nxt += 1
            if g < GROUPS - 1:
                ev.append(("AD", g + 1, 3))
            if g == 0:
                ev += [("V", 0), ("V", 1)]
            return ev

        TAIL = [("M",), ("M2",)] + [e for n in range(CU + 1) for e in
                                    [("C", n)] + ([("N", 0)] if n == 6 else []) + ([("O", 0)] if n == 7 else [])] \
            + [("N", 1), ("O", 1)]

        def run_plan(eng, handler):
            def batch(b, first):
                for g in range(GROUPS):
                    lead = not (first and g == 0)
                    pb, pg = (b, g - 1) if g else (b - 1, GROUPS - 1)
                    for ev in slot_plan(g, lead):
                        handler(eng, ev, b, g, pb, pg, first and g == 0, first and g <= 1)
            batch(0, True)
            with eng.Fori(1, BATCH) as b:
                batch(b, False)
            for ev in TAIL:
                handler(eng, ev, BATCH, 0, BATCH - 1, GROUPS - 1, False, False)

        def attention_handlers():
            a = {s_: sem("attn_" + s_) for s_ in (
                "stats", "sd", "xn_ready", "tr_full", "xT_ready", "hi_ready", "lo_ready", "w_loaded", "w_rep", "w_hi",
                "w_lo", "zeroed", "band_chain", "band_ready", "bo_added", "pr_full", "pr_ready", "split_done",
                "part_ready", "q_ready", "k_ready", "v_full", "v_ready", "t_ready", "mx_done", "m_chain", "m4_ready",
                "nm_ready", "mt_full", "mt_done", "td_ready", "s_full", "exp_done", "pv_done", "cs_ready", "den_full",
                "rec_ready", "ctxn_ready", "o_full", "x_added", "pool_steps")}
            a["b_full"] = [sem(f"attn_b_full{u}") for u in range(2)]
            a["b_free"] = [sem(f"attn_b_free{u}") for u in range(2)]

            def at_group(pb, pg, per, k):
                return pb * (GROUPS * per) + (pg * per + k)

            def pe_h(pe, ev, b, g, pb, pg, fresh, young):
                kind = ev[0]
                par, ppar = g % 2, pg % 2
                if kind == "A":
                    ag, p = ev[1], ev[2]
                    w_h, w_l = (wq_hi, wq_lo) if p < 2 else (wk_hi, wk_lo)
                    cols = bass.ds(b * SEQ + CHUNK * (p % 2), CHUNK)
                    misc_wait(pe)
                    pe.matmul(bank[7], w_h[:, ag, :], t_hi[:, cols], start=True, stop=False)
                    pe.matmul(bank[7], w_h[:, ag, :], t_lo[:, cols], start=False, stop=False)
                    pe.matmul(bank[7], w_l[:, ag, :], t_hi[:, cols], start=False, stop=True).then_inc(a["pr_full"], 1)
                    misc_used(a["pr_ready"], at_group(b, ag, 4, p + 1))
                elif kind == "V":
                    r = ev[1]
                    misc_wait(pe)
                    for k in range(TPC):
                        tok = bass.ds(b * SEQ + P * (TPC * r + k), P)
                        o = bank[7][:, P * k:P * (k + 1)]
                        pe.matmul(o, t_hi[:, tok], wv_hi, start=(k == 0), stop=False, skip_group_check=True)
                        pe.matmul(o, t_hi[:, tok], wv_lo, start=False, stop=False, skip_group_check=True)
                        ins = pe.matmul(o, t_lo[:, tok], wv_hi, start=False, stop=True, skip_group_check=True)
                    ins.then_inc(a["v_full"], 1)
                    misc_used(a["v_ready"], b * 2 + (r + 1))
                elif kind == "B":
                    i, u = ev[1], ev[2]
                    if i == 0 and u == 0:
                        pe.wait_ge(a["k_ready"], at_group(b, g, 2, 2))
                        pe.wait_ge(a["q_ready"], at_group(b, g, 2, 2))
                    for n, (k0, k1, band) in enumerate(b_steps(i)):
                        cnt = B_COUNT[i] + n
                        if not (fresh and cnt == 0):
                            pe.wait_ge(a["b_free"][u], at_group(b, g, B_PER, cnt))
                        far = k1 - k0
                        for j in (2 * u, 2 * u + 1):
                            bk = bank[j]
                            qs = slice(P * i, P * (i + 1))
                            if band:
                                pe.matmul(bk[:, far + (CLIP if i else 0):far + (BAND if i else P)], ident_bf[:], neg_bf[:],
                                          start=True, stop=False, skip_group_check=True)
                            if far:
                                ins = pe.matmul(bk[:, 0:far], QF[:, par, qs], KM[:, par, j, k0:k1],
                                                start=not band, stop=True, skip_group_check=True)
                            if band:
                                ins = pe.matmul(bk[:, far:far + (BAND if i else P)], QB[:, par, qs],
                                                KM[:, par, j, k1:k1 + (BAND if i else P)], start=False, stop=True,
                                                skip_group_check=True)
                        ins.then_inc(a["b_full"][u], 1)
                elif kind in ("M", "M2"):
                    r = 0 if kind == "M" else 1
                    pe.wait_ge(a["m4_ready"], at_group(pb, pg, 1, 1))
                    misc_wait(pe)
                    for k in range(TPC):
                        ins = pe.matmul(bank[7][:, P * k:P * (k + 1)], M4[:, TPC * r + k, :], ident_bf[:],
                                        start=(k == 0), stop=True, skip_group_check=True)
                    ins.then_inc(a["mt_full"], 1)
                    misc_used(a["mt_done"], at_group(pb, pg, 2, r + 1))
                elif kind == "C":
                    n = ev[1]
                    if n < CU:
                        c, kt = C_UNITS[n]
                        q0 = max(CHUNK * c, P * kt)
                        off = q0 - CHUNK * c
                        diag = P * kt >= CHUNK * c
                        if kt == 0:
                            pe.wait_ge(a["mt_done"], at_group(pb, pg, 2, c + 1))
                        if diag:
                            pe.wait_ge(a["td_ready"], at_group(pb, pg, QT, kt + 1))
                        for j in range(4):
                            idx = 4 * n + j
                            bk = bank[4 + idx % 2]
                            if not (young and idx < 2 and pg == 0):
                                pe.wait_ge(a["exp_done"], at_group(pb, pg, 4 * CU, idx - 1))
                            far = off
                            if diag:
                                ins = pe.matmul(bk[:, off:off + P], TD[:, kt, j, :], ident, start=True, stop=True,
                                                is_transpose=True, skip_group_check=True)
                                far = off + P
                            if far < CHUNK:
                                ins = pe.matmul(bk[:, far:], KM[:, ppar, j, P * kt:P * (kt + 1)],
                                                QF[:, ppar, CHUNK * c + far:CHUNK * (c + 1)], start=not diag, stop=True,
                                                skip_group_check=True)
                            nq = P * (kt + 1) - CHUNK * c
                            if 0 <= nq < CHUNK:
                                ins = pe.matmul(bk[96:128, nq:nq + CLIP], E[:, ppar, kt + 1, j, :], ident[0:CLIP, 0:CLIP],
                                                start=False, stop=True, skip_group_check=True)
                            ins.then_inc(a["s_full"], 1)
                    if n > 0:
                        c, kt = C_UNITS[n - 1]
                        off = max(CHUNK * c, P * kt) - CHUNK * c
                        pe.wait_ge(a["exp_done"], at_group(pb, pg, 4 * CU, 4 * n))
                        if n == 1:
                            pe.wait_ge(a["v_ready"], pb * 2 + 2)
                        if kt == 0 and not (young and c == 0 and pg == 0):
                            pe.wait_ge(a["cs_ready"], at_group(pb, pg, 2, c))
                        last = kt == TPC * (c + 1) - 1
                        for j in range(4):
                            ins = pe.matmul(bank[6][32 * j:32 * (j + 1), off:], vaug[:, kt, 4 * pg + j, :],
                                            PT[:, (n - 1) % 2, j, off:], start=(kt == 0), stop=last,
                                            skip_group_check=True)
                        ins.then_inc(a["pv_done"], 1)
                elif kind == "N":
                    c = ev[1]
                    pe.wait_ge(a["cs_ready"], at_group(pb, pg, 2, c + 1))
                    misc_wait(pe)
                    pe.matmul(bank[7], C[:, C_SEL:C_SEL + P], cs, start=True, stop=True).then_inc(a["den_full"], 1)
                    misc_used(a["rec_ready"], at_group(pb, pg, 2, c + 1))
                elif kind == "O":
                    c = ev[1]
                    pe.wait_ge(a["ctxn_ready"], at_group(pb, pg, 2, c + 1))
                    misc_wait(pe)
                    for k in range(TPC):
                        ins = pe.matmul(bank[7][:, P * k:P * (k + 1)], ctxn[:, c, P * k:P * (k + 1)], wo_rep[:, pg, :],
                                        start=(k == 0), stop=True, skip_group_check=True)
                    ins.then_inc(a["o_full"], 1)
                    misc_used(a["x_added"], at_group(pb, pg, 2, c + 1))

            misc = [None]

            def misc_wait(pe):
                if misc[0] is not None:
                    pe.wait_ge(*misc[0])

            def misc_used(sem_, value):
                misc[0] = (sem_, value)

            def act_h(act, ev, b, g, pb, pg, fresh, young):
                kind = ev[0]
                if kind == "A":
                    ag, p = ev[1], ev[2]
                    act.wait_ge(a["pr_full"], at_group(b, ag, 4, p + 1))
                    if not (fresh and ag == 0 and p < 2):
                        act.wait_ge(a["split_done"], at_group(b, ag, 4, p - 1))
                    act.activation(pr32[:, p % 2, :], bank[7], ACT.Identity).then_inc(a["pr_ready"], 1)
                elif kind == "V":
                    r = ev[1]
                    act.wait_ge(a["v_full"], b * 2 + (r + 1))
                    act.activation(vaug[:, TPC * r:TPC * (r + 1), :, 0:HD].rearrange("p t h d -> p (t h) d"),
                                   bank[7].rearrange("p (th d) -> p th d", d=HD),
                                   ACT.Identity).then_inc(a["v_ready"], 1)
                elif kind == "C":
                    n = ev[1]
                    if n in (5, CU):
                        c = 0 if n == 5 else 1
                        act.wait_ge(a["pv_done"], at_group(pb, pg, CU, 4 if c == 0 else CU))
                        if not (young and c == 0 and pg == 0):
                            act.wait_ge(a["ctxn_ready"], at_group(pb, pg, 2, c))
                        act.activation(cs, bank[6], ACT.Identity).then_inc(a["cs_ready"], 1)
                    if n < CU:
                        c, kt = C_UNITS[n]
                        off = max(CHUNK * c, P * kt) - CHUNK * c
                        if not (young and n < 2 and pg == 0):
                            act.wait_ge(a["pv_done"], at_group(pb, pg, CU, n - 1))
                        for j in range(4):
                            idx = 4 * n + j
                            act.wait_ge(a["s_full"], at_group(pb, pg, 4 * CU, idx + 1))
                            act.activation(PT[:, n % 2, j, off:], bank[4 + idx % 2][:, off:],
                                           ACT.Exp).then_inc(a["exp_done"], 1)

            def pool_h(pool, ev, b, g, pb, pg, fresh, young):
                kind = ev[0]
                if kind == "A":
                    ag, p = ev[1], ev[2]
                    pool.wait_ge(a["pr_ready"], at_group(b, ag, 4, p + 1))
                    if not (fresh and ag == 0 and p < 2):
                        pool.wait_ge(a["split_done"], at_group(b, ag, 4, p - 1))
                    pool.sem_inc(a["pool_steps"], 1)
                    s = p % 2
                    if p < 2:
                        pool.tensor_scalar(part_far[:, s, :], pr32[:, s, :], sq_far, C[:, C_QLO:C_QLO + 1],
                                           ALU.mult, ALU.mult)
                        pool.tensor_scalar(part_band[:, s, :], pr32[:, s, :], sq_band, C[:, C_QLO:C_QLO + 1],
                                           ALU.mult, ALU.mult).then_inc(a["part_ready"], 1)
                    else:
                        pool.tensor_scalar(part_far[:, s, :], pr32[:, s, :], C[:, C_KLO:C_KLO + 1],
                                           C[:, C_ONE:C_ONE + 1], ALU.mult, ALU.add).then_inc(a["part_ready"], 1)
                elif kind == "M":
                    pool.wait_ge(a["nm_ready"], at_group(pb, pg, 1, 1))
                    if not (young and pg == 0):
                        pool.wait_ge(a["s_full"], at_group(pb, pg, 4 * CU, 0))
                    for i in range(QT):
                        pool.tensor_tensor(TD[:, i, :, :], T[:, i, :, CLIP:],
                                           nmr[:, i, :].unsqueeze(2).to_broadcast([P, 4, P]),
                                           ALU.add).then_inc(a["td_ready"], 1)

            def dve_h(dve, ev, b, g, pb, pg, fresh, young):
                kind = ev[0]
                par, ppar = g % 2, pg % 2
                if kind == "AD":
                    ag, p = ev[1], ev[2]
                    s, apar = p % 2, ag % 2
                    cols = slice(CHUNK * s, CHUNK * (s + 1))
                    dve.wait_ge(a["part_ready"], at_group(b, ag, 4, p + 1))
                    if p < 2:
                        dve.scalar_tensor_tensor(out=QF[:, apar, cols], in0=pr32[:, s, :], scalar=sq_far,
                                                 in1=part_far[:, s, :], op0=ALU.mult, op1=ALU.subtract)
                        dve.scalar_tensor_tensor(out=QB[:, apar, cols], in0=pr32[:, s, :], scalar=sq_band,
                                                 in1=part_band[:, s, :], op0=ALU.mult,
                                                 op1=ALU.subtract).then_inc(a["split_done"], 1)
                        dve.wait_ge(a["split_done"], at_group(b, ag, 4, p + 1))
                        dve.sem_inc(a["q_ready"], 1)
                    else:
                        dve.tensor_tensor(Kfull[:, s, :], pr32[:, s, :], part_far[:, s, :],
                                          ALU.subtract).then_inc(a["split_done"], 1)
                        dve.wait_ge(a["split_done"], at_group(b, ag, 4, p + 1))
                        for j in range(4):
                            rows = slice(32 * j, 32 * (j + 1))
                            ins = dve.tensor_copy(KM[rows, apar, j, cols], Kfull[rows, s, :])
                        ins.then_inc(a["k_ready"], 1)
                elif kind == "B":
                    i, u = ev[1], ev[2]
                    pair = PS[:, 2 * u:2 * u + 2, :]
                    js = slice(2 * u, 2 * u + 2)
                    for n, (k0, k1, band) in enumerate(b_steps(i)):
                        cnt = B_COUNT[i] + n
                        far = k1 - k0
                        dve.wait_ge(a["b_full"][u], at_group(b, g, B_PER, cnt + 1))
                        if not band:
                            dve.tensor_reduce(mxp[:, i, js, 0], pair[:, :, 0:far], AXX,
                                              ALU.max).then_inc(a["b_free"][u], 1)
                            continue
                        lo = 0 if i else CLIP
                        w = BAND - lo
                        if not fresh:
                            dve.wait_ge(a["td_ready"], at_group(b, g, QT, i + 1 - QT))
                        if i:
                            dve.tensor_tensor(E[:, par, i, js, CLIP:], pair[0:CLIP, :, far:far + CLIP],
                                              D[0:CLIP, :].unsqueeze(1).to_broadcast([CLIP, 2, CLIP]), ALU.mult)
                        ins = dve.tensor_tensor(T[:, i, js, lo:], pair[:, :, far:far + w],
                                                A[:, lo:].unsqueeze(1).to_broadcast([P, 2, w]), ALU.mult)
                        if far:
                            ins.then_inc(a["t_ready"], 1)
                            dve.tensor_reduce(mxp[:, i, js, 1], pair[:, :, 0:far], AXX,
                                              ALU.max).then_inc(a["b_free"][u], 1)
                        else:
                            ins.then_inc(a["b_free"][u], 1)
                        if far:
                            dve.wait_ge(a["t_ready"], at_group(b, g, 2 * T_PER, T_AT[i] + u + 1))
                        else:
                            dve.wait_ge(a["b_free"][u], at_group(b, g, B_PER, cnt + 1))
                        dve.tensor_reduce(mxp[:, i, js, 2], T[:, i, js, lo:], AXX, ALU.max).then_inc(a["mx_done"], 1)
                elif kind == "M":
                    k = [0]
                    dve.wait_ge(a["mx_done"], at_group(pb, pg, 2 * QT, 2 * QT))
                    m4v = M4.rearrange("p t (j r) -> p t j r", r=32)

                    def step(ins):
                        k[0] += 1
                        ins.then_inc(a["m_chain"], 1)
                        dve.wait_ge(a["m_chain"], at_group(pb, pg, 3, k[0]))
                    step(dve.tensor_reduce(nmax, mxp, AXX, ALU.max, negate=True))
                    step(dve.tensor_copy(m4v[:, :, :, 24], nmax))
                    step(dve.tensor_tensor(m4v[:, :, :, 25], nmax, m4v[:, :, :, 24], ALU.subtract))
                    dve.sem_inc(a["m4_ready"], 1)
                    dve.tensor_tensor(nmr, m4v[:, :, :, 24], m4v[:, :, :, 25], ALU.add).then_inc(a["nm_ready"], 1)
                elif kind == "M2":
                    for r in range(2):
                        cols = slice(CHUNK * r, CHUNK * (r + 1))
                        dve.wait_ge(a["mt_full"], at_group(pb, pg, 2, r + 1))
                        dve.tensor_tensor(QF[:, ppar, cols], bank[7], QF[:, ppar, cols],
                                          ALU.add).then_inc(a["mt_done"], 1)
                elif kind == "N":
                    c = ev[1]
                    dve.wait_ge(a["den_full"], at_group(pb, pg, 2, c + 1))
                    dve.reciprocal(crec, bank[7]).then_inc(a["rec_ready"], 1)
                    dve.wait_ge(a["rec_ready"], at_group(pb, pg, 2, c + 1))
                    dve.tensor_tensor(ctxn[:, c, :], cs, crec, ALU.mult).then_inc(a["ctxn_ready"], 1)
                elif kind == "O":
                    c = ev[1]
                    dve.wait_ge(a["o_full"], at_group(pb, pg, 2, c + 1))
                    if not (young and c == 0 and pg == 0):
                        dve.wait_ge(a["x_added"], at_group(pb, pg, 2, c))
                    tiles = bass.ds(pb * QT + TPC * c, TPC)
                    dve.tensor_tensor(X[:, tiles, :], bank[7].rearrange("p (t d) -> p t d", t=TPC), X[:, tiles, :],
                                      ALU.add).then_inc(a["x_added"], 1)

            return a, pe_h, act_h, pool_h, dve_h

        T_AT, n = [], 0
        for i in range(QT):
            T_AT.append(n)
            n += 2 * (b_steps(i)[-1][1] - b_steps(i)[-1][0] > 0)
        T_PER = n // 2

        a, pe_h, act_h, pool_h, dve_h = attention_handlers() if "at" in phases else (None,) * 5

        def sp_attention(sp):
            if "f1" in phases:
                sp.wait_ge(F[1]["x_done"], CHUNKS)
            else:
                sp.wait_ge(s_lo, 2)
            for i, w in enumerate((Wq, Wk, Wv)):
                sp.dma_start(wqkv[:, i, :], w).then_inc(a["w_loaded"], 16)
            sp.wait_ge(a["zeroed"], 1)
            for j in range(4):
                sp.dma_start(wo_rep[32 * j:32 * j + HD, :, :],
                             Wo.rearrange("(g j d) n -> j d g n", j=4, d=HD)[j]).then_inc(a["w_loaded"], 16)

        def pool_attention(pool):
            if "f1" in phases:
                pool.wait_ge(F[1]["x_done"], CHUNKS)
            else:
                pool.wait_ge(s_lo, 2)
            pool.memset(wo_rep, 0.0).then_inc(a["zeroed"], 1)
            pool.memset(wq_rep, 0.0)
            pool.memset(wk_rep, 0.0)
            pool.memset(M4, 0.0)
            pool.memset(E, 0.0)
            pool.memset(KM, 0.0)
            pool.memset(mxp, LOWEST)
            pool.memset(vaug, 0.0).then_inc(a["zeroed"], 1)
            pool.wait_ge(a["zeroed"], 2)
            pool.memset(vaug[:, :, :, HD:HD + 1], 1.0).then_inc(a["zeroed"], 1)
            pool.wait_ge(a["w_loaded"], 16 * 7)
            for rep_, i in ((wq_rep, 0), (wk_rep, 1)):
                for r in range(3):
                    ins = pool.tensor_copy(rep_[:, :, HD * r:HD * (r + 1)],
                                           wqkv[:, i, :].rearrange("p (h d) -> p h d", d=HD))
            ins.then_inc(a["w_rep"], 1)
            pool.sem_inc(a["lo_ready"], 2)
            with pool.Fori(0, CHUNKS // 2) as c2:
                for u in range(2):
                    pool.wait_ge(a["hi_ready"], c2 * 2 + (u + 1))
                    cols = bass.ds(c2 * (2 * CHUNK) + u * CHUNK, CHUNK)
                    pool.tensor_tensor(t_lo[:, cols], xT32[:, u, :], t_hi[:, cols],
                                       ALU.subtract).then_inc(a["lo_ready"], 1)
            pool.wait_ge(a["band_ready"], 1)
            run_plan(pool, pool_h)

        def act_attention(act):
            act.wait_ge(a["stats"], 1)
            act.activation(tmp0[:], var[:], ACT.Sqrt).then_inc(a["sd"], 1)
            act.wait_ge(a["w_rep"], 1)
            for hi, src in ((wq_hi, wq_rep), (wk_hi, wk_rep)):
                act.activation(hi.rearrange("p g c -> p (g c)"), src.rearrange("p h r -> p (h r)"), ACT.Identity)
            act.activation(wv_hi, wqkv[:, 2, :], ACT.Identity).then_inc(a["w_hi"], 1)
            with act.Fori(0, CHUNKS // 2) as c2:
                for u in range(2):
                    c1 = c2 * 2 + (u + 1)
                    act.wait_ge(a["tr_full"], c1 + 2)
                    act.wait_ge(a["lo_ready"], c1)
                    act.activation(xT32[:, u, :], bank[u], ACT.Identity).then_inc(a["xT_ready"], 1)
                    act.wait_ge(a["xT_ready"], c1 + 2)
                    act.activation(t_hi[:, bass.ds(c2 * (2 * CHUNK) + u * CHUNK, CHUNK)], xT32[:, u, :],
                                   ACT.Identity).then_inc(a["hi_ready"], 1)
            act.wait_ge(a["lo_ready"], CHUNKS + 2)
            act.wait_ge(a["w_lo"], 1)
            act.wait_ge(a["zeroed"], 3)
            run_plan(act, act_h)

        def pe_attention(pe):
            pe.sem_inc(a["tr_full"], 2)
            with pe.Fori(0, CHUNKS // 2) as c2:
                for u in range(2):
                    c1 = c2 * 2 + (u + 1)
                    pe.wait_ge(a["xT_ready"], c1)
                    pe_transpose_chunk(pe, u, a["xn_ready"], a["tr_full"], c1)
            pe.wait_ge(a["lo_ready"], CHUNKS + 2)
            pe.wait_ge(a["hi_ready"], CHUNKS)
            pe.wait_ge(a["w_lo"], 1)
            pe.wait_ge(a["xT_ready"], CHUNKS + 2)
            run_plan(pe, pe_h)

        def dve_attention(dve):
            dve_stats(dve, a["stats"], a["sd"])
            dve.sem_inc(a["xT_ready"], 2)
            dve_normalise(dve, a["xn_ready"], a["tr_full"])
            dve.wait_ge(a["xn_ready"], CHUNKS)
            dve.tensor_tensor(X[:], X[:], bo_bc[:].unsqueeze(1).to_broadcast([P, TILES, P]),
                              ALU.add).then_inc(a["bo_added"], 1)
            dve.wait_ge(a["bo_added"], 1)
            link(dve, dve.tensor_scalar(sq_far, rel_bc[:, CLIP:CLIP + 1], SCALE, None, ALU.mult))
            link(dve, dve.memset(sq_band, SCALE))
            rel_diff = crec[:, 0:CLIP]
            link(dve, dve.tensor_scalar(rel_diff, rel_bc[:, 0:CLIP], rel_bc[:, CLIP:CLIP + 1], None, ALU.subtract))
            link(dve, dve.memset(A, 0.0))
            for dist in range(CLIP):
                ind = C[:, C_SHIFT + 144 + dist:C_SHIFT + 144 + dist + BAND]
                link(dve, dve.scalar_tensor_tensor(out=A, in0=ind, scalar=rel_diff[:, dist:dist + 1], in1=A,
                                                   op0=ALU.mult, op1=ALU.add))
            link(dve, dve.tensor_copy(D, A[:, 0:CLIP]))
            link(dve, dve.tensor_scalar(A, A, rel_bc[:, CLIP:CLIP + 1], None, ALU.add))
            msk, m2 = crec[:, 0:P], crec[:, P:2 * P]
            link(dve, dve.tensor_scalar(msk, C[:, C_NEG:C_NEG + P], 0.0, None, ALU.is_lt))
            link(dve, dve.tensor_scalar(m2, A[:, CLIP:], -1.0, 1.0, ALU.mult, ALU.add))
            link(dve, dve.tensor_tensor(m2, m2, msk, ALU.mult))
            link(dve, dve.tensor_tensor(A[:, CLIP:], A[:, CLIP:], m2, ALU.add))
            dve.sem_inc(a["band_ready"], 1)
            dve.wait_ge(a["w_hi"], 1)
            for lo, hi, src in ((wq_lo, wq_hi, wq_rep), (wk_lo, wk_hi, wk_rep)):
                dve.tensor_tensor(lo.rearrange("p g c -> p (g c)"), src.rearrange("p h r -> p (h r)"),
                                  hi.rearrange("p g c -> p (g c)"), ALU.subtract)
            dve.tensor_tensor(wv_lo, wqkv[:, 2, :], wv_hi, ALU.subtract).then_inc(a["w_lo"], 1)
            dve.wait_ge(a["w_lo"], 1)
            dve.wait_ge(a["zeroed"], 3)
            run_plan(dve, dve_h)
            dve.wait_ge(a["x_added"], BATCH * GROUPS * 2)


        @block.sync
        def _(sp):
            sp.dma_start(C[:], cst).then_inc(s_w, 16)
            for b in range(BATCH):
                sp.dma_start(X[:, QT * b:QT * (b + 1), :],
                             x[b].rearrange("(t p) d -> p t d", p=P)).then_inc(s_x, 16)
            sp.dma_start(w_in[:], W_in).then_inc(s_w, 16)
            sp.dma_start(w_gate[:], W_gate).then_inc(s_w, 16)
            sp.dma_start(b_in_col[:], b_in.rearrange("(p a) -> p a", a=1)).then_inc(s_w, 16)
            sp.dma_start(b_gate_bc[:], b_gate.partition_broadcast(P)).then_inc(s_w, 16)
            sp.dma_start(b1_rows[:], b1.rearrange("e (t p) -> (e t) p", p=P)).then_inc(s_w, 16)
            sp.dma_start(b2_rows[:], b2).then_inc(s_w, 16)
            sp.dma_start(w_out[:], W_out).then_inc(s_w, 16)
            sp.dma_start(half_b_out[:], b_out.partition_broadcast(P)).then_inc(s_w, 16)
            sp.dma_start(bo_bc[:], bo.partition_broadcast(P)).then_inc(s_w, 16)
            sp.dma_start(rel_bc[:], rel_emb.partition_broadcast(P)).then_inc(s_w, 16)
            sp.dma_start(stage.rearrange("p (e h) -> p e h", e=EXPERTS),
                         W1.rearrange("e d h -> d e h")).then_inc(s_stage, 16)
            sp.wait_ge(s_lo, 1)
            sp.dma_start(stage.rearrange("p (e t d) -> p e t d", e=EXPERTS, t=HT),
                         W2.rearrange("e (t p) d -> p e t d", p=P)).then_inc(s_stage, 16)
            if "at" in phases:
                sp_attention(sp)
            last = F[2] if "f2" in phases else None
            for c in range(CHUNKS):
                if last:
                    sp.wait_ge(last["x_done"], c + 1)
                else:
                    sp.wait_ge(s_in_done, 1)
                b, r = c // 2, c % 2
                sp.dma_start(out[b, CHUNK * r:CHUNK * (r + 1), :].rearrange("(t p) d -> p t d", p=P),
                             X[:, TPC * c:TPC * (c + 1), :]).then_inc(s_out, 16)
            sp.wait_ge(s_out, 16 * CHUNKS)

        N_W = 16 * 11

        def dve_ffn(dve, f, n):
            dve_stats(dve, f["stats"], f["sd"])
            dve_normalise(dve, f["xn_ready"], f["tr_full"])
            dve.wait_ge(f["lg_ready"], CHUNKS)
            bc = [P, TILES, EXPERTS]
            link(dve, dve.tensor_tensor(logits, logits, b_gate_bc[:].unsqueeze(1).to_broadcast(bc), ALU.add))
            ordb = order[:].unsqueeze(1).to_broadcast(bc)
            src = logits
            for oh, top in ((oh1, top1), (oh2, top2)):
                link(dve, dve.tensor_reduce(top, src, AXX, ALU.max))
                link(dve, dve.tensor_tensor(oh, src, top.unsqueeze(2).to_broadcast(bc), ALU.is_ge))
                link(dve, dve.tensor_tensor(oh, oh, ordb, ALU.mult))
                link(dve, dve.tensor_reduce(rt1, oh, AXX, ALU.max))
                link(dve, dve.tensor_tensor(oh, ordb, rt1.unsqueeze(2).to_broadcast(bc), ALU.is_equal))
                if oh is oh1:
                    link(dve, dve.scalar_tensor_tensor(out=rtmp, in0=oh, scalar=LOWEST, in1=logits,
                                                       op0=ALU.mult, op1=ALU.add))
                    src = rtmp
            dve.tensor_tensor(rt1, top2, top1, ALU.subtract).then_inc(f["rt_d"], 1)
            dve.wait_ge(f["rt_e"], 1)
            link(dve, dve.tensor_scalar(top1, rt2, 1.0, None, ALU.add))
            link(dve, dve.reciprocal(top2, top1))
            link(dve, dve.tensor_tensor(rt2, rt2, top2, ALU.mult))
            link(dve, dve.tensor_tensor(oh1, oh1, top2.unsqueeze(2).to_broadcast(bc), ALU.mult))
            link(dve, dve.tensor_tensor(oh2, oh2, rt2.unsqueeze(2).to_broadcast(bc), ALU.mult))
            link(dve, dve.tensor_tensor(route, oh1, oh2, ALU.add))

            dve.sem_inc(f["fa_full"], 1)
            dve.sem_inc(f["acc_chain"], 2)
            with dve.Fori(0, CHUNKS) as c:
                tiles = bass.ds(c * TPC, TPC)
                dve.wait_ge(f["fa_full"], c + 1)
                dve.tensor_copy(route_c, route[:, tiles, :]).then_inc(f["rc_ready"], 1)
                dve.wait_ge(f["rc_ready"], c + 1)
                for e in range(EXPERTS + 1):
                    if e < EXPERTS:
                        s = e % 2
                        dve.wait_ge(f["dn_full"], c * EXPERTS + (e + 1))
                        for ht in range(HT):
                            dve.wait_ge(f["mid32_ready"], c * 32 + (HT * e + ht + 1 + HT))
                            if ht % 2:
                                dve.tensor_copy(mid_hi[:, s, ht, :], mid32[:, ht, :]).then_inc(f["hi_dve"], 1)
                                dve.wait_ge(f["hi_dve"], c * 16 + (2 * e + ht // 2 + 1))
                            else:
                                dve.wait_ge(f["hi_act"], c * 16 + (2 * e + ht // 2 + 1))
                            dve.tensor_tensor(mid_lo[:, s, ht, :], mid32[:, ht, :], mid_hi[:, s, ht, :],
                                              ALU.subtract).then_inc(f["lo_done"], 1)
                    if e > 0:
                        dve.wait_ge(f["dn_full"], c * EXPERTS + (e + 2))
                        if e > 1:
                            dve.wait_ge(f["acc_chain"], c * EXPERTS + (e + 1))
                        y = bank[4 + (e - 1) % 2].rearrange("p (t d) -> p t d", t=TPC)
                        for k in range(TPC):
                            if e == 1:
                                ins = dve.tensor_scalar(acc[:, k, :], y[:, k, :], route_c[:, k, e - 1:e], None,
                                                        ALU.mult)
                            else:
                                ins = dve.scalar_tensor_tensor(out=acc[:, k, :], in0=y[:, k, :],
                                                               scalar=route_c[:, k, e - 1:e], in1=acc[:, k, :],
                                                               op0=ALU.mult, op1=ALU.add)
                        ins.then_inc(f["acc_chain"], 1)
                Xc = X[:, tiles, :]
                dve.tensor_tensor(Xc, Xc, half_b_out[:].unsqueeze(1).to_broadcast([P, TPC, P]),
                                  ALU.add).then_inc(f["fa_chain"], 1)
                dve.wait_ge(f["fa_chain"], c + 1)
                dve.wait_ge(f["fb_full"], c + 1)
                dve.scalar_tensor_tensor(out=Xc, in0=bank[7].rearrange("p (t d) -> p t d", t=TPC),
                                         scalar=0.5, in1=Xc, op0=ALU.mult, op1=ALU.add).then_inc(f["x_done"], 1)
            dve.wait_ge(f["x_done"], CHUNKS)

        def act_ffn(act, f, n):
            act.wait_ge(f["stats"], 1)
            act.activation(tmp0[:], var[:], ACT.Sqrt).then_inc(f["sd"], 1)
            with act.Fori(0, CHUNKS // 2) as c2:
                for u in range(2):
                    c1 = c2 * 2 + (u + 1)
                    act.wait_ge(f["tr_full"], c1 + 2)
                    act.wait_ge(f["h_full"], c1)
                    act.activation(xnT[:, u, :], bank[u], ACT.Identity).then_inc(f["xnT_ready"], 1)
                    act.wait_ge(f["h_full"], c1 + 2)
                    act.wait_ge(f["lo_ready"], c1)
                    act.activation(h32[:, u, :], bank[2 + u], ACT.Identity,
                                   bias=b_in_col[:]).then_inc(f["h32_ready"], 1)
                    act.wait_ge(f["h32_ready"], c1)
                    act.activation(t_hi[:, bass.ds(c2 * (2 * CHUNK) + u * CHUNK, CHUNK)], h32[:, u, :],
                                   ACT.Identity).then_inc(f["hi_ready"], 1)
                    act.wait_ge(f["lg_full"], c1)
                    act.activation(logits[:, bass.ds(c2 * (2 * TPC) + u * TPC, TPC), :],
                                   bank[4 + u][:, 0:TPC * EXPERTS].rearrange("p (t e) -> p t e", t=TPC),
                                   ACT.Identity).then_inc(f["lg_ready"], 1)
            act.wait_ge(f["rt_d"], 1)
            act.activation(rt2, rt1, ACT.Exp).then_inc(f["rt_e"], 1)
            act.sem_inc(f["mid32_ready"], HT)
            with act.Fori(0, CHUNKS) as c:
                act.wait_ge(f["rT_full"], c + 1)
                act.activation(routeT, bank[7][0:EXPERTS, :], ACT.Identity).then_inc(f["rT_ready"], 1)
                for e in range(EXPERTS):
                    s = e % 2
                    act.wait_ge(f["dn_full"], c * EXPERTS + (e + 1))
                    for ht in range(HT):
                        i = HT * e + ht
                        act.wait_ge(f["up_full"], c * 32 + (i + 1))
                        act.wait_ge(f["lo_done"], c * 32 + (i + 1))
                        act.activation(mid32[:, ht, :], bank[ht], ACT.Relu,
                                       bias=b1_cols[:, i:i + 1]).then_inc(f["mid32_ready"], 1)
                        if ht % 2:
                            act.wait_ge(f["mid32_ready"], c * 32 + (i + HT))
                            act.activation(mid_hi[:, s, ht - 1, :], mid32[:, ht - 1, :],
                                           ACT.Identity).then_inc(f["hi_act"], 1)
                act.wait_ge(f["fa_full"], c + 2)
                act.activation(moT, bank[6], ACT.Identity).then_inc(f["fa_ready"], 1)

        def pe_transpose_chunk(pe, u, xn_ready, tr_full, c1):
            pe.wait_ge(xn_ready, c1)
            for k in range(TPC):
                ins = pe.matmul(bank[u][:, P * k:P * (k + 1)], xn[:, u, k, :], ident, start=(k == 0), stop=True,
                                is_transpose=True, skip_group_check=True)
            ins.then_inc(tr_full, 1)

        def pe_ffn(pe, f, n):
            pe.sem_inc(f["h_full"], 2)
            pe.sem_inc(f["tr_full"], 2)
            with pe.Fori(0, CHUNKS // 2) as c2:
                for u in range(2):
                    c1 = c2 * 2 + (u + 1)
                    pe_transpose_chunk(pe, u, f["xn_ready"], f["tr_full"], c1)
                    pe.wait_ge(f["xnT_ready"], c1)
                    pe.matmul(bank[2 + u], w_in[:], xnT[:, u, :], start=True, stop=True).then_inc(f["h_full"], 1)
                    pe.wait_ge(f["h32_ready"], c1)
                    for k in range(TPC):
                        ins = pe.matmul(bank[4 + u][:, EXPERTS * k:EXPERTS * (k + 1)], h32[:, u, P * k:P * (k + 1)],
                                        w_gate[:], start=(k == 0), stop=True, skip_group_check=True)
                    ins.then_inc(f["lg_full"], 1)
            if n == 1:
                pe.wait_ge(s_lo, 2)
                pe.wait_ge(s_hi, 2)
            pe.wait_ge(s_b1, 1)
            pe.wait_ge(f["lo_ready"], CHUNKS + 2)
            pe.wait_ge(f["hi_ready"], CHUNKS)
            pe.wait_ge(f["lg_ready"], CHUNKS)
            pe.sem_inc(f["lo_done"], HT)
            pe.sem_inc(f["dn_full"], 2)
            with pe.Fori(0, CHUNKS) as c:
                cols = bass.ds(c * CHUNK, CHUNK)
                pe.wait_ge(f["rc_ready"], c + 1)
                for k in range(TPC):
                    ins = pe.matmul(bank[7][0:EXPERTS, P * k:P * (k + 1)], route_c[:, k, :], ident,
                                    start=(k == 0), stop=True, is_transpose=True, skip_group_check=True)
                ins.then_inc(f["rT_full"], 1)
                for e in range(EXPERTS + 1):
                    if e < EXPERTS:
                        for ht in range(HT):
                            i = HT * e + ht
                            pe.wait_ge(f["mid32_ready"], c * 32 + (i + 1))
                            w_h, w_l = w1_hi[:, e, P * ht:P * (ht + 1)], w1_lo[:, e, P * ht:P * (ht + 1)]
                            pe.matmul(bank[ht], w_h, t_hi[:, cols], start=True, stop=False)
                            pe.matmul(bank[ht], w_h, t_lo[:, cols], start=False, stop=False)
                            pe.matmul(bank[ht], w_l, t_hi[:, cols], start=False,
                                      stop=True).then_inc(f["up_full"], 1)
                    if e > 0:
                        d, s = e - 1, (e - 1) % 2
                        pe.wait_ge(f["hi_act"], c * 16 + (2 * d + 2))
                        pe.wait_ge(f["lo_done"], c * 32 + (HT * d + 2 * HT))
                        pe.wait_ge(f["acc_chain"], c * EXPERTS + (d + 1))
                        for k in range(TPC):
                            tok = slice(P * k, P * (k + 1))
                            for ht in range(HT):
                                m_h, m_l = mid_hi[:, s, ht, tok], mid_lo[:, s, ht, tok]
                                o = bank[4 + s][:, tok]
                                pe.matmul(o, m_h, w2_hi[:, d, ht, :], start=(k == 0 and ht == 0), stop=False,
                                          skip_group_check=True)
                                pe.matmul(o, m_h, w2_lo[:, d, ht, :], start=False, stop=False,
                                          skip_group_check=True)
                                ins = pe.matmul(o, m_l, w2_hi[:, d, ht, :], start=False, stop=(ht == HT - 1),
                                                skip_group_check=True)
                        ins.then_inc(f["dn_full"], 1)
                pe.wait_ge(f["rT_ready"], c + 1)
                pe.matmul(bank[6], b2_rows[:], routeT, start=True, stop=False, skip_group_check=True)
                pe.wait_ge(f["acc_chain"], c * EXPERTS + (EXPERTS + 2))
                for k in range(TPC):
                    ins = pe.matmul(bank[6][:, P * k:P * (k + 1)], acc[:, k, :], ident, start=False, stop=True,
                                    skip_group_check=True)
                ins.then_inc(f["fa_full"], 1)
                pe.wait_ge(f["fa_ready"], c + 1)
                for k in range(TPC):
                    ins = pe.matmul(bank[7][:, P * k:P * (k + 1)], moT[:, P * k:P * (k + 1)], w_out[:],
                                    start=(k == 0), stop=True, skip_group_check=True)
                ins.then_inc(f["fb_full"], 1)
                pe.wait_ge(f["x_done"], c + 1)

        def pool_ffn(pool, f):
            pool.sem_inc(f["lo_ready"], 2)
            with pool.Fori(0, CHUNKS // 2) as c2:
                for u in range(2):
                    pool.wait_ge(f["hi_ready"], c2 * 2 + (u + 1))
                    cols = bass.ds(c2 * (2 * CHUNK) + u * CHUNK, CHUNK)
                    pool.tensor_tensor(t_lo[:, cols], h32[:, u, :], t_hi[:, cols],
                                       ALU.subtract).then_inc(f["lo_ready"], 1)

        @block.gpsimd
        def _(pool):
            for e in range(EXPERTS):
                ins = pool.memset(order[:, e:e + 1], float(EXPERTS - e))
            ins.then_inc(s_cst, 1)
            if "f1" in phases:
                pool_ffn(pool, F[1])
            if "at" in phases:
                pool_attention(pool)
            if "f2" in phases:
                pool_ffn(pool, F[2])

        @block.vector
        def _(dve):
            dve.wait_ge(s_w, N_W)
            dve.tensor_copy(ident_bf[:], ident)
            dve.tensor_copy(neg_bf[:], C[:, C_NEG:C_NEG + P])
            link(dve, dve.tensor_scalar(half_b_out[:], half_b_out[:], 0.5, None, ALU.mult))
            dve.wait_ge(s_b1T, 1)
            dve.tensor_copy(b1_cols[:], bank[6][:, 0:EXPERTS * HT]).then_inc(s_b1, 1)
            dve.wait_ge(s_hi, 1)
            dve.tensor_tensor(w1_lo[:].rearrange("p e h -> p (e h)"), stage, w1_hi[:].rearrange("p e h -> p (e h)"),
                              ALU.subtract).then_inc(s_lo, 1)
            dve.wait_ge(s_hi, 2)
            dve.tensor_tensor(w2_lo[:].rearrange("p e t d -> p (e t d)"), stage,
                              w2_hi[:].rearrange("p e t d -> p (e t d)"), ALU.subtract).then_inc(s_lo, 1)
            dve.wait_ge(s_x, 16 * BATCH)
            dve.wait_ge(s_cst, 1)
            if "f1" in phases:
                dve_ffn(dve, F[1], 1)
            if "at" in phases:
                dve_attention(dve)
            if "f2" in phases:
                dve_ffn(dve, F[2], 2)
            dve.sem_inc(s_in_done, 1)

        @block.scalar
        def _(act):
            act.wait_ge(s_stage, 16)
            act.activation(w1_hi[:].rearrange("p e h -> p (e h)"), stage, ACT.Identity).then_inc(s_hi, 1)
            act.wait_ge(s_stage, 32)
            act.activation(w2_hi[:].rearrange("p e t d -> p (e t d)"), stage, ACT.Identity).then_inc(s_hi, 1)
            act.wait_ge(s_w, N_W)
            if "f1" in phases:
                act_ffn(act, F[1], 1)
            if "at" in phases:
                act_attention(act)
            if "f2" in phases:
                act_ffn(act, F[2], 2)

        @block.tensor
        def _(pe):
            pe.wait_ge(s_w, N_W)
            pe.transpose(bank[6][:, 0:EXPERTS * HT], b1_rows[:], C[0:EXPERTS * HT, C_ID:C_ID + EXPERTS * HT]).then_inc(s_b1T, 1)
            if "f1" in phases:
                pe_ffn(pe, F[1], 1)
            if "at" in phases:
                pe_attention(pe)
            if "f2" in phases:
                pe_ffn(pe, F[2], 2)


_INS = ["L0_attn_x", "L0_attn_Wq", "L0_attn_Wk", "L0_attn_Wv", "L0_attn_Wo", "L0_attn_bo", "L0_attn_rel_emb",
        "L0_ffn_W_in", "L0_ffn_b_in", "L0_ffn_W_gate", "L0_ffn_b_gate", "L0_ffn_W1", "L0_ffn_b1", "L0_ffn_W2",
        "L0_ffn_b2", "L0_ffn_W_out", "L0_ffn_b_out"]


def kernel(**inputs):
    import numpy as _np
    import concourse.bacc as _bacc
    from concourse import mybir as _mybir
    from concourse.bass_utils import run_bass_kernel_spmd as _run

    nc = _bacc.Bacc("TRN2", target_bir_lowering=False, num_devices=1)
    arrays, args = {}, []
    for name in _INS:
        a = _np.ascontiguousarray(inputs[name])
        arrays[f"in_{name}"] = a
        args.append(nc.dram_tensor(f"in_{name}", a.shape, _mybir.dt.from_np(a.dtype), kind="ExternalInput").ap())
    c = consts()
    arrays["consts"] = c
    args.append(nc.dram_tensor("consts", c.shape, _mybir.dt.float32, kind="ExternalInput").ap())
    args.append(nc.dram_tensor("out_0", (BATCH, SEQ, P), _mybir.dt.float32, kind="ExternalOutput").ap())
    build(nc, *args)
    r = _run(nc, [arrays], core_ids=[0])
    return r.results[0]["out_0"]
```

```python
from contextlib import ExitStack

import concourse.bass as bass
from concourse import mybir

F32 = mybir.dt.float32
BF16 = mybir.dt.bfloat16
ALU = mybir.AluOpType
ACT = mybir.ActivationFunctionType
AXX = mybir.AxisListType.X

P = 128
BATCH = 4
SEQ = 1024
TOKENS = BATCH * SEQ
TILES = TOKENS // P
CHUNK = 512
CHUNKS = TOKENS // CHUNK
TPC = CHUNK // P
EXPERTS = 8
HID = 512
HT = HID // P
HEADS = 16
HD = 8
CLIP = 16
GROUPS = HEADS // 4
QT = SEQ // P
BAND = P + CLIP
LN_EPS = 1e-5
MASKED = -1e30
LOWEST = -3e38
SCALE = float(HD) ** -0.5
C_ID, C_SHIFT, C_NEG, C_SEL, C_QLO, C_KLO, C_ONE = 0, 128, 448, 576, 704, 705, 706
C_ALL = 707


def consts():
    import numpy as np
    c = np.zeros((P, C_ALL), np.float32)
    p = np.arange(P)
    c[p, C_ID + p] = 1.0
    c[p, C_SHIFT + 160 + p] = 1.0
    c[:, C_NEG:C_NEG + P] = np.where(np.arange(P)[None, :] > p[:, None], MASKED, 0.0)
    c[32 * (p // 32) + HD, C_SEL + p] = 1.0
    r = p % 32
    c[:, C_QLO] = (r >= 8) & (r < 16)
    c[:, C_KLO] = (r >= 16) & (r < 24)
    c[:, C_ONE] = np.where((r == 24) | (r == 25), -1.0, 0.0)
    return c


def build(nc, x, Wq, Wk, Wv, Wo, bo, rel_emb, W_in, b_in, W_gate, b_gate, W1, b1, W2, b2,
          W_out, b_out, cst, out, phases=("f1", "at", "f2")):
    ctx = ExitStack()
    with ctx:
        def sb(name, shape, dt=F32):
            return ctx.enter_context(nc.sbuf_tensor(name, shape, dt))

        def sem(name):
            return ctx.enter_context(nc.semaphore(name))

        PS = ctx.enter_context(nc.psum_tensor("PS", [P, 8, CHUNK], F32))
        bank = [PS[:, i, :] for i in range(8)]

        X = sb("X", [P, TILES, P])
        C = sb("C", [P, C_ALL])
        ident = C[:, C_ID:C_ID + P]
        ident_bf = sb("ident_bf", [P, P], BF16)
        neg_bf = sb("neg_bf", [P, P], BF16)
        W_PART = EXPERTS * HID
        weights = sb("weights", [P, 4, W_PART], BF16)
        w1_hi, w1_lo = (weights[:, k, :].rearrange("p (e h) -> p e h", e=EXPERTS) for k in (0, 1))
        w2_hi, w2_lo = (weights[:, k, :].rearrange("p (e t d) -> p e t d", e=EXPERTS, t=HT) for k in (2, 3))
        w_in, w_out = sb("w_in", [P, P]), sb("w_out", [P, P])
        w_gate = sb("w_gate", [P, EXPERTS])
        b_in_col = sb("b_in_col", [P, 1])
        b_gate_bc = sb("b_gate_bc", [P, EXPERTS])
        b1_rows = sb("b1_rows", [EXPERTS * HT, P])
        b1_cols = sb("b1_cols", [P, EXPERTS * HT])
        b2_rows = sb("b2_rows", [EXPERTS, P])
        half_b_out = sb("half_b_out", [P, P])
        bo_bc = sb("bo_bc", [P, P])
        rel_bc = sb("rel_bc", [P, CLIP + 1])
        t_hi, t_lo = sb("t_hi", [P, TOKENS], BF16), sb("t_lo", [P, TOKENS], BF16)
        order = sb("order", [P, EXPERTS])
        bn = sb("bn", [P, TILES, 6])
        mean, var, rstd, tmp0, tmp1 = (sb(n, [P, TILES]) for n in ("mean", "var", "rstd", "tmp0", "tmp1"))
        xn = sb("xn", [P, 2, TPC, P])
        big = sb("big", [P, 33000])

        def carve():
            at = [0]

            def take(shape, dt=F32, parts=P):
                n = 1
                for s in shape:
                    n *= s
                words = n if dt == F32 else (n + 1) // 2
                v = big[0:parts, at[0]:at[0] + words]
                at[0] += words
                assert at[0] <= 33000, at[0]
                if dt != F32:
                    v = v.bitcast(dt)
                names = " ".join(f"a{i}" for i in range(len(shape)))
                if len(shape) > 1:
                    v = v.rearrange(f"p ({names}) -> p {names}", **{f"a{i}": s for i, s in enumerate(shape)})
                return v
            return take, at

        T_AT = 12577

        take, used = carve()
        xnT, h32 = take([2, CHUNK]), take([2, CHUNK])
        mid32 = take([HT, CHUNK])
        mid_hi, mid_lo = take([2, HT, CHUNK], BF16), take([2, HT, CHUNK], BF16)
        acc = take([TPC, P])
        moT = take([CHUNK])
        routeT = take([CHUNK], parts=EXPERTS)
        route_c = take([TPC, EXPERTS])
        logits, oh1, oh2, rtmp, route = (take([TILES, EXPERTS]) for _ in range(5))
        top1, top2, rt1, rt2 = (take([TILES]) for _ in range(4))
        take([T_AT - used[0]])
        stage = take([2, W_PART])

        take, used = carve()
        wq_hi, wq_lo, wk_hi, wk_lo = (take([GROUPS, P], BF16) for _ in range(4))
        wv_hi, wv_lo = take([P], BF16), take([P], BF16)
        wo_rep = take([GROUPS, P])
        A = take([BAND])
        D = take([CLIP])
        sq_far = take([1])
        pr_far, pr_band = take([2, CHUNK]), take([2, CHUNK])
        sum_rows = C[:, C_ID:C_ID + P].rearrange("p (j r) -> p j r", r=32)[:, :, HD]
        part_far, part_band = take([2, CHUNK], BF16), take([2, CHUNK], BF16)
        QF, QB = take([GROUPS, SEQ], BF16), take([2, SEQ], BF16)
        Kfull = take([2, CHUNK], BF16)
        KM = weights[:].rearrange("p k n -> p (k n)").rearrange("p (g j s) -> p g j s", g=GROUPS, j=4)
        TD = take([QT, 4, P])
        take([T_AT - used[0]])
        T = take([QT, 4, BAND])
        E = take([2, QT, 4, 32], parts=CLIP)
        mxp = take([QT, 4, 3])
        nmax, nmr = take([QT, 4]), take([QT, 4])
        M4 = take([QT, P], BF16)
        PT = take([2, 4, CHUNK])
        vaug = take([QT, HEADS, 32])
        cs = take([CHUNK])
        rexp = take([CHUNK])
        rec = take([4 * TPC])
        ctxn = xn[:].rearrange("p s k d -> p s (k d)")
        ptw = PT.rearrange("p a b c -> p (a b c)")
        xT32 = ptw[:, 0:2 * CHUNK].rearrange("p (s c) -> p s c", s=2)
        wqkv = ptw[:, 1024:1024 + 3 * P].rearrange("p (w n) -> p w n", w=3)
        wq_rep = ptw[:, 1536:2048].rearrange("p (h r) -> p h r", h=HEADS)
        wk_rep = ptw[:, 2048:2560].rearrange("p (h r) -> p h r", h=HEADS)

        s_x = sem("x_loaded")
        s_w = sem("weights_loaded")
        s_stage = sem("expert_weights_staged")
        s_stage2 = sem("expert_w2_staged")
        s_hi = sem("expert_hi_ready")
        s_lo = sem("expert_lo_ready")
        s_vc = sem("vector_chain")
        s_cst = sem("constants_ready")
        s_b1T = sem("b1_transposed")
        s_b1 = sem("b1_cols_ready")
        s_out = sem("stored")
        s_in_done = sem("phase_done")

        block = ctx.enter_context(nc.Block())

        chain = [0]

        def link(dve, ins):
            chain[0] += 1
            ins.then_inc(s_vc, 1)
            dve.wait_ge(s_vc, chain[0])

        def ffn_semaphores(n):
            return {s: sem(f"ffn{n}_{s}") for s in (
                "stats", "sd", "xn_ready", "tr_full", "xnT_ready", "h_full", "h32_ready", "lg_full", "lg_ready",
                "hi_ready", "lo_ready", "rt_d", "rt_e", "route_ready", "up_full", "mid32_ready", "hi_act", "hi_dve",
                "lo_done", "dn_full", "acc_chain", "rc_ready", "rT_full", "rT_ready", "fa_full", "fa_ready",
                "fb_full", "x_done", "fa_chain")}

        F = {1: ffn_semaphores(1), 2: ffn_semaphores(2)}

        def dve_stats(dve, stats_sem, sd_sem):
            for t in range(TILES):
                ins = dve.bn_stats(bn[:, t, :], X[:, t, :])
            link(dve, ins)
            m_e, v_e, m_o, v_o = bn[:, :, 1], bn[:, :, 2], bn[:, :, 4], bn[:, :, 5]
            dve.tensor_tensor(mean[:], m_e, m_o, ALU.add)
            dve.tensor_tensor(tmp0[:], m_e, m_o, ALU.subtract)
            link(dve, dve.tensor_tensor(var[:], v_e, v_o, ALU.add))
            dve.tensor_scalar(mean[:], mean[:], 0.5, None, ALU.mult)
            dve.tensor_tensor(tmp1[:], tmp0[:], tmp0[:], ALU.mult)
            link(dve, dve.tensor_scalar(var[:], var[:], 1.0 / P, LN_EPS, ALU.mult, ALU.add))
            link(dve, dve.scalar_tensor_tensor(out=var[:], in0=tmp1[:], scalar=0.25, in1=var[:],
                                               op0=ALU.mult, op1=ALU.add))
            dve.sem_inc(stats_sem, 1)
            dve.wait_ge(sd_sem, 1)
            link(dve, dve.reciprocal(rstd[:], tmp0[:]))
            link(dve, dve.tensor_tensor(tmp1[:], rstd[:], rstd[:], ALU.mult))
            link(dve, dve.tensor_tensor(tmp1[:], tmp1[:], var[:], ALU.mult))
            link(dve, dve.tensor_scalar(tmp1[:], tmp1[:], -0.5, 1.5, ALU.mult, ALU.add))
            link(dve, dve.tensor_tensor(rstd[:], rstd[:], tmp1[:], ALU.mult))

        def dve_normalise(dve, xn_ready, tr_full):
            with dve.Fori(0, CHUNKS // 2) as c2:
                for u in range(2):
                    dve.wait_ge(tr_full, c2 * 2 + (u + 1))
                    for k in range(TPC):
                        t = bass.ds(c2 * (2 * TPC) + (u * TPC + k), 1)
                        ins = dve.tensor_scalar(xn[:, u, k, :], X[:, t, :].rearrange("p a d -> p (a d)"), mean[:, t], rstd[:, t],
                                                ALU.subtract, ALU.mult)
                    ins.then_inc(xn_ready, 1)

        def b_steps(i):
            far = max(P * i - CLIP, 0)
            if far + BAND <= CHUNK:
                return [(0, far, True)]
            cut = min(far, CHUNK)
            return [(0, cut, False), (cut, far, True)]

        FILL_ORDER = [(6, 0), (7, 0), (5, 0), (0, 0), (4, 0), (1, 0), (2, 0), (3, 0), (4, 1), (5, 1), (6, 1), (7, 1)]
        FILLS = [(i, u, n) for i, n in FILL_ORDER for u in range(2)]
        FILL_HEADS = [f_ + (h,) for f_ in FILLS for h in range(2)]
        B_PER = len(FILL_ORDER)

        def fill_at(i, n):
            return FILL_ORDER.index((i, n))

        C_UNITS = [(c, k) for c in range(SEQ // CHUNK) for k in range(TPC * (c + 1))]
        CU = len(C_UNITS)

        ENDS = ("N", "ND", "R", "N2", "N2D", "O", "OD")
        AT = {"CS": (4, 2), ("N", -1): (0, 0), ("ND", -1): (0, 3), ("R", -1): (1, 1),
              ("N2", -1): (1, 3), ("N2D", -1): (2, 0), ("O", -1): (2, 3), ("OD", -1): (3, 0),
              ("N", 0): (5, 2), ("ND", 0): (5, 3), ("R", 0): (6, 1), ("N2", 0): (6, 3),
              ("N2D", 0): (7, 1), ("O", 0): (7, 3), ("OD", 0): (8, 1), ("A", 0): (3, 2),
              ("A", 1): (4, 1), ("A", 2): (8, 3), ("A", 3): (9, 3), ("AD", 2): (9, 3),
              ("AD", 3): (11, 3)}
        FILLS_AT = ((0, 0, 1, 2), (0, 1, 2, 3), (0, 1, 2), (0, 1, 2, 3), (0, 1, 2), (0, 1, 2, 3),
                    (1, 2), (0, 1, 2, 3), (0, 1, 2), (0, 1, 2, 3), (0, 1, 2), (0, 1, 1, 3))
        FILLS_BEFORE, FILLS_START, FILLS_LAST, FILLS_END = 4, 0, 2, 4

        def c_events(lead2, nxt=None):
            ev = []
            for n in range(CU):
                for j in range(4):
                    ev.append(("S", n, j))
                    ev += ["b"] * FILLS_AT[n].count(j)
                    if n and j == 1:
                        ev.append(("PV", n - 1))
                    if (n, j) == AT["CS"]:
                        ev.append(("CS", 0))
                    for c in (-1, 0):
                        if c == 0 or lead2:
                            ev += [(e, c) for e in ENDS if AT[e, c] == (n, j)]
                    if nxt is not None:
                        ev += [("A", nxt, p) for p in range(4) if AT["A", p] == (n, j)]
                        ev += [("AD", nxt, p) for p in (2, 3) if AT["AD", p] == (n, j)]
            return ev

        def slot_plan(g, lead, lead2):
            nxt = g + 1
            pieces = [("A", nxt, p) for p in range(4)]
            ev = []
            if lead:
                v = [("V", 0), ("V", 1)] if g == 0 else []
                ev += [("M",)] + ["bp"] * FILLS_BEFORE + [("MP",), ("M2",)] + ["bd"] + ["b"] * FILLS_START + c_events(lead2, nxt) \
                    + ["b"] * FILLS_LAST + [("PV", CU - 1), ("CS", 1)] + v + ["b"] * FILLS_END
            else:
                for k in range(len(FILL_HEADS)):
                    ev.append("b")
                    ev += {8: [("V", 0)], 12: [("V", 1)], 18: pieces[:1], 22: pieces[1:2], 28: pieces[2:3],
                           34: pieces[3:], 40: [("AD", nxt, 2)], 44: [("AD", nxt, 3)]}.get(k, [])
            fills, out_, held = list(FILL_HEADS), [], []
            for e in ev:
                if e == "bp":
                    f_ = fills.pop(0)
                    out_.append(("B",) + f_)
                    held += [("BD",) + f_] if f_[3] else []
                elif e == "bd":
                    out_ += held
                elif e != "b":
                    out_.append(e)
                elif fills:
                    f_ = fills.pop(0)
                    out_.append(("B",) + f_)
                    out_ += [("BD",) + f_] if f_[3] else []
            for f_ in fills:
                out_.append(("B",) + f_)
                out_ += [("BD",) + f_] if f_[3] else []
            return out_

        TAIL = [("M",), ("MP",), ("M2",)] + [e for e in c_events(True) if e != "b"] \
            + [("PV", CU - 1), ("CS", 1)] + [(e, 1) for e in ENDS]

        def run_plan(eng, handler):
            for ev in [("A", 0, p) for p in range(4)] + [("AD", 0, 2), ("AD", 0, 3)]:
                handler(eng, ev, 0, 0, 0, 0, True, True)

            def batch(b, first):
                for g in range(GROUPS):
                    lead = not (first and g == 0)
                    pb, pg = (b, g - 1) if g else (b - 1, GROUPS - 1)
                    qb, qg = (b, g - 2) if g >= 2 else (b - 1, g + GROUPS - 2)
                    for ev in slot_plan(g, lead, lead and not (first and g == 1)):
                        if ev[-1] == -1:
                            handler(eng, (ev[0], 1), b, g, qb, qg, False, False)
                        else:
                            handler(eng, ev, b, g, pb, pg, first and g == 0, first and g <= 1)
            batch(0, True)
            with eng.Fori(1, BATCH) as b:
                batch(b, False)
            for ev in TAIL:
                if ev[-1] == -1:
                    handler(eng, (ev[0], 1), BATCH, 0, BATCH - 1, GROUPS - 2, False, False)
                else:
                    handler(eng, ev, BATCH, 0, BATCH - 1, GROUPS - 1, False, False)

        def attention_handlers():
            a = {s_: sem("attn_" + s_) for s_ in (
                "stats", "sd", "xn_ready", "tr_full", "xT_ready", "hi_ready", "lo_ready", "w_loaded", "w_rep", "w_hi",
                "w_lo", "zeroed", "band_chain", "band_ready", "bo_added", "pr_full", "pr_ready", "split_done",
                "part_ready", "k_ready", "v_full", "v_ready", "t_ready", "mx_done", "m_chain", "m4_ready",
                "nm_ready", "mt_full", "mt_done", "td_ready", "s_full", "exp_done", "pv_done", "cs_ready", "den_full",
                "rec_ready", "rexp_ready", "rb_full", "ctxn_ready", "o_full", "x_added", "pool_steps")}
            a["b_full"] = [sem(f"attn_b_full{u}") for u in range(2)]
            a["b_free"] = [sem(f"attn_b_free{u}") for u in range(2)]

            def at_group(pb, pg, per, k):
                return pb * (GROUPS * per) + (pg * per + k)

            def pe_h(pe, ev, b, g, pb, pg, fresh, young):
                kind = ev[0]
                par, ppar = g % 2, pg % 2
                if kind == "A":
                    ag, p = ev[1], ev[2]
                    w_h, w_l = (wq_hi, wq_lo) if p < 2 else (wk_hi, wk_lo)
                    start = (b * SEQ + SEQ) % TOKENS if ag == GROUPS else b * SEQ
                    cols = bass.ds(start + CHUNK * (p % 2), CHUNK)
                    misc_wait(pe)
                    pe.matmul(bank[7], w_h[:, ag % GROUPS, :], t_hi[:, cols], start=True, stop=False)
                    pe.matmul(bank[7], w_h[:, ag % GROUPS, :], t_lo[:, cols], start=False, stop=False)
                    pe.matmul(bank[7], w_l[:, ag % GROUPS, :], t_hi[:, cols], start=False, stop=True).then_inc(a["pr_full"], 1)
                    misc_used(a["pr_ready"], at_group(b, ag, 4, p + 1))
                elif kind == "V":
                    r = ev[1]
                    misc_wait(pe)
                    for k in range(TPC):
                        tok = bass.ds(b * SEQ + P * (TPC * r + k), P)
                        o = bank[7][:, P * k:P * (k + 1)]
                        pe.matmul(o, t_hi[:, tok], wv_hi, start=(k == 0), stop=False, skip_group_check=True)
                        pe.matmul(o, t_hi[:, tok], wv_lo, start=False, stop=False, skip_group_check=True)
                        ins = pe.matmul(o, t_lo[:, tok], wv_hi, start=False, stop=True, skip_group_check=True)
                    ins.then_inc(a["v_full"], 1)
                    misc_used(a["v_ready"], b * 2 + (r + 1))
                elif kind == "B":
                    i, u, n, h = ev[1:]
                    if (i, u, n, h) == FILL_HEADS[0]:
                        pe.wait_ge(a["k_ready"], at_group(b, g, 2, 2))
                        pe.wait_ge(a["split_done"], at_group(b, g, 4, 2))
                    k0, k1, band = b_steps(i)[n]
                    cnt = fill_at(i, n)
                    if h == 0 and not (fresh and cnt == 0):
                        pe.wait_ge(a["b_free"][u], at_group(b, g, B_PER, cnt))
                    far = k1 - k0
                    w = BAND if i else P
                    j = 2 * u + h
                    bk = bank[j]
                    qs = slice(P * i, P * (i + 1))
                    if band:
                        pe.matmul(bk[:, far + w - P:far + w], ident_bf[:], neg_bf[:],
                                  start=True, stop=False, skip_group_check=True)
                    if far:
                        ins = pe.matmul(bk[:, 0:far], QF[:, g, qs], KM[:, g, j, k0:k1],
                                        start=not band, stop=True, skip_group_check=True)
                    if band:
                        ins = pe.matmul(bk[:, far:far + w], QB[:, par, qs], KM[:, g, j, k1:k1 + w],
                                        start=False, stop=True, skip_group_check=True)
                    if h:
                        ins.then_inc(a["b_full"][u], 1)
                elif kind == "MP":
                    pe.wait_ge(a["m4_ready"], at_group(pb, pg, 1, 1))
                    misc_wait(pe)
                    if not (young and pg == 0):
                        pe.wait_ge(a["cs_ready"], at_group(pb, pg, 2, 0))
                    for r in range(2):
                        for k in range(TPC):
                            ins = pe.matmul(bank[7 - r][:, P * k:P * (k + 1)], M4[:, TPC * r + k, :], ident_bf[:],
                                            start=(k == 0), stop=True, skip_group_check=True)
                        ins.then_inc(a["mt_full"], 1)
                    misc_used(a["mt_done"], at_group(pb, pg, 2, 1))
                elif kind == "S":
                    n, j = ev[1:]
                    c, kt = C_UNITS[n]
                    off = max(CHUNK * c, P * kt) - CHUNK * c
                    diag = P * kt >= CHUNK * c
                    if kt == 0 and j == 0:
                        pe.wait_ge(a["mt_done"], at_group(pb, pg, 2, c + 1))
                    if diag and j == 0:
                        pe.wait_ge(a["td_ready"], at_group(pb, pg, QT, kt + 1))
                    idx = 4 * n + j
                    bk = bank[4 + idx % 2]
                    if not (young and idx < 2 and pg == 0):
                        pe.wait_ge(a["exp_done"], at_group(pb, pg, 4 * CU, idx - 1))
                    far = off
                    if diag:
                        ins = pe.matmul(bk[:, off:off + P], TD[:, kt, j, :], ident, start=True, stop=True,
                                        is_transpose=True, skip_group_check=True)
                        far = off + P
                    if far < CHUNK:
                        ins = pe.matmul(bk[:, far:], KM[:, pg, j, P * kt:P * (kt + 1)],
                                        QF[:, pg, CHUNK * c + far:CHUNK * (c + 1)], start=not diag, stop=True,
                                        skip_group_check=True)
                    nq = P * (kt + 1) - CHUNK * c
                    if 0 <= nq < CHUNK:
                        ins = pe.matmul(bk[96:128, nq:nq + CLIP], E[:, ppar, kt + 1, j, :], ident[0:CLIP, 0:CLIP],
                                        start=False, stop=True, skip_group_check=True)
                    ins.then_inc(a["s_full"], 1)
                elif kind == "PV":
                    n = ev[1]
                    c, kt = C_UNITS[n]
                    off = max(CHUNK * c, P * kt) - CHUNK * c
                    pe.wait_ge(a["exp_done"], at_group(pb, pg, 4 * CU, 4 * n + 4))
                    if n == 0:
                        pe.wait_ge(a["v_ready"], pb * 2 + 2)
                        pe.wait_ge(a["mt_done"], at_group(pb, pg, 2, 2))
                    if kt == 0 and not (young and c == 0 and pg == 0):
                        pe.wait_ge(a["cs_ready"], at_group(pb, pg, 2, c))
                    last = kt == TPC * (c + 1) - 1
                    for j in range(4):
                        ins = pe.matmul(bank[6][32 * j:32 * (j + 1), off:], vaug[:, kt, 4 * pg + j, :],
                                        PT[:, n % 2, j, off:], start=(kt == 0), stop=last,
                                        skip_group_check=True)
                    ins.then_inc(a["pv_done"], 1)
                elif kind == "N":
                    c = ev[1]
                    pe.wait_ge(a["cs_ready"], at_group(pb, pg, 2, c + 1))
                    misc_wait(pe)
                    for k in range(TPC):
                        ins = pe.matmul(bank[7][:, 4 * k:4 * k + 4], cs[:, P * k:P * (k + 1)], sum_rows,
                                        start=(k == 0), stop=True, skip_group_check=True)
                    ins.then_inc(a["den_full"], 1)
                    misc_used(a["rec_ready"], at_group(pb, pg, 2, c + 1))
                elif kind == "N2":
                    c = ev[1]
                    pe.wait_ge(a["rexp_ready"], at_group(pb, pg, 2, c + 1))
                    misc_wait(pe)
                    for k in range(TPC):
                        ins = pe.matmul(bank[7][:, P * k:P * (k + 1)], rexp[:, P * k:P * (k + 1)], ident,
                                        start=(k == 0), stop=True, is_transpose=True, skip_group_check=True)
                    ins.then_inc(a["rb_full"], 1)
                    misc_used(a["ctxn_ready"], at_group(pb, pg, 2, c + 1))
                elif kind == "O":
                    c = ev[1]
                    pe.wait_ge(a["ctxn_ready"], at_group(pb, pg, 2, c + 1))
                    misc_wait(pe)
                    for k in range(TPC):
                        ins = pe.matmul(bank[7][:, P * k:P * (k + 1)], ctxn[:, c, P * k:P * (k + 1)], wo_rep[:, pg, :],
                                        start=(k == 0), stop=True, skip_group_check=True)
                    ins.then_inc(a["o_full"], 1)
                    misc_used(a["x_added"], at_group(pb, pg, 2, c + 1))

            misc = [None]

            def misc_wait(pe):
                if misc[0] is not None:
                    pe.wait_ge(*misc[0])

            def misc_used(sem_, value):
                misc[0] = (sem_, value)

            def act_h(act, ev, b, g, pb, pg, fresh, young):
                kind = ev[0]
                if kind == "A":
                    ag, p = ev[1], ev[2]
                    s = p % 2
                    act.wait_ge(a["pr_full"], at_group(b, ag, 4, p + 1))
                    if not (fresh and ag == 0 and p < 2):
                        act.wait_ge(a["split_done"], at_group(b, ag, 4, p - 1))
                    if p < 2:
                        act.activation(pr_band[:, s, :], bank[7], ACT.Identity, scale=SCALE)
                        act.activation(pr_far[:, s, :], bank[7], ACT.Identity, scale=sq_far).then_inc(a["pr_ready"], 1)
                    else:
                        act.activation(pr_far[:, s, :], bank[7], ACT.Identity).then_inc(a["pr_ready"], 1)
                elif kind == "V":
                    r = ev[1]
                    act.wait_ge(a["v_full"], b * 2 + (r + 1))
                    act.activation(vaug[:, TPC * r:TPC * (r + 1), :, 0:HD].rearrange("p t h d -> p (t h) d"),
                                   bank[7].rearrange("p (th d) -> p th d", d=HD),
                                   ACT.Identity).then_inc(a["v_ready"], 1)
                elif kind == "CS":
                    c = ev[1]
                    act.wait_ge(a["pv_done"], at_group(pb, pg, CU, 4 if c == 0 else CU))
                    if not (young and c == 0 and pg == 0):
                        act.wait_ge(a["ctxn_ready"], at_group(pb, pg, 2, c))
                    act.activation(cs, bank[6], ACT.Identity).then_inc(a["cs_ready"], 1)
                elif kind == "R":
                    c = ev[1]
                    act.wait_ge(a["rec_ready"], at_group(pb, pg, 2, c + 1))
                    if not (young and c == 0 and pg == 0):
                        act.wait_ge(a["rb_full"], at_group(pb, pg, 2, c))
                    act.activation(rexp.rearrange("p (k r) -> p k r", r=32),
                                   rec.unsqueeze(2).to_broadcast([P, 4 * TPC, 32]),
                                   ACT.Identity).then_inc(a["rexp_ready"], 1)
                elif kind == "S":
                    n, j = ev[1:]
                    c, kt = C_UNITS[n]
                    off = max(CHUNK * c, P * kt) - CHUNK * c
                    if j == 0 and not (young and n < 2 and pg == 0):
                        act.wait_ge(a["pv_done"], at_group(pb, pg, CU, n - 1))
                    idx = 4 * n + j
                    act.wait_ge(a["s_full"], at_group(pb, pg, 4 * CU, idx + 1))
                    act.activation(PT[:, n % 2, j, off:], bank[4 + idx % 2][:, off:],
                                   ACT.Exp).then_inc(a["exp_done"], 1)

            def pool_h(pool, ev, b, g, pb, pg, fresh, young):
                kind = ev[0]
                if kind == "A":
                    ag, p = ev[1], ev[2]
                    pool.wait_ge(a["pr_ready"], at_group(b, ag, 4, p + 1))
                    if not (fresh and ag == 0 and p < 2):
                        pool.wait_ge(a["split_done"], at_group(b, ag, 4, p - 1))
                    pool.sem_inc(a["pool_steps"], 1)
                    s = p % 2
                    if p < 2:
                        pool.tensor_scalar(part_far[:, s, :], pr_far[:, s, :], C[:, C_QLO:C_QLO + 1], 0.0,
                                           ALU.mult, ALU.add)
                        pool.tensor_scalar(part_band[:, s, :], pr_band[:, s, :], C[:, C_QLO:C_QLO + 1], 0.0,
                                           ALU.mult, ALU.add).then_inc(a["part_ready"], 1)
                        pool.wait_ge(a["part_ready"], at_group(b, ag, 4, p + 1))
                        cols, apar = slice(CHUNK * s, CHUNK * (s + 1)), ag % 2
                        pool.tensor_tensor(QF[:, ag % GROUPS, cols], pr_far[:, s, :], part_far[:, s, :], ALU.subtract)
                        pool.tensor_tensor(QB[:, apar, cols], pr_band[:, s, :], part_band[:, s, :],
                                           ALU.subtract).then_inc(a["split_done"], 1)
                    else:
                        pool.tensor_scalar(part_far[:, s, :], pr_far[:, s, :], C[:, C_KLO:C_KLO + 1],
                                           C[:, C_ONE:C_ONE + 1], ALU.mult, ALU.add).then_inc(a["part_ready"], 1)
                        pool.wait_ge(a["part_ready"], at_group(b, ag, 4, p + 1))
                        if not (fresh and ag == 0):
                            pool.wait_ge(a["k_ready"], at_group(b, ag, 2, p - 3))
                        pool.tensor_tensor(Kfull[:, s, :], pr_far[:, s, :], part_far[:, s, :],
                                           ALU.subtract).then_inc(a["split_done"], 1)
                elif kind == "M":
                    pool.wait_ge(a["nm_ready"], at_group(pb, pg, 1, 1))
                    if not (young and pg == 0):
                        pool.wait_ge(a["s_full"], at_group(pb, pg, 4 * CU, 0))
                    for i in range(QT):
                        pool.tensor_tensor(TD[:, i, :, :], T[:, i, :, CLIP:],
                                           nmr[:, i, :].unsqueeze(2).to_broadcast([P, 4, P]),
                                           ALU.add).then_inc(a["td_ready"], 1)

            def band_max(dve, b, g, i):
                lo = 0 if i else CLIP
                for u in range(2):
                    dve.wait_ge(a["b_free"][u], at_group(b, g, B_PER, fill_at(i, len(b_steps(i)) - 1) + 1))
                dve.tensor_reduce(mxp[:, i, :, 2], T[:, i, :, lo:], AXX, ALU.max).then_inc(a["mx_done"], 1)

            def dve_h(dve, ev, b, g, pb, pg, fresh, young):
                kind = ev[0]
                par, ppar = g % 2, pg % 2
                if kind == "AD":
                    ag, p = ev[1], ev[2]
                    s, apar = p % 2, ag % 2
                    cols = slice(CHUNK * s, CHUNK * (s + 1))
                    if p >= 2:
                        dve.wait_ge(a["split_done"], at_group(b, ag, 4, p + 1))
                        for j in range(4):
                            rows = slice(32 * j, 32 * (j + 1))
                            ins = dve.tensor_copy(KM[rows, ag % GROUPS, j, cols], Kfull[rows, s, :])
                        ins.then_inc(a["k_ready"], 1)
                elif kind == "BD":
                    i, u, n, h = ev[1:]
                    pair = PS[:, 2 * u:2 * u + 2, :]
                    js = slice(2 * u, 2 * u + 2)
                    k0, k1, band = b_steps(i)[n]
                    cnt = fill_at(i, n)
                    far = k1 - k0
                    dve.wait_ge(a["b_full"][u], at_group(b, g, B_PER, cnt + 1))
                    if not band:
                        dve.tensor_reduce(mxp[:, i, js, 0], pair[:, :, 0:far], AXX,
                                          ALU.max).then_inc(a["b_free"][u], 1)
                        return
                    lo = 0 if i else CLIP
                    w = BAND - lo
                    if not fresh and u == 0:
                        dve.wait_ge(a["td_ready"], at_group(b, g, QT, i + 1 - QT))
                    if i:
                        dve.tensor_tensor(E[:, par, i, js, CLIP:], pair[0:CLIP, :, far:far + CLIP],
                                          D[0:CLIP, :].unsqueeze(1).to_broadcast([CLIP, 2, CLIP]), ALU.mult)
                    if far:
                        dve.tensor_reduce(mxp[:, i, js, 1], pair[:, :, 0:far], AXX, ALU.max)
                    dve.tensor_tensor(T[:, i, js, lo:], pair[:, :, far:far + w],
                                      A[:, lo:].unsqueeze(1).to_broadcast([P, 2, w]),
                                      ALU.mult).then_inc(a["b_free"][u], 1)
                    if u == 1 and i:
                        band_max(dve, b, g, i - 1)
                    if u == 1 and i == QT - 1:
                        dve.wait_ge(a["b_free"][u], at_group(b, g, B_PER, cnt + 1))
                        band_max(dve, b, g, i)
                elif kind == "M":
                    k = [0]
                    dve.wait_ge(a["mx_done"], at_group(pb, pg, QT, QT))
                    m4v = M4.rearrange("p t (j r) -> p t j r", r=32)

                    def step(ins):
                        k[0] += 1
                        ins.then_inc(a["m_chain"], 1)
                        dve.wait_ge(a["m_chain"], at_group(pb, pg, 3, k[0]))
                    step(dve.tensor_reduce(nmax, mxp, AXX, ALU.max, negate=True))
                    step(dve.tensor_copy(m4v[:, :, :, 24], nmax))
                    step(dve.tensor_tensor(m4v[:, :, :, 25], nmax, m4v[:, :, :, 24], ALU.subtract))
                    dve.sem_inc(a["m4_ready"], 1)
                    dve.tensor_tensor(nmr, m4v[:, :, :, 24], m4v[:, :, :, 25], ALU.add).then_inc(a["nm_ready"], 1)
                elif kind == "M2":
                    for r in range(2):
                        cols = slice(CHUNK * r, CHUNK * (r + 1))
                        dve.wait_ge(a["mt_full"], at_group(pb, pg, 2, r + 1))
                        dve.tensor_tensor(QF[:, pg, cols], bank[7 - r], QF[:, pg, cols],
                                          ALU.add).then_inc(a["mt_done"], 1)
                elif kind == "ND":
                    c = ev[1]
                    dve.wait_ge(a["den_full"], at_group(pb, pg, 2, c + 1))
                    if not (young and c == 0 and pg == 0):
                        dve.wait_ge(a["rexp_ready"], at_group(pb, pg, 2, c))
                    dve.reciprocal(rec, bank[7][:, 0:4 * TPC]).then_inc(a["rec_ready"], 1)
                elif kind == "N2D":
                    c = ev[1]
                    dve.wait_ge(a["rb_full"], at_group(pb, pg, 2, c + 1))
                    dve.tensor_tensor(ctxn[:, c, :], bank[7], cs, ALU.mult).then_inc(a["ctxn_ready"], 1)
                elif kind == "OD":
                    c = ev[1]
                    dve.wait_ge(a["o_full"], at_group(pb, pg, 2, c + 1))
                    if not (young and c == 0 and pg == 0):
                        dve.wait_ge(a["x_added"], at_group(pb, pg, 2, c))
                    tiles = bass.ds(pb * QT + TPC * c, TPC)
                    dve.tensor_tensor(X[:, tiles, :], bank[7].rearrange("p (t d) -> p t d", t=TPC), X[:, tiles, :],
                                      ALU.add).then_inc(a["x_added"], 1)

            return a, pe_h, act_h, pool_h, dve_h

        a, pe_h, act_h, pool_h, dve_h = attention_handlers() if "at" in phases else (None,) * 5

        def sp_attention(sp):
            if "f1" in phases:
                sp.wait_ge(F[1]["x_done"], CHUNKS)
            for i, w in enumerate((Wq, Wk, Wv)):
                sp.dma_start(wqkv[:, i, :], w).then_inc(a["w_loaded"], 16)
            sp.wait_ge(a["zeroed"], 1)
            for j in range(4):
                sp.dma_start(wo_rep[32 * j:32 * j + HD, :, :],
                             Wo.rearrange("(g j d) n -> j d g n", j=4, d=HD)[j]).then_inc(a["w_loaded"], 16)

        def pool_attention(pool):
            if "f1" in phases:
                pool.wait_ge(F[1]["x_done"], CHUNKS)
            pool.memset(wo_rep, 0.0).then_inc(a["zeroed"], 1)
            pool.memset(wq_rep, 0.0)
            pool.memset(wk_rep, 0.0)
            pool.memset(M4, 0.0)
            pool.memset(E, 0.0)
            pool.memset(KM, 0.0)
            pool.memset(mxp, LOWEST)
            pool.memset(vaug, 0.0).then_inc(a["zeroed"], 1)
            pool.wait_ge(a["zeroed"], 2)
            pool.memset(vaug[:, :, :, HD:HD + 1], 1.0).then_inc(a["zeroed"], 1)
            pool.wait_ge(a["w_loaded"], 16 * 7)
            for rep_, i in ((wq_rep, 0), (wk_rep, 1)):
                for r in range(3):
                    ins = pool.tensor_copy(rep_[:, :, HD * r:HD * (r + 1)],
                                           wqkv[:, i, :].rearrange("p (h d) -> p h d", d=HD))
            ins.then_inc(a["w_rep"], 1)
            pool.sem_inc(a["lo_ready"], 2)
            with pool.Fori(0, CHUNKS // 2) as c2:
                for u in range(2):
                    pool.wait_ge(a["hi_ready"], c2 * 2 + (u + 1))
                    cols = bass.ds(c2 * (2 * CHUNK) + u * CHUNK, CHUNK)
                    pool.tensor_tensor(t_lo[:, cols], xT32[:, u, :], t_hi[:, cols],
                                       ALU.subtract).then_inc(a["lo_ready"], 1)
            pool.wait_ge(a["band_ready"], 1)
            run_plan(pool, pool_h)

        def act_attention(act):
            act.wait_ge(a["stats"], 1)
            act.activation(tmp0[:], var[:], ACT.Sqrt).then_inc(a["sd"], 1)
            act.wait_ge(a["w_rep"], 1)
            for hi, src in ((wq_hi, wq_rep), (wk_hi, wk_rep)):
                act.activation(hi.rearrange("p g c -> p (g c)"), src.rearrange("p h r -> p (h r)"), ACT.Identity)
            act.activation(wv_hi, wqkv[:, 2, :], ACT.Identity).then_inc(a["w_hi"], 1)
            with act.Fori(0, CHUNKS // 2) as c2:
                for u in range(2):
                    c1 = c2 * 2 + (u + 1)
                    act.wait_ge(a["tr_full"], c1 + 2)
                    act.wait_ge(a["lo_ready"], c1)
                    act.activation(xT32[:, u, :], bank[u], ACT.Identity).then_inc(a["xT_ready"], 1)
                    act.wait_ge(a["xT_ready"], c1 + 2)
                    act.activation(t_hi[:, bass.ds(c2 * (2 * CHUNK) + u * CHUNK, CHUNK)], xT32[:, u, :],
                                   ACT.Identity).then_inc(a["hi_ready"], 1)
            act.wait_ge(a["lo_ready"], CHUNKS + 2)
            act.wait_ge(a["w_lo"], 1)
            act.wait_ge(a["zeroed"], 3)
            run_plan(act, act_h)

        def pe_attention(pe):
            pe.sem_inc(a["tr_full"], 2)
            with pe.Fori(0, CHUNKS // 2) as c2:
                for u in range(2):
                    c1 = c2 * 2 + (u + 1)
                    pe.wait_ge(a["xT_ready"], c1)
                    pe_transpose_chunk(pe, u, a["xn_ready"], a["tr_full"], c1)
            pe.wait_ge(a["lo_ready"], CHUNKS + 2)
            pe.wait_ge(a["hi_ready"], CHUNKS)
            pe.wait_ge(a["w_lo"], 1)
            pe.wait_ge(a["xT_ready"], CHUNKS + 2)
            run_plan(pe, pe_h)

        def dve_attention(dve):
            dve_stats(dve, a["stats"], a["sd"])
            dve.sem_inc(a["xT_ready"], 2)
            dve_normalise(dve, a["xn_ready"], a["tr_full"])
            dve.wait_ge(a["xn_ready"], CHUNKS)
            dve.tensor_tensor(X[:], X[:], bo_bc[:].unsqueeze(1).to_broadcast([P, TILES, P]),
                              ALU.add).then_inc(a["bo_added"], 1)
            dve.wait_ge(a["bo_added"], 1)
            link(dve, dve.tensor_scalar(sq_far, rel_bc[:, CLIP:CLIP + 1], SCALE, None, ALU.mult))
            rel_diff = rexp[:, 0:CLIP]
            link(dve, dve.tensor_scalar(rel_diff, rel_bc[:, 0:CLIP], rel_bc[:, CLIP:CLIP + 1], None, ALU.subtract))
            link(dve, dve.memset(A, 0.0))
            for dist in range(CLIP):
                ind = C[:, C_SHIFT + 144 + dist:C_SHIFT + 144 + dist + BAND]
                link(dve, dve.scalar_tensor_tensor(out=A, in0=ind, scalar=rel_diff[:, dist:dist + 1], in1=A,
                                                   op0=ALU.mult, op1=ALU.add))
            link(dve, dve.tensor_copy(D, A[:, 0:CLIP]))
            link(dve, dve.tensor_scalar(A, A, rel_bc[:, CLIP:CLIP + 1], None, ALU.add))
            msk, m2 = rexp[:, 0:P], rexp[:, P:2 * P]
            link(dve, dve.tensor_scalar(msk, C[:, C_NEG:C_NEG + P], 0.0, None, ALU.is_lt))
            link(dve, dve.tensor_scalar(m2, A[:, CLIP:], -1.0, 1.0, ALU.mult, ALU.add))
            link(dve, dve.tensor_tensor(m2, m2, msk, ALU.mult))
            link(dve, dve.tensor_tensor(A[:, CLIP:], A[:, CLIP:], m2, ALU.add))
            dve.sem_inc(a["band_ready"], 1)
            dve.wait_ge(a["w_hi"], 1)
            for lo, hi, src in ((wq_lo, wq_hi, wq_rep), (wk_lo, wk_hi, wk_rep)):
                dve.tensor_tensor(lo.rearrange("p g c -> p (g c)"), src.rearrange("p h r -> p (h r)"),
                                  hi.rearrange("p g c -> p (g c)"), ALU.subtract)
            dve.tensor_tensor(wv_lo, wqkv[:, 2, :], wv_hi, ALU.subtract).then_inc(a["w_lo"], 1)
            dve.wait_ge(a["w_lo"], 1)
            dve.wait_ge(a["zeroed"], 3)
            run_plan(dve, dve_h)
            dve.wait_ge(a["x_added"], BATCH * GROUPS * 2)


        def sp_expert_weights(sp, n):
            if n:
                sp.wait_ge(a["td_ready"], BATCH * GROUPS * QT)
            sp.dma_start(stage[:, 0, :].rearrange("p (e h) -> p e h", e=EXPERTS),
                         W1.rearrange("e d h -> d e h")).then_inc(s_stage, 16)
            if n:
                sp.wait_ge(a["x_added"], BATCH * GROUPS * 2)
            sp.dma_start(stage[:, 1, :].rearrange("p (e t d) -> p e t d", e=EXPERTS, t=HT),
                         W2.rearrange("e (t p) d -> p e t d", p=P)).then_inc(s_stage2, 16)

        def act_expert_weights(act, n, k):
            act.wait_ge((s_stage, s_stage2)[k], 16 * (n + 1))
            act.activation(weights[:, 2 * k, :], stage[:, k, :], ACT.Identity).then_inc(s_hi, 1)

        def dve_expert_weights(dve, n, k):
            dve.wait_ge(s_hi, 2 * n + k + 1)
            dve.tensor_tensor(weights[:, 2 * k + 1, :], stage[:, k, :], weights[:, 2 * k, :],
                              ALU.subtract).then_inc(s_lo, 1)

        @block.sync
        def _(sp):
            sp.dma_start(C[:], cst).then_inc(s_w, 16)
            for b in range(BATCH):
                sp.dma_start(X[:, QT * b:QT * (b + 1), :],
                             x[b].rearrange("(t p) d -> p t d", p=P)).then_inc(s_x, 16)
            sp.dma_start(w_in[:], W_in).then_inc(s_w, 16)
            sp.dma_start(w_gate[:], W_gate).then_inc(s_w, 16)
            sp.dma_start(b_in_col[:], b_in.rearrange("(p a) -> p a", a=1)).then_inc(s_w, 16)
            sp.dma_start(b_gate_bc[:], b_gate.partition_broadcast(P)).then_inc(s_w, 16)
            sp.dma_start(b1_rows[:], b1.rearrange("e (t p) -> (e t) p", p=P)).then_inc(s_w, 16)
            sp.dma_start(b2_rows[:], b2).then_inc(s_w, 16)
            sp.dma_start(w_out[:], W_out).then_inc(s_w, 16)
            sp.dma_start(half_b_out[:], b_out.partition_broadcast(P)).then_inc(s_w, 16)
            sp.dma_start(bo_bc[:], bo.partition_broadcast(P)).then_inc(s_w, 16)
            sp.dma_start(rel_bc[:], rel_emb.partition_broadcast(P)).then_inc(s_w, 16)
            if "f1" in phases:
                sp_expert_weights(sp, 0)
            if "at" in phases:
                sp_attention(sp)
            if "f2" in phases:
                sp_expert_weights(sp, 1)
            last = F[2] if "f2" in phases else None
            for c in range(CHUNKS):
                if last:
                    sp.wait_ge(last["x_done"], c + 1)
                else:
                    sp.wait_ge(s_in_done, 1)
                b, r = c // 2, c % 2
                sp.dma_start(out[b, CHUNK * r:CHUNK * (r + 1), :].rearrange("(t p) d -> p t d", p=P),
                             X[:, TPC * c:TPC * (c + 1), :]).then_inc(s_out, 16)
            sp.wait_ge(s_out, 16 * CHUNKS)

        N_W = 16 * 11

        def dve_ffn(dve, f, n):
            dve_stats(dve, f["stats"], f["sd"])
            dve_normalise(dve, f["xn_ready"], f["tr_full"])
            dve_expert_weights(dve, n - 1, 0)
            dve_expert_weights(dve, n - 1, 1)
            dve.wait_ge(f["lg_ready"], CHUNKS)
            bc = [P, TILES, EXPERTS]
            link(dve, dve.tensor_tensor(logits, logits, b_gate_bc[:].unsqueeze(1).to_broadcast(bc), ALU.add))
            ordb = order[:].unsqueeze(1).to_broadcast(bc)
            src = logits
            for oh, top in ((oh1, top1), (oh2, top2)):
                link(dve, dve.tensor_reduce(top, src, AXX, ALU.max))
                link(dve, dve.tensor_tensor(oh, src, top.unsqueeze(2).to_broadcast(bc), ALU.is_ge))
                link(dve, dve.tensor_tensor(oh, oh, ordb, ALU.mult))
                link(dve, dve.tensor_reduce(rt1, oh, AXX, ALU.max))
                link(dve, dve.tensor_tensor(oh, ordb, rt1.unsqueeze(2).to_broadcast(bc), ALU.is_equal))
                if oh is oh1:
                    link(dve, dve.scalar_tensor_tensor(out=rtmp, in0=oh, scalar=LOWEST, in1=logits,
                                                       op0=ALU.mult, op1=ALU.add))
                    src = rtmp
            dve.tensor_tensor(rt1, top2, top1, ALU.subtract).then_inc(f["rt_d"], 1)
            dve.wait_ge(f["rt_e"], 1)
            link(dve, dve.tensor_scalar(top1, rt2, 1.0, None, ALU.add))
            link(dve, dve.reciprocal(top2, top1))
            link(dve, dve.tensor_tensor(rt2, rt2, top2, ALU.mult))
            link(dve, dve.tensor_tensor(oh1, oh1, top2.unsqueeze(2).to_broadcast(bc), ALU.mult))
            link(dve, dve.tensor_tensor(oh2, oh2, rt2.unsqueeze(2).to_broadcast(bc), ALU.mult))
            link(dve, dve.tensor_tensor(route, oh1, oh2, ALU.add))

            dve.sem_inc(f["fa_full"], 1)
            dve.sem_inc(f["acc_chain"], 2)

            def parts(c, e):
                s = e % 2
                dve.wait_ge(f["dn_full"], c * EXPERTS + (e + 1))
                for ht in range(HT):
                    dve.wait_ge(f["mid32_ready"], c * 32 + (HT * e + ht + 1 + HT))
                    if ht % 2:
                        dve.tensor_copy(mid_hi[:, s, ht, :], mid32[:, ht, :]).then_inc(f["hi_dve"], 1)
                        dve.wait_ge(f["hi_dve"], c * 16 + (2 * e + ht // 2 + 1))
                    else:
                        dve.wait_ge(f["hi_act"], c * 16 + (2 * e + ht // 2 + 1))
                    dve.tensor_tensor(mid_lo[:, s, ht, :], mid32[:, ht, :], mid_hi[:, s, ht, :],
                                      ALU.subtract).then_inc(f["lo_done"], 1)

            def add_expert(c, d):
                dve.wait_ge(f["dn_full"], c * EXPERTS + (d + 3))
                if d == 0:
                    dve.wait_ge(f["fa_full"], c + 1)
                else:
                    dve.wait_ge(f["acc_chain"], c * EXPERTS + (d + 2))
                y = bank[4 + d % 2].rearrange("p (t d) -> p t d", t=TPC)
                for k in range(TPC):
                    r = route_c[:, k, d % EXPERTS:d % EXPERTS + 1]
                    if d == 0:
                        ins = dve.tensor_scalar(acc[:, k, :], y[:, k, :], r, None, ALU.mult)
                    else:
                        ins = dve.scalar_tensor_tensor(out=acc[:, k, :], in0=y[:, k, :], scalar=r,
                                                       in1=acc[:, k, :], op0=ALU.mult, op1=ALU.add)
                ins.then_inc(f["acc_chain"], 1)

            def add_output(c):
                Xc = X[:, bass.ds(c * TPC - TPC, TPC), :]
                dve.tensor_tensor(Xc, Xc, half_b_out[:].unsqueeze(1).to_broadcast([P, TPC, P]),
                                  ALU.add).then_inc(f["fa_chain"], 1)
                dve.wait_ge(f["fa_chain"], c)
                dve.wait_ge(f["fb_full"], c)
                dve.scalar_tensor_tensor(out=Xc, in0=bank[7].rearrange("p (t d) -> p t d", t=TPC),
                                         scalar=0.5, in1=Xc, op0=ALU.mult, op1=ALU.add).then_inc(f["x_done"], 1)

            def chunk(c, first):
                for e in range(EXPERTS):
                    parts(c, e)
                    if e or not first:
                        add_expert(c, e - 1)
                    if e == 0:
                        if not first:
                            dve.wait_ge(f["rT_full"], c)
                            dve.wait_ge(f["acc_chain"], c * EXPERTS + 2)
                        dve.tensor_copy(route_c, route[:, bass.ds(c * TPC, TPC), :]).then_inc(f["rc_ready"], 1)
                        dve.wait_ge(f["rc_ready"], c + 1)
                    if e == 2 and not first:
                        add_output(c)

            chunk(0, True)
            with dve.Fori(1, CHUNKS) as c:
                chunk(c, False)
            add_expert(CHUNKS, -1)
            add_output(CHUNKS)
            dve.wait_ge(f["x_done"], CHUNKS)

        def act_ffn(act, f, n):
            act.wait_ge(f["stats"], 1)
            act.activation(tmp0[:], var[:], ACT.Sqrt).then_inc(f["sd"], 1)
            if n == 2:
                act_expert_weights(act, n - 1, 0)

            def tokens_copy(c, u):
                act.wait_ge(f["tr_full"], c + 3)
                act.wait_ge(f["h_full"], c + 1)
                act.activation(xnT[:, u, :], bank[u], ACT.Identity).then_inc(f["xnT_ready"], 1)

            def hidden_copy(c, u):
                act.wait_ge(f["h_full"], c + 3)
                act.wait_ge(f["lo_ready"], c + 1)
                act.activation(h32[:, u, :], bank[2 + u], ACT.Identity,
                               bias=b_in_col[:]).then_inc(f["h32_ready"], 1)
                act.wait_ge(f["h32_ready"], c + 1)
                act.activation(t_hi[:, bass.ds(c * CHUNK, CHUNK)], h32[:, u, :],
                               ACT.Identity).then_inc(f["hi_ready"], 1)

            def logits_copy(c, u):
                act.wait_ge(f["lg_full"], c + 1)
                act.activation(logits[:, bass.ds(c * TPC, TPC), :],
                               bank[4 + u][:, 0:TPC * EXPERTS].rearrange("p (t e) -> p t e", t=TPC),
                               ACT.Identity).then_inc(f["lg_ready"], 1)

            tokens_copy(0, 0)
            tokens_copy(1, 1)
            hidden_copy(0, 0)
            with act.Fori(0, CHUNKS // 2 - 1) as c2:
                for u in range(2):
                    c = c2 * 2 + (u + 1)
                    tokens_copy(c + 1, u)
                    hidden_copy(c, 1 - u)
                    logits_copy(c2 * 2 + u, u)
            hidden_copy(CHUNKS - 1, 1)
            logits_copy(CHUNKS - 2, 0)
            logits_copy(CHUNKS - 1, 1)
            if n == 1:
                act_expert_weights(act, n - 1, 0)
            act_expert_weights(act, n - 1, 1)
            act.wait_ge(f["rt_d"], 1)
            act.activation(rt2, rt1, ACT.Exp).then_inc(f["rt_e"], 1)
            act.sem_inc(f["mid32_ready"], HT)

            def sum_copy(c):
                act.wait_ge(f["fa_full"], c + 1)
                act.activation(moT, bank[6], ACT.Identity).then_inc(f["fa_ready"], 1)

            def chunk(c, first):
                for e in range(EXPERTS):
                    s = e % 2
                    if e == 2 and not first:
                        sum_copy(c)
                    if e == 5:
                        act.wait_ge(f["rT_full"], c + 1)
                        act.wait_ge(f["fa_full"], c + 1)
                        act.activation(routeT, bank[7][0:EXPERTS, :], ACT.Identity).then_inc(f["rT_ready"], 1)
                    act.wait_ge(f["dn_full"], c * EXPERTS + (e + 1))
                    for ht in range(HT):
                        i = HT * e + ht
                        act.wait_ge(f["up_full"], c * 32 + (i + 1))
                        act.wait_ge(f["lo_done"], c * 32 + (i + 1))
                        act.activation(mid32[:, ht, :], bank[ht], ACT.Relu,
                                       bias=b1_cols[:, i:i + 1]).then_inc(f["mid32_ready"], 1)
                        if ht % 2:
                            act.wait_ge(f["mid32_ready"], c * 32 + (i + HT))
                            act.activation(mid_hi[:, s, ht - 1, :], mid32[:, ht - 1, :],
                                           ACT.Identity).then_inc(f["hi_act"], 1)

            chunk(0, True)
            with act.Fori(1, CHUNKS) as c:
                chunk(c, False)
            sum_copy(CHUNKS)

        def pe_transpose_chunk(pe, u, xn_ready, tr_full, c1):
            pe.wait_ge(xn_ready, c1)
            for k in range(TPC):
                ins = pe.matmul(bank[u][:, P * k:P * (k + 1)], xn[:, u, k, :], ident, start=(k == 0), stop=True,
                                is_transpose=True, skip_group_check=True)
            ins.then_inc(tr_full, 1)

        def pe_ffn(pe, f, n):
            pe.sem_inc(f["h_full"], 2)
            pe.sem_inc(f["tr_full"], 2)

            def transposes(c, u):
                pe_transpose_chunk(pe, u, f["xn_ready"], f["tr_full"], c + 1)

            def hidden(c, u):
                pe.wait_ge(f["xnT_ready"], c + 1)
                pe.matmul(bank[2 + u], w_in[:], xnT[:, u, :], start=True, stop=True).then_inc(f["h_full"], 1)

            def gate(c, u):
                pe.wait_ge(f["h32_ready"], c + 1)
                for k in range(TPC):
                    ins = pe.matmul(bank[4 + u][:, EXPERTS * k:EXPERTS * (k + 1)], h32[:, u, P * k:P * (k + 1)],
                                    w_gate[:], start=(k == 0), stop=True, skip_group_check=True)
                ins.then_inc(f["lg_full"], 1)

            transposes(0, 0)
            transposes(1, 1)
            hidden(0, 0)
            with pe.Fori(0, CHUNKS // 2 - 1) as c2:
                for u in range(2):
                    c = c2 * 2 + (u + 1)
                    transposes(c + 1, u)
                    hidden(c, 1 - u)
                    gate(c2 * 2 + u, u)
            hidden(CHUNKS - 1, 1)
            gate(CHUNKS - 2, 0)
            gate(CHUNKS - 1, 1)
            pe.wait_ge(s_lo, 2 * n - 1)
            pe.wait_ge(s_b1, 1)
            pe.wait_ge(f["lo_ready"], CHUNKS + 2)
            pe.wait_ge(f["hi_ready"], CHUNKS)
            pe.wait_ge(f["lg_ready"], CHUNKS)
            pe.sem_inc(f["lo_done"], HT)
            pe.sem_inc(f["dn_full"], 2)

            def up(c, e):
                cols = bass.ds(c * CHUNK, CHUNK)
                for ht in range(HT):
                    i = HT * e + ht
                    pe.wait_ge(f["mid32_ready"], c * 32 + (i + 1))
                    w_h, w_l = w1_hi[:, e, P * ht:P * (ht + 1)], w1_lo[:, e, P * ht:P * (ht + 1)]
                    pe.matmul(bank[ht], w_h, t_hi[:, cols], start=True, stop=False)
                    pe.matmul(bank[ht], w_h, t_lo[:, cols], start=False, stop=False)
                    pe.matmul(bank[ht], w_l, t_hi[:, cols], start=False, stop=True).then_inc(f["up_full"], 1)

            def down(c, d):
                s, w = d % 2, d % EXPERTS
                pe.wait_ge(f["hi_act"], c * 16 + (2 * d + 2))
                pe.wait_ge(f["lo_done"], c * 32 + (HT * d + 2 * HT))
                pe.wait_ge(f["acc_chain"], c * EXPERTS + (d + 1))
                for k in range(TPC):
                    tok = slice(P * k, P * (k + 1))
                    for ht in range(HT):
                        m_h, m_l = mid_hi[:, s, ht, tok], mid_lo[:, s, ht, tok]
                        o = bank[4 + s][:, tok]
                        pe.matmul(o, m_h, w2_hi[:, w, ht, :], start=(k == 0 and ht == 0), stop=False,
                                  skip_group_check=True)
                        pe.matmul(o, m_h, w2_lo[:, w, ht, :], start=False, stop=False,
                                  skip_group_check=True)
                        ins = pe.matmul(o, m_l, w2_hi[:, w, ht, :], start=False, stop=(ht == HT - 1),
                                        skip_group_check=True)
                ins.then_inc(f["dn_full"], 1)

            def last_sum(c):
                pe.wait_ge(f["rT_ready"], c)
                pe.matmul(bank[6], b2_rows[:], routeT, start=True, stop=False, skip_group_check=True)

            def transpose_sum(c):
                pe.wait_ge(f["acc_chain"], c * EXPERTS + 2)
                for k in range(TPC):
                    ins = pe.matmul(bank[6][:, P * k:P * (k + 1)], acc[:, k, :], ident, start=False, stop=True,
                                    skip_group_check=True)
                ins.then_inc(f["fa_full"], 1)

            def output(c):
                pe.wait_ge(f["fa_ready"], c)
                for k in range(TPC):
                    ins = pe.matmul(bank[7][:, P * k:P * (k + 1)], moT[:, P * k:P * (k + 1)], w_out[:],
                                    start=(k == 0), stop=True, skip_group_check=True)
                ins.then_inc(f["fb_full"], 1)

            def chunk(c, first):
                for e in range(EXPERTS):
                    up(c, e)
                    if e == 1 and not first:
                        transpose_sum(c)
                    if e == 2 and not first:
                        output(c)
                    if e or not first:
                        if e == 0 or (e == 1 and first):
                            pe.wait_ge(s_lo, 2 * n)
                        down(c, e - 1)
                    if e == 0 and not first:
                        last_sum(c)
                    if e == 4:
                        pe.wait_ge(f["rc_ready"], c + 1)
                        if not first:
                            pe.wait_ge(f["x_done"], c)
                        for k in range(TPC):
                            ins = pe.matmul(bank[7][0:EXPERTS, P * k:P * (k + 1)], route_c[:, k, :], ident,
                                            start=(k == 0), stop=True, is_transpose=True, skip_group_check=True)
                        ins.then_inc(f["rT_full"], 1)

            chunk(0, True)
            with pe.Fori(1, CHUNKS) as c:
                chunk(c, False)
            down(CHUNKS, -1)
            last_sum(CHUNKS)
            transpose_sum(CHUNKS)
            output(CHUNKS)

        def pool_ffn(pool, f):
            pool.sem_inc(f["lo_ready"], 2)
            with pool.Fori(0, CHUNKS // 2) as c2:
                for u in range(2):
                    pool.wait_ge(f["hi_ready"], c2 * 2 + (u + 1))
                    cols = bass.ds(c2 * (2 * CHUNK) + u * CHUNK, CHUNK)
                    pool.tensor_tensor(t_lo[:, cols], h32[:, u, :], t_hi[:, cols],
                                       ALU.subtract).then_inc(f["lo_ready"], 1)

        @block.gpsimd
        def _(pool):
            for e in range(EXPERTS):
                ins = pool.memset(order[:, e:e + 1], float(EXPERTS - e))
            ins.then_inc(s_cst, 1)
            if "f1" in phases:
                pool_ffn(pool, F[1])
            if "at" in phases:
                pool_attention(pool)
            if "f2" in phases:
                pool_ffn(pool, F[2])

        @block.vector
        def _(dve):
            dve.wait_ge(s_w, N_W)
            dve.tensor_copy(ident_bf[:], ident)
            dve.tensor_copy(neg_bf[:], C[:, C_NEG:C_NEG + P])
            link(dve, dve.tensor_scalar(half_b_out[:], half_b_out[:], 0.5, None, ALU.mult))
            dve.wait_ge(s_b1T, 1)
            dve.tensor_copy(b1_cols[:], bank[6][:, 0:EXPERTS * HT]).then_inc(s_b1, 1)
            dve.wait_ge(s_x, 16 * BATCH)
            dve.wait_ge(s_cst, 1)
            if "f1" in phases:
                dve_ffn(dve, F[1], 1)
            if "at" in phases:
                dve_attention(dve)
            if "f2" in phases:
                dve_ffn(dve, F[2], 2)
            dve.sem_inc(s_in_done, 1)

        @block.scalar
        def _(act):
            act.wait_ge(s_w, N_W)
            if "f1" in phases:
                act_ffn(act, F[1], 1)
            if "at" in phases:
                act_attention(act)
            if "f2" in phases:
                act_ffn(act, F[2], 2)

        @block.tensor
        def _(pe):
            pe.wait_ge(s_w, N_W)
            pe.transpose(bank[6][:, 0:EXPERTS * HT], b1_rows[:], C[0:EXPERTS * HT, C_ID:C_ID + EXPERTS * HT]).then_inc(s_b1T, 1)
            if "f1" in phases:
                pe_ffn(pe, F[1], 1)
            if "at" in phases:
                pe_attention(pe)
            if "f2" in phases:
                pe_ffn(pe, F[2], 2)


_INS = ["L0_attn_x", "L0_attn_Wq", "L0_attn_Wk", "L0_attn_Wv", "L0_attn_Wo", "L0_attn_bo", "L0_attn_rel_emb",
        "L0_ffn_W_in", "L0_ffn_b_in", "L0_ffn_W_gate", "L0_ffn_b_gate", "L0_ffn_W1", "L0_ffn_b1", "L0_ffn_W2",
        "L0_ffn_b2", "L0_ffn_W_out", "L0_ffn_b_out"]


def kernel(**inputs):
    import numpy as _np
    import concourse.bacc as _bacc
    from concourse import mybir as _mybir
    from concourse.bass_utils import run_bass_kernel_spmd as _run

    nc = _bacc.Bacc("TRN2", target_bir_lowering=False, num_devices=1)
    arrays, args = {}, []
    for name in _INS:
        a = _np.ascontiguousarray(inputs[name])
        arrays[f"in_{name}"] = a
        args.append(nc.dram_tensor(f"in_{name}", a.shape, _mybir.dt.from_np(a.dtype), kind="ExternalInput").ap())
    c = consts()
    arrays["consts"] = c
    args.append(nc.dram_tensor("consts", c.shape, _mybir.dt.float32, kind="ExternalInput").ap())
    args.append(nc.dram_tensor("out_0", (BATCH, SEQ, P), _mybir.dt.float32, kind="ExternalOutput").ap())
    build(nc, *args)
    r = _run(nc, [arrays], core_ids=[0])
    return r.results[0]["out_0"]
```

```python
from contextlib import ExitStack

import concourse.bass as bass
from concourse import mybir

F32 = mybir.dt.float32
BF16 = mybir.dt.bfloat16
ALU = mybir.AluOpType
ACT = mybir.ActivationFunctionType
AXX = mybir.AxisListType.X

P = 128
BATCH = 4
SEQ = 1024
TOKENS = BATCH * SEQ
TILES = TOKENS // P
CHUNK = 512
CHUNKS = TOKENS // CHUNK
TPC = CHUNK // P
EXPERTS = 8
HID = 512
HT = HID // P
HEADS = 16
HD = 8
CLIP = 16
GROUPS = HEADS // 4
QT = SEQ // P
BAND = P + CLIP
LN_EPS = 1e-5
MASKED = -1e30
LOWEST = -3e38
SCALE = float(HD) ** -0.5
C_ID, C_SHIFT, C_NEG, C_SEL, C_QLO, C_KLO, C_ONE = 0, 128, 448, 576, 704, 705, 706
C_ALL = 707


def consts():
    import numpy as np
    c = np.zeros((P, C_ALL), np.float32)
    p = np.arange(P)
    c[p, C_ID + p] = 1.0
    c[p, C_SHIFT + 160 + p] = 1.0
    c[:, C_NEG:C_NEG + P] = np.where(np.arange(P)[None, :] > p[:, None], MASKED, 0.0)
    c[32 * (p // 32) + HD, C_SEL + p] = 1.0
    r = p % 32
    c[:, C_QLO] = (r >= 8) & (r < 16)
    c[:, C_KLO] = (r >= 16) & (r < 24)
    c[:, C_ONE] = np.where((r == 24) | (r == 25), -1.0, 0.0)
    return c


def build(nc, x, Wq, Wk, Wv, Wo, bo, rel_emb, W_in, b_in, W_gate, b_gate, W1, b1, W2, b2,
          W_out, b_out, cst, out, phases=("f1", "at", "f2")):
    ctx = ExitStack()
    with ctx:
        def sb(name, shape, dt=F32):
            return ctx.enter_context(nc.sbuf_tensor(name, shape, dt))

        def sem(name):
            return ctx.enter_context(nc.semaphore(name))

        PS = ctx.enter_context(nc.psum_tensor("PS", [P, 8, CHUNK], F32))
        bank = [PS[:, i, :] for i in range(8)]

        X = sb("X", [P, TILES, P])
        C = sb("C", [P, C_ALL])
        ident = C[:, C_ID:C_ID + P]
        ident_bf = sb("ident_bf", [P, P], BF16)
        neg_bf = sb("neg_bf", [P, P], BF16)
        W_PART = EXPERTS * HID
        weights = sb("weights", [P, 4, W_PART], BF16)
        w1_hi, w1_lo = (weights[:, k, :].rearrange("p (e h) -> p e h", e=EXPERTS) for k in (0, 1))
        w2_hi, w2_lo = (weights[:, k, :].rearrange("p (e t d) -> p e t d", e=EXPERTS, t=HT) for k in (2, 3))
        w_in, w_out = sb("w_in", [P, P]), sb("w_out", [P, P])
        w_gate = sb("w_gate", [P, EXPERTS])
        b_in_col = sb("b_in_col", [P, 1])
        b_gate_bc = sb("b_gate_bc", [P, EXPERTS])
        b1_rows = sb("b1_rows", [EXPERTS * HT, P])
        b1_cols = sb("b1_cols", [P, EXPERTS * HT])
        b2_rows = sb("b2_rows", [EXPERTS, P])
        half_b_out = sb("half_b_out", [P, P])
        bo_bc = sb("bo_bc", [P, P])
        rel_bc = sb("rel_bc", [P, CLIP + 1])
        t_hi, t_lo = sb("t_hi", [P, TOKENS], BF16), sb("t_lo", [P, TOKENS], BF16)
        order = sb("order", [P, EXPERTS])
        bn = sb("bn", [P, TILES, 6])
        mean, var, rstd, tmp0, tmp1 = (sb(n, [P, TILES]) for n in ("mean", "var", "rstd", "tmp0", "tmp1"))
        xn = sb("xn", [P, 2, TPC, P])
        A, D, sq_far = sb("A", [P, BAND])[:], sb("D", [P, CLIP])[:], sb("sq_far", [P, 1])[:]
        BIG = 33000 - BAND - CLIP - 1
        big = sb("big", [P, BIG])

        def carve():
            at = [0]

            def take(shape, dt=F32, parts=P):
                n = 1
                for s in shape:
                    n *= s
                words = n if dt == F32 else (n + 1) // 2
                v = big[0:parts, at[0]:at[0] + words]
                at[0] += words
                assert at[0] <= BIG, at[0]
                if dt != F32:
                    v = v.bitcast(dt)
                names = " ".join(f"a{i}" for i in range(len(shape)))
                if len(shape) > 1:
                    v = v.rearrange(f"p ({names}) -> p {names}", **{f"a{i}": s for i, s in enumerate(shape)})
                return v
            return take, at

        T_AT = 12416

        take, used = carve()
        xnT, h32 = take([2, CHUNK]), take([2, CHUNK])
        mid32 = take([HT, CHUNK])
        mid_hi, mid_lo = take([2, HT, CHUNK], BF16), take([2, HT, CHUNK], BF16)
        acc = take([TPC, P])
        moT = take([CHUNK])
        routeT = take([CHUNK], parts=EXPERTS)
        route_c = take([TPC, EXPERTS])
        logits, oh1, oh2, rtmp, route = (take([TILES, EXPERTS]) for _ in range(5))
        top1, top2, rt1, rt2 = (take([TILES]) for _ in range(4))
        take([T_AT - used[0]])
        stage = take([2, W_PART])

        take, used = carve()
        wq_hi, wq_lo, wk_hi, wk_lo = (take([GROUPS, P], BF16) for _ in range(4))
        wv_hi, wv_lo = take([P], BF16), take([P], BF16)
        wo_rep = take([GROUPS, P])
        pr_far, pr_band = take([2, CHUNK]), take([2, CHUNK])
        sum_rows = C[:, C_ID:C_ID + P].rearrange("p (j r) -> p j r", r=32)[:, :, HD]
        part_far, part_band = take([2, CHUNK], BF16), take([2, CHUNK], BF16)
        QF, QB = take([GROUPS, SEQ], BF16), take([2, SEQ], BF16)
        Kfull = take([2, CHUNK], BF16)
        KM = weights[:].rearrange("p k n -> p (k n)").rearrange("p (g j s) -> p g j s", g=GROUPS, j=4)
        TD = take([QT, 4, P])
        take([T_AT - used[0]])
        T = take([QT, 4, BAND])
        nmax, nmr = take([QT, 4]), take([QT, 4])
        PT = take([2, 4, CHUNK])
        assert used[0] >= T_AT + 2 * W_PART
        vaug = take([QT, HEADS, 32])
        E = take([2, QT, 4, 32], parts=CLIP)
        mxp = take([QT, 4, 3])
        M4 = take([QT, P], BF16)
        cs = take([CHUNK])
        rexp = take([CHUNK])
        band_tmp = stage[:, 0, 0:2 * P]
        rec = take([4 * TPC])
        ctxn = xn[:].rearrange("p s k d -> p s (k d)")
        ptw = PT.rearrange("p a b c -> p (a b c)")
        xT32 = ptw[:, 0:2 * CHUNK].rearrange("p (s c) -> p s c", s=2)
        wqkv = ptw[:, 1024:1024 + 3 * P].rearrange("p (w n) -> p w n", w=3)
        wq_rep = ptw[:, 1536:2048].rearrange("p (h r) -> p h r", h=HEADS)
        wk_rep = ptw[:, 2048:2560].rearrange("p (h r) -> p h r", h=HEADS)

        s_x = [sem(f"x_loaded{b}") for b in range(BATCH)]
        s_w = sem("weights_loaded")
        s_stage = sem("expert_weights_staged")
        s_stage2 = sem("expert_w2_staged")
        s_hi = sem("expert_hi_ready")
        s_lo = sem("expert_lo_ready")
        s_hi2 = sem("expert_w2_hi_ready")
        s_lo2 = sem("expert_w2_lo_ready")
        s_vc = sem("vector_chain")
        s_cst = sem("constants_ready")
        s_b1T = sem("b1_transposed")
        s_b1 = sem("b1_cols_ready")
        s_band = sem("band_ready")
        s_zero = sem("zeros_ready")
        s_out = sem("stored")
        s_in_done = sem("phase_done")

        block = ctx.enter_context(nc.Block())

        chain = [0]

        def link(dve, ins):
            chain[0] += 1
            ins.then_inc(s_vc, 1)
            dve.wait_ge(s_vc, chain[0])

        def ffn_semaphores(n):
            return {s: sem(f"ffn{n}_{s}") for s in (
                "stats", "sd", "xn_ready", "tr_full", "xnT_ready", "h_full", "h32_ready", "lg_full", "lg_ready",
                "hi_ready", "lo_ready", "rt_d", "rt_e", "up_full", "mid32_ready", "hi_act", "hi_dve",
                "lo_done", "dn_full", "acc_chain", "rc_ready", "rT_full", "rT_ready", "fa_full", "fa_ready",
                "fb_full", "x_done", "fa_chain")}

        F = {1: ffn_semaphores(1), 2: ffn_semaphores(2)}

        BAND_STEPS = 6

        def dve_band(dve, step):
            rel_diff, msk, m2 = band_tmp[:, 0:CLIP], band_tmp[:, 0:P], band_tmp[:, P:2 * P]
            if step == 0:
                if "f1" in phases:
                    dve.wait_ge(s_lo, 2)
                link(dve, dve.tensor_scalar(sq_far, rel_bc[:, CLIP:CLIP + 1], SCALE, None, ALU.mult))
                link(dve, dve.tensor_scalar(rel_diff, rel_bc[:, 0:CLIP], rel_bc[:, CLIP:CLIP + 1], None, ALU.subtract))
                link(dve, dve.memset(A, 0.0))
            elif step < 5:
                for dist in range(CLIP // 4 * (step - 1), CLIP // 4 * step):
                    ind = C[:, C_SHIFT + 144 + dist:C_SHIFT + 144 + dist + BAND]
                    link(dve, dve.scalar_tensor_tensor(out=A, in0=ind, scalar=rel_diff[:, dist:dist + 1], in1=A,
                                                       op0=ALU.mult, op1=ALU.add))
            else:
                link(dve, dve.tensor_copy(D, A[:, 0:CLIP]))
                link(dve, dve.tensor_scalar(A, A, rel_bc[:, CLIP:CLIP + 1], None, ALU.add))
                link(dve, dve.tensor_scalar(msk, C[:, C_NEG:C_NEG + P], 0.0, None, ALU.is_lt))
                link(dve, dve.tensor_scalar(m2, A[:, CLIP:], -1.0, 1.0, ALU.mult, ALU.add))
                link(dve, dve.tensor_tensor(m2, m2, msk, ALU.mult))
                link(dve, dve.tensor_tensor(A[:, CLIP:], A[:, CLIP:], m2, ALU.add))
                dve.sem_inc(s_band, 1)

        def tile_stats(dve, tiles):
            for t in tiles:
                ins = dve.bn_stats(bn[:, t, :], X[:, t, :])
            return ins

        def dve_stats(dve, stats_sem, sd_sem, tiles=range(TILES)):
            link(dve, tile_stats(dve, tiles))
            m_e, v_e, m_o, v_o = bn[:, :, 1], bn[:, :, 2], bn[:, :, 4], bn[:, :, 5]
            dve.tensor_tensor(mean[:], m_e, m_o, ALU.add)
            dve.tensor_tensor(tmp0[:], m_e, m_o, ALU.subtract)
            link(dve, dve.tensor_tensor(var[:], v_e, v_o, ALU.add))
            dve.tensor_scalar(mean[:], mean[:], 0.5, None, ALU.mult)
            dve.tensor_tensor(tmp1[:], tmp0[:], tmp0[:], ALU.mult)
            link(dve, dve.tensor_scalar(var[:], var[:], 1.0 / P, LN_EPS, ALU.mult, ALU.add))
            link(dve, dve.scalar_tensor_tensor(out=var[:], in0=tmp1[:], scalar=0.25, in1=var[:],
                                               op0=ALU.mult, op1=ALU.add))
            dve.sem_inc(stats_sem, 1)
            dve.wait_ge(sd_sem, 1)
            link(dve, dve.reciprocal(rstd[:], tmp0[:]))
            link(dve, dve.tensor_tensor(tmp1[:], rstd[:], rstd[:], ALU.mult))
            link(dve, dve.tensor_tensor(tmp1[:], tmp1[:], var[:], ALU.mult))
            link(dve, dve.tensor_scalar(tmp1[:], tmp1[:], -0.5, 1.5, ALU.mult, ALU.add))
            link(dve, dve.tensor_tensor(rstd[:], rstd[:], tmp1[:], ALU.mult))

        def normalise(dve, c, u, xn_ready, tr_full):
            dve.wait_ge(tr_full, c + 1)
            for k in range(TPC):
                t = bass.ds(c * TPC + k, 1)
                ins = dve.tensor_scalar(xn[:, u, k, :], X[:, t, :].rearrange("p a d -> p (a d)"), mean[:, t], rstd[:, t],
                                        ALU.subtract, ALU.mult)
            ins.then_inc(xn_ready, 1)

        def dve_normalise(dve, xn_ready, tr_full):
            with dve.Fori(0, CHUNKS // 2) as c2:
                for u in range(2):
                    normalise(dve, c2 * 2 + u, u, xn_ready, tr_full)

        def b_steps(i):
            far = max(P * i - CLIP, 0)
            if far + BAND <= CHUNK:
                return [(0, far, True)]
            cut = min(far, CHUNK)
            return [(0, cut, False), (cut, far, True)]

        FILL_ORDER = [(7, 0), (5, 0), (6, 0), (4, 0), (0, 0), (1, 0), (2, 0), (3, 0), (4, 1), (5, 1), (6, 1), (7, 1)]
        FILLS = [(i, u, n) for i, n in FILL_ORDER for u in range(2)]
        FILL_HEADS = [f_ + (h,) for f_ in FILLS for h in range(2)]
        B_PER = len(FILL_ORDER)

        def fill_at(i, n):
            return FILL_ORDER.index((i, n))

        C_UNITS = [(c, k) for c in range(SEQ // CHUNK) for k in range(TPC * (c + 1))]
        CU = len(C_UNITS)

        ENDS = ("N", "ND", "R", "N2", "N2D", "O", "OD")
        AT = {"CS": (4, 3), ("N", -1): (0, 0), ("ND", -1): (0, 0), ("R", -1): (1, 0),
              ("N2", -1): (1, 3), ("N2D", -1): (2, 2), ("O", -1): (2, 3), ("OD", -1): (3, 0),
              ("N", 0): (5, 3), ("ND", 0): (6, 0), ("R", 0): (6, 2), ("N2", 0): (6, 3),
              ("N2D", 0): (7, 0), ("O", 0): (7, 3), ("OD", 0): (8, 0), ("A", 0): (3, 2),
              ("A", 1): (5, 0), ("A", 2): (9, 0), ("A", 3): (9, 3), ("AD", 2): (10, 0),
              ("AD", 3): (10, 0), "M": (10, 1), ("MP", 0): (11, 0), ("M2", 0): (11, 1),
              ("MP", 1): (11, 2), ("M2", 1): (11, 3)}
        FILLS_AT = ((0, 1, 2, 3), (0, 1, 1, 2, 2, 3), (0, 1, 2, 3), (0, 1, 3), (0, 1, 2, 3), (0, 2, 3),
                    (0, 1, 2, 3, 3), (0, 1, 2, 3), (0, 1, 1, 2), (0, 2, 3), (0, 3), (0, 1, 2, 3))
        FILLS_LAST, FILLS_END = 1, 0
        M_EVENTS = [("M", ()), ("MP", (0,)), ("M2", (0,)), ("MP", (1,)), ("M2", (1,))]

        def c_events(lead2, nxt=None):
            ev = []
            for n in range(CU):
                for j in range(4):
                    ev.append(("S", n, j))
                    ev += ["b"] * FILLS_AT[n].count(j)
                    if n and j == 1:
                        ev.append(("PV", n - 1))
                    if (n, j) == AT["CS"]:
                        ev.append(("CS", 0))
                    for c in (-1, 0):
                        if c == 0 or lead2:
                            ev += [(e, c) for e in ENDS if AT[e, c] == (n, j)]
                    if nxt is not None:
                        ev += [(e,) + v for e, v in M_EVENTS if AT[(e,) + v[:1] if v else e] == (n, j)]
                        ev += [("A", nxt, p) for p in range(4) if AT["A", p] == (n, j)]
                        ev += [("AD", nxt, p) for p in (2, 3) if AT["AD", p] == (n, j)]
            return ev

        AHEAD = 8

        def slot_plan(g, lead, lead2):
            nxt = g + 1
            pieces = [("A", nxt, p) for p in range(4)]
            ev = []
            if lead:
                v = [("V", 0), ("V", 1)] if g == 0 else []
                ev += c_events(lead2, nxt) + ["b"] * FILLS_LAST + [("PV", CU - 1), ("CS", 1)] + v + ["b"] * FILLS_END
            else:
                for k in range(len(FILL_HEADS)):
                    ev.append("b")
                    ev += {8: [("V", 0)], 12: [("V", 1)], 18: pieces[:1], 22: pieces[1:2], 28: pieces[2:3],
                           34: pieces[3:], 40: [("AD", nxt, 2)], 44: [("AD", nxt, 3)]}.get(k, [])
                ev += [("M",)] + ["b"] * AHEAD + [(e,) + v for e, v in M_EVENTS[1:]]
            here = FILL_HEADS[AHEAD if lead else 0:]
            fills = [f_ + (g,) for f_ in here] + [f_ + (nxt,) for f_ in FILL_HEADS[:AHEAD]]
            assert not any(b_steps(f_[0])[f_[2]][2] for f_ in FILL_HEADS[:AHEAD])
            out_ = []

            def fill():
                f_ = fills.pop(0)
                out_.append(("B",) + f_)
                if f_[3]:
                    out_.append(("BD",) + f_)
            for e in ev:
                if e == ("M",):
                    while fills and fills[0][-1] == g:
                        fill()
                if e != "b":
                    out_.append(e)
                elif fills and (fills[0][-1] == g or ("M",) in out_):
                    fill()
            while fills:
                fill()
            return out_

        TAIL = [("ST",)] + [e for e in c_events(True) if e != "b"] \
            + [("PV", CU - 1), ("CS", 1)] + [(e, 1) for e in ENDS]

        def run_plan(eng, handler):
            for ev in [("A", 0, p) for p in range(4)] + [("AD", 0, 2), ("AD", 0, 3)]:
                handler(eng, ev, 0, 0, 0, 0, True, True)

            def batch(b, first):
                if not first:
                    handler(eng, ("START",), b, 0, b, 0, False, False)
                for g in range(GROUPS):
                    lead = not (first and g == 0)
                    pb, pg = (b, g - 1) if g else (b - 1, GROUPS - 1)
                    qb, qg = (b, g - 2) if g >= 2 else (b - 1, g + GROUPS - 2)
                    for ev in slot_plan(g, lead, lead and not (first and g == 1)):
                        if ev[-1] == -1:
                            handler(eng, (ev[0], 1), b, g, qb, qg, False, False)
                        elif ev[0] in ("B", "BD"):
                            handler(eng, ev[:-1], b, ev[-1], pb, pg, first and ev[-1] == 0, first and ev[-1] <= 1)
                        elif ev[0] in ("M", "MP", "M2"):
                            handler(eng, ev, b, g, b, g, first and g == 0, first and g == 0)
                        else:
                            handler(eng, ev, b, g, pb, pg, first and g == 0, first and g <= 1)
            batch(0, True)
            with eng.Fori(1, BATCH) as b:
                batch(b, False)
            for ev in [("START",)] + TAIL:
                if ev[-1] == -1:
                    handler(eng, (ev[0], 1), BATCH, 0, BATCH - 1, GROUPS - 2, False, False)
                else:
                    handler(eng, ev, BATCH, 0, BATCH - 1, GROUPS - 1, False, False)

        def attention_handlers():
            a = {s_: sem("attn_" + s_) for s_ in (
                "stats", "sd", "xn_ready", "tr_full", "xT_ready", "hi_ready", "lo_ready", "w_loaded", "wo_loaded", "w_rep", "w_hi",
                "w_lo", "zeroed", "bo_added", "pr_full", "pr_ready", "split_done",
                "part_ready", "k_ready", "v_full", "v_ready", "mx_done", "m_chain", "m4_ready",
                "nm_ready", "mt_full", "mt_done", "td_ready", "s_full", "exp_done", "pv_done", "cs_ready", "den_full",
                "rec_ready", "rexp_ready", "rb_full", "ctxn_ready", "o_full", "x_added", "pool_steps")}
            a["b_full"] = [sem(f"attn_b_full{u}") for u in range(2)]
            a["b_free"] = [sem(f"attn_b_free{u}") for u in range(2)]

            def at_group(pb, pg, per, k):
                return pb * (GROUPS * per) + (pg * per + k)

            def pe_h(pe, ev, b, g, pb, pg, fresh, young):
                kind = ev[0]
                par, ppar = g % 2, pg % 2
                if kind == "START":
                    misc[0] = (a["mt_done"], at_group(b, 0, 2, 0))
                elif kind == "A":
                    ag, p = ev[1], ev[2]
                    w_h, w_l = (wq_hi, wq_lo) if p < 2 else (wk_hi, wk_lo)
                    start = (b * SEQ + SEQ) % TOKENS if ag == GROUPS else b * SEQ
                    cols = bass.ds(start + CHUNK * (p % 2), CHUNK)
                    misc_wait(pe)
                    pe.matmul(bank[7], w_h[:, ag % GROUPS, :], t_hi[:, cols], start=True, stop=False)
                    pe.matmul(bank[7], w_h[:, ag % GROUPS, :], t_lo[:, cols], start=False, stop=False)
                    pe.matmul(bank[7], w_l[:, ag % GROUPS, :], t_hi[:, cols], start=False, stop=True).then_inc(a["pr_full"], 1)
                    misc_used(a["pr_ready"], at_group(b, ag, 4, p + 1))
                elif kind == "V":
                    r = ev[1]
                    misc_wait(pe)
                    for k in range(TPC):
                        tok = bass.ds(b * SEQ + P * (TPC * r + k), P)
                        o = bank[7][:, P * k:P * (k + 1)]
                        pe.matmul(o, t_hi[:, tok], wv_hi, start=(k == 0), stop=False, skip_group_check=True)
                        pe.matmul(o, t_hi[:, tok], wv_lo, start=False, stop=False, skip_group_check=True)
                        ins = pe.matmul(o, t_lo[:, tok], wv_hi, start=False, stop=True, skip_group_check=True)
                    ins.then_inc(a["v_full"], 1)
                    misc_used(a["v_ready"], b * 2 + (r + 1))
                elif kind == "B":
                    i, u, n, h = ev[1:]
                    if (i, u, n, h) == FILL_HEADS[0]:
                        pe.wait_ge(a["k_ready"], at_group(b, g, 2, 2))
                        pe.wait_ge(a["split_done"], at_group(b, g, 4, 2))
                    k0, k1, band = b_steps(i)[n]
                    cnt = fill_at(i, n)
                    if h == 0 and not (fresh and cnt == 0):
                        pe.wait_ge(a["b_free"][u], at_group(b, g, B_PER, cnt))
                    far = k1 - k0
                    w = BAND if i else P
                    j = 2 * u + h
                    bk = bank[j]
                    qs = slice(P * i, P * (i + 1))
                    if band:
                        pe.matmul(bk[:, far + w - P:far + w], ident_bf[:], neg_bf[:],
                                  start=True, stop=False, skip_group_check=True)
                    if far:
                        ins = pe.matmul(bk[:, 0:far], QF[:, g % GROUPS, qs], KM[:, g % GROUPS, j, k0:k1],
                                        start=not band, stop=True, skip_group_check=True)
                    if band:
                        ins = pe.matmul(bk[:, far:far + w], QB[:, par, qs], KM[:, g % GROUPS, j, k1:k1 + w],
                                        start=False, stop=True, skip_group_check=True)
                    if h:
                        ins.then_inc(a["b_full"][u], 1)
                elif kind == "MP":
                    r = ev[1]
                    pe.wait_ge(a["m4_ready"], at_group(pb, pg, 1, 1))
                    misc_wait(pe)
                    for k in range(TPC):
                        ins = pe.matmul(bank[7][:, P * k:P * (k + 1)], M4[:, TPC * r + k, :], ident_bf[:],
                                        start=(k == 0), stop=True, skip_group_check=True)
                    ins.then_inc(a["mt_full"], 1)
                    misc_used(a["mt_done"], at_group(pb, pg, 2, r + 1))
                elif kind == "S":
                    n, j = ev[1:]
                    c, kt = C_UNITS[n]
                    off = max(CHUNK * c, P * kt) - CHUNK * c
                    diag = P * kt >= CHUNK * c
                    if kt == 0 and j == 0:
                        pe.wait_ge(a["mt_done"], at_group(pb, pg, 2, c + 1))
                    if diag and j == 0:
                        pe.wait_ge(a["td_ready"], at_group(pb, pg, QT, kt + 1))
                    idx = 4 * n + j
                    bk = bank[4 + idx % 2]
                    if not (young and idx < 2 and pg == 0):
                        pe.wait_ge(a["exp_done"], at_group(pb, pg, 4 * CU, idx - 1))
                    far = off
                    if diag:
                        ins = pe.matmul(bk[:, off:off + P], TD[:, kt, j, :], ident, start=True, stop=True,
                                        is_transpose=True, skip_group_check=True)
                        far = off + P
                    if far < CHUNK:
                        ins = pe.matmul(bk[:, far:], KM[:, pg, j, P * kt:P * (kt + 1)],
                                        QF[:, pg, CHUNK * c + far:CHUNK * (c + 1)], start=not diag, stop=True,
                                        skip_group_check=True)
                    nq = P * (kt + 1) - CHUNK * c
                    if 0 <= nq < CHUNK:
                        ins = pe.matmul(bk[96:128, nq:nq + CLIP], E[:, ppar, kt + 1, j, :], ident[0:CLIP, 0:CLIP],
                                        start=False, stop=True, skip_group_check=True)
                    ins.then_inc(a["s_full"], 1)
                elif kind == "PV":
                    n = ev[1]
                    c, kt = C_UNITS[n]
                    off = max(CHUNK * c, P * kt) - CHUNK * c
                    pe.wait_ge(a["exp_done"], at_group(pb, pg, 4 * CU, 4 * n + 4))
                    if n == 0:
                        pe.wait_ge(a["v_ready"], pb * 2 + 2)
                    if kt == 0 and not (young and c == 0 and pg == 0):
                        pe.wait_ge(a["cs_ready"], at_group(pb, pg, 2, c))
                    last = kt == TPC * (c + 1) - 1
                    for j in range(4):
                        ins = pe.matmul(bank[6][32 * j:32 * (j + 1), off:], vaug[:, kt, 4 * pg + j, :],
                                        PT[:, n % 2, j, off:], start=(kt == 0), stop=last,
                                        skip_group_check=True)
                    ins.then_inc(a["pv_done"], 1)
                elif kind == "N":
                    c = ev[1]
                    pe.wait_ge(a["cs_ready"], at_group(pb, pg, 2, c + 1))
                    misc_wait(pe)
                    for k in range(TPC):
                        ins = pe.matmul(bank[7][:, 4 * k:4 * k + 4], cs[:, P * k:P * (k + 1)], sum_rows,
                                        start=(k == 0), stop=True, skip_group_check=True)
                    ins.then_inc(a["den_full"], 1)
                    misc_used(a["rec_ready"], at_group(pb, pg, 2, c + 1))
                elif kind == "N2":
                    c = ev[1]
                    pe.wait_ge(a["rexp_ready"], at_group(pb, pg, 2, c + 1))
                    misc_wait(pe)
                    for k in range(TPC):
                        ins = pe.matmul(bank[7][:, P * k:P * (k + 1)], rexp[:, P * k:P * (k + 1)], ident,
                                        start=(k == 0), stop=True, is_transpose=True, skip_group_check=True)
                    ins.then_inc(a["rb_full"], 1)
                    misc_used(a["ctxn_ready"], at_group(pb, pg, 2, c + 1))
                elif kind == "O":
                    c = ev[1]
                    pe.wait_ge(a["ctxn_ready"], at_group(pb, pg, 2, c + 1))
                    misc_wait(pe)
                    for k in range(TPC):
                        ins = pe.matmul(bank[7][:, P * k:P * (k + 1)], ctxn[:, c, P * k:P * (k + 1)], wo_rep[:, pg, :],
                                        start=(k == 0), stop=True, skip_group_check=True)
                    ins.then_inc(a["o_full"], 1)
                    misc_used(a["x_added"], at_group(pb, pg, 2, c + 1))

            misc = [None]

            def misc_wait(pe):
                if misc[0] is not None:
                    pe.wait_ge(*misc[0])

            def misc_used(sem_, value):
                misc[0] = (sem_, value)

            def act_h(act, ev, b, g, pb, pg, fresh, young):
                kind = ev[0]
                if kind == "A":
                    ag, p = ev[1], ev[2]
                    s = p % 2
                    act.wait_ge(a["pr_full"], at_group(b, ag, 4, p + 1))
                    if not (fresh and ag == 0 and p < 2):
                        act.wait_ge(a["split_done"], at_group(b, ag, 4, p - 1))
                    if p < 2:
                        act.activation(pr_band[:, s, :], bank[7], ACT.Identity, scale=SCALE)
                        act.activation(pr_far[:, s, :], bank[7], ACT.Identity, scale=sq_far).then_inc(a["pr_ready"], 1)
                    else:
                        act.activation(pr_far[:, s, :], bank[7], ACT.Identity).then_inc(a["pr_ready"], 1)
                elif kind == "V":
                    r = ev[1]
                    act.wait_ge(a["v_full"], b * 2 + (r + 1))
                    act.activation(vaug[:, TPC * r:TPC * (r + 1), :, 0:HD].rearrange("p t h d -> p (t h) d"),
                                   bank[7].rearrange("p (th d) -> p th d", d=HD),
                                   ACT.Identity).then_inc(a["v_ready"], 1)
                elif kind == "CS":
                    c = ev[1]
                    act.wait_ge(a["pv_done"], at_group(pb, pg, CU, 4 if c == 0 else CU))
                    if not (young and c == 0 and pg == 0):
                        act.wait_ge(a["ctxn_ready"], at_group(pb, pg, 2, c))
                    act.activation(cs, bank[6], ACT.Identity).then_inc(a["cs_ready"], 1)
                elif kind == "R":
                    c = ev[1]
                    act.wait_ge(a["rec_ready"], at_group(pb, pg, 2, c + 1))
                    if not (young and c == 0 and pg == 0):
                        act.wait_ge(a["rb_full"], at_group(pb, pg, 2, c))
                    act.activation(rexp.rearrange("p (k r) -> p k r", r=32),
                                   rec.unsqueeze(2).to_broadcast([P, 4 * TPC, 32]),
                                   ACT.Identity).then_inc(a["rexp_ready"], 1)
                elif kind == "S":
                    n, j = ev[1:]
                    c, kt = C_UNITS[n]
                    off = max(CHUNK * c, P * kt) - CHUNK * c
                    if j == 0 and not (young and n < 2 and pg == 0):
                        act.wait_ge(a["pv_done"], at_group(pb, pg, CU, n - 1))
                    idx = 4 * n + j
                    act.wait_ge(a["s_full"], at_group(pb, pg, 4 * CU, idx + 1))
                    act.activation(PT[:, n % 2, j, off:], bank[4 + idx % 2][:, off:],
                                   ACT.Exp).then_inc(a["exp_done"], 1)

            def pool_h(pool, ev, b, g, pb, pg, fresh, young):
                kind = ev[0]
                if kind == "A":
                    ag, p = ev[1], ev[2]
                    pool.wait_ge(a["pr_ready"], at_group(b, ag, 4, p + 1))
                    if not (fresh and ag == 0 and p < 2):
                        pool.wait_ge(a["split_done"], at_group(b, ag, 4, p - 1))
                    pool.sem_inc(a["pool_steps"], 1)
                    s = p % 2
                    if p < 2:
                        pool.tensor_scalar(part_far[:, s, :], pr_far[:, s, :], C[:, C_QLO:C_QLO + 1], 0.0,
                                           ALU.mult, ALU.add)
                        pool.tensor_scalar(part_band[:, s, :], pr_band[:, s, :], C[:, C_QLO:C_QLO + 1], 0.0,
                                           ALU.mult, ALU.add).then_inc(a["part_ready"], 1)
                        pool.wait_ge(a["part_ready"], at_group(b, ag, 4, p + 1))
                        cols, apar = slice(CHUNK * s, CHUNK * (s + 1)), ag % 2
                        pool.tensor_tensor(QF[:, ag % GROUPS, cols], pr_far[:, s, :], part_far[:, s, :], ALU.subtract)
                        pool.tensor_tensor(QB[:, apar, cols], pr_band[:, s, :], part_band[:, s, :],
                                           ALU.subtract).then_inc(a["split_done"], 1)
                    else:
                        pool.tensor_scalar(part_far[:, s, :], pr_far[:, s, :], C[:, C_KLO:C_KLO + 1],
                                           C[:, C_ONE:C_ONE + 1], ALU.mult, ALU.add).then_inc(a["part_ready"], 1)
                        pool.wait_ge(a["part_ready"], at_group(b, ag, 4, p + 1))
                        if not (fresh and ag == 0):
                            pool.wait_ge(a["k_ready"], at_group(b, ag, 2, p - 3))
                        pool.tensor_tensor(Kfull[:, s, :], pr_far[:, s, :], part_far[:, s, :],
                                           ALU.subtract).then_inc(a["split_done"], 1)
                elif kind == "M":
                    pool.wait_ge(a["nm_ready"], at_group(pb, pg, 1, 1))
                    for i in range(QT):
                        if not (young and pg == 0):
                            last = C_UNITS.index((i // TPC, i))
                            pool.wait_ge(a["s_full"], at_group(pb, pg, 4 * CU, 4 * (last + 1) - 4 * CU))
                        pool.tensor_tensor(TD[:, i, :, :], T[:, i, :, CLIP:],
                                           nmr[:, i, :].unsqueeze(2).to_broadcast([P, 4, P]),
                                           ALU.add).then_inc(a["td_ready"], 1)

            def band_max(dve, b, g, i):
                lo = 0 if i else CLIP
                for u in range(2):
                    dve.wait_ge(a["b_free"][u], at_group(b, g, B_PER, fill_at(i, len(b_steps(i)) - 1) + 1))
                dve.tensor_reduce(mxp[:, i, :, 2], T[:, i, :, lo:], AXX, ALU.max).then_inc(a["mx_done"], 1)

            def dve_h(dve, ev, b, g, pb, pg, fresh, young):
                kind = ev[0]
                par, ppar = g % 2, pg % 2
                if kind == "AD":
                    ag, p = ev[1], ev[2]
                    s, apar = p % 2, ag % 2
                    cols = slice(CHUNK * s, CHUNK * (s + 1))
                    if p >= 2:
                        dve.wait_ge(a["split_done"], at_group(b, ag, 4, p + 1))
                        for j in range(4):
                            rows = slice(32 * j, 32 * (j + 1))
                            ins = dve.tensor_copy(KM[rows, ag % GROUPS, j, cols], Kfull[rows, s, :])
                        ins.then_inc(a["k_ready"], 1)
                elif kind == "BD":
                    i, u, n, h = ev[1:]
                    pair = PS[:, 2 * u:2 * u + 2, :]
                    js = slice(2 * u, 2 * u + 2)
                    k0, k1, band = b_steps(i)[n]
                    cnt = fill_at(i, n)
                    far = k1 - k0
                    dve.wait_ge(a["b_full"][u], at_group(b, g, B_PER, cnt + 1))
                    if not band:
                        dve.tensor_reduce(mxp[:, i, js, 0], pair[:, :, 0:far], AXX,
                                          ALU.max).then_inc(a["b_free"][u], 1)
                        return
                    lo = 0 if i else CLIP
                    w = BAND - lo
                    if not fresh and u == 0:
                        dve.wait_ge(a["td_ready"], at_group(b, g, QT, i + 1 - QT))
                    if i:
                        dve.tensor_tensor(E[:, par, i, js, CLIP:], pair[0:CLIP, :, far:far + CLIP],
                                          D[0:CLIP, :].unsqueeze(1).to_broadcast([CLIP, 2, CLIP]), ALU.mult)
                    if far:
                        dve.tensor_reduce(mxp[:, i, js, 1], pair[:, :, 0:far], AXX, ALU.max)
                    dve.tensor_tensor(T[:, i, js, lo:], pair[:, :, far:far + w],
                                      A[:, lo:].unsqueeze(1).to_broadcast([P, 2, w]),
                                      ALU.mult).then_inc(a["b_free"][u], 1)
                    if u == 1 and i:
                        band_max(dve, b, g, i - 1)
                    if u == 1 and i == QT - 1:
                        dve.wait_ge(a["b_free"][u], at_group(b, g, B_PER, cnt + 1))
                        band_max(dve, b, g, i)
                elif kind == "M":
                    k = [0]
                    dve.wait_ge(a["mx_done"], at_group(pb, pg, QT, QT))
                    m4v = M4.rearrange("p t (j r) -> p t j r", r=32)

                    def step(ins):
                        k[0] += 1
                        ins.then_inc(a["m_chain"], 1)
                        dve.wait_ge(a["m_chain"], at_group(pb, pg, 3, k[0]))
                    step(dve.tensor_reduce(nmax, mxp, AXX, ALU.max, negate=True))
                    step(dve.tensor_copy(m4v[:, :, :, 24], nmax))
                    step(dve.tensor_tensor(m4v[:, :, :, 25], nmax, m4v[:, :, :, 24], ALU.subtract))
                    dve.sem_inc(a["m4_ready"], 1)
                    dve.tensor_tensor(nmr, m4v[:, :, :, 24], m4v[:, :, :, 25], ALU.add).then_inc(a["nm_ready"], 1)
                elif kind == "M2":
                    r = ev[1]
                    cols = slice(CHUNK * r, CHUNK * (r + 1))
                    dve.wait_ge(a["mt_full"], at_group(pb, pg, 2, r + 1))
                    dve.tensor_tensor(QF[:, pg, cols], bank[7], QF[:, pg, cols],
                                      ALU.add).then_inc(a["mt_done"], 1)
                elif kind == "ST":
                    dve.wait_ge(a["x_added"], at_group(BATCH - 2, GROUPS - 1, 2, 2))
                    tile_stats(dve, range((BATCH - 1) * QT))
                elif kind == "ND":
                    c = ev[1]
                    dve.wait_ge(a["den_full"], at_group(pb, pg, 2, c + 1))
                    if not (young and c == 0 and pg == 0):
                        dve.wait_ge(a["rexp_ready"], at_group(pb, pg, 2, c))
                    dve.reciprocal(rec, bank[7][:, 0:4 * TPC]).then_inc(a["rec_ready"], 1)
                elif kind == "N2D":
                    c = ev[1]
                    dve.wait_ge(a["rb_full"], at_group(pb, pg, 2, c + 1))
                    dve.tensor_tensor(ctxn[:, c, :], bank[7], cs, ALU.mult).then_inc(a["ctxn_ready"], 1)
                elif kind == "OD":
                    c = ev[1]
                    dve.wait_ge(a["o_full"], at_group(pb, pg, 2, c + 1))
                    if not (young and c == 0 and pg == 0):
                        dve.wait_ge(a["x_added"], at_group(pb, pg, 2, c))
                    tiles = bass.ds(pb * QT + TPC * c, TPC)
                    dve.tensor_tensor(X[:, tiles, :], bank[7].rearrange("p (t d) -> p t d", t=TPC), X[:, tiles, :],
                                      ALU.add).then_inc(a["x_added"], 1)

            return a, pe_h, act_h, pool_h, dve_h

        a, pe_h, act_h, pool_h, dve_h = attention_handlers() if "at" in phases else (None,) * 5

        def sp_attention(sp):
            if "f1" in phases:
                sp.wait_ge(F[1]["x_done"], CHUNKS)
            for i, w in enumerate((Wq, Wk, Wv)):
                sp.dma_start(wqkv[:, i, :], w).then_inc(a["w_loaded"], 16)
            sp.wait_ge(a["zeroed"], 1)
            for j in range(4):
                sp.dma_start(wo_rep[32 * j:32 * j + HD, :, :],
                             Wo.rearrange("(g j d) n -> j d g n", j=4, d=HD)[j]).then_inc(a["wo_loaded"], 16)

        def pool_attention(pool):
            if "f1" in phases:
                pool.wait_ge(F[1]["x_done"], CHUNKS)
            pool.memset(wo_rep, 0.0).then_inc(a["zeroed"], 1)
            pool.memset(wq_rep, 0.0)
            pool.memset(wk_rep, 0.0).then_inc(a["zeroed"], 1)
            pool.wait_ge(a["zeroed"], 2)
            pool.wait_ge(a["w_loaded"], 16 * 3)
            for rep_, i in ((wq_rep, 0), (wk_rep, 1)):
                for r in range(3):
                    ins = pool.tensor_copy(rep_[:, :, HD * r:HD * (r + 1)],
                                           wqkv[:, i, :].rearrange("p (h d) -> p h d", d=HD))
            ins.then_inc(a["w_rep"], 1)
            pool.memset(weights[:, GROUPS - 1, :].bitcast(F32), 0.0).then_inc(a["zeroed"], 1)
            pool.sem_inc(a["lo_ready"], 2)
            with pool.Fori(0, CHUNKS // 2) as c2:
                for u in range(2):
                    pool.wait_ge(a["hi_ready"], c2 * 2 + (u + 1))
                    cols = bass.ds(c2 * (2 * CHUNK) + u * CHUNK, CHUNK)
                    pool.tensor_tensor(t_lo[:, cols], xT32[:, u, :], t_hi[:, cols],
                                       ALU.subtract).then_inc(a["lo_ready"], 1)
            pool.wait_ge(s_band, 1)
            run_plan(pool, pool_h)

        def act_attention(act):
            act.wait_ge(a["stats"], 1)
            act.activation(tmp0[:], var[:], ACT.Sqrt).then_inc(a["sd"], 1)
            with act.Fori(0, CHUNKS // 2) as c2:
                for u in range(2):
                    c1 = c2 * 2 + (u + 1)
                    act.wait_ge(a["tr_full"], c1 + 2)
                    act.wait_ge(a["lo_ready"], c1)
                    act.activation(xT32[:, u, :], bank[u], ACT.Identity).then_inc(a["xT_ready"], 1)
                    act.wait_ge(a["xT_ready"], c1 + 2)
                    act.activation(t_hi[:, bass.ds(c2 * (2 * CHUNK) + u * CHUNK, CHUNK)], xT32[:, u, :],
                                   ACT.Identity).then_inc(a["hi_ready"], 1)
            act.wait_ge(a["w_rep"], 1)
            for hi, src in ((wq_hi, wq_rep), (wk_hi, wk_rep)):
                act.activation(hi.rearrange("p g c -> p (g c)"), src.rearrange("p h r -> p (h r)"), ACT.Identity)
            act.activation(wv_hi, wqkv[:, 2, :], ACT.Identity).then_inc(a["w_hi"], 1)
            act.wait_ge(a["lo_ready"], CHUNKS + 2)
            act.wait_ge(a["w_lo"], 1)
            act.wait_ge(a["zeroed"], 3)
            act.wait_ge(s_zero, 2)
            run_plan(act, act_h)

        def pe_attention(pe):
            pe.sem_inc(a["tr_full"], 2)
            with pe.Fori(0, CHUNKS // 2) as c2:
                for u in range(2):
                    c1 = c2 * 2 + (u + 1)
                    pe.wait_ge(a["xT_ready"], c1)
                    pe_transpose_chunk(pe, u, a["xn_ready"], a["tr_full"], c1)
            pe.wait_ge(a["lo_ready"], CHUNKS + 2)
            pe.wait_ge(a["hi_ready"], CHUNKS)
            pe.wait_ge(a["w_lo"], 1)
            pe.wait_ge(a["wo_loaded"], 16 * 4)
            pe.wait_ge(a["xT_ready"], CHUNKS + 2)
            run_plan(pe, pe_h)

        def dve_attention(dve):
            dve_stats(dve, a["stats"], a["sd"], range(TILES - TPC if "f1" in phases else 0, TILES))
            dve.sem_inc(a["xT_ready"], 2)
            dve_normalise(dve, a["xn_ready"], a["tr_full"])
            if "f1" not in phases:
                for step in range(BAND_STEPS):
                    dve_band(dve, step)
            dve.wait_ge(a["w_hi"], 1)
            for lo, hi, src in ((wq_lo, wq_hi, wq_rep), (wk_lo, wk_hi, wk_rep)):
                dve.tensor_tensor(lo.rearrange("p g c -> p (g c)"), src.rearrange("p h r -> p (h r)"),
                                  hi.rearrange("p g c -> p (g c)"), ALU.subtract)
            dve.tensor_tensor(wv_lo, wqkv[:, 2, :], wv_hi, ALU.subtract).then_inc(a["w_lo"], 1)
            dve.wait_ge(a["xn_ready"], CHUNKS)
            dve.tensor_tensor(X[:], X[:], bo_bc[:].unsqueeze(1).to_broadcast([P, TILES, P]),
                              ALU.add).then_inc(a["bo_added"], 1)
            dve.wait_ge(a["bo_added"], 1)
            dve.wait_ge(a["w_lo"], 1)
            dve.wait_ge(a["zeroed"], 3)
            dve.wait_ge(s_zero, 2)
            for g in range(GROUPS - 1):
                ins = dve.memset(weights[:, g, :].bitcast(F32), 0.0)
            link(dve, ins)
            run_plan(dve, dve_h)
            dve.wait_ge(a["x_added"], BATCH * GROUPS * 2)


        def sp_expert_weights(sp, n):
            if n:
                sp.wait_ge(a["td_ready"], BATCH * GROUPS * QT)
            sp.dma_start(stage[:, 0, :].rearrange("p (e h) -> p e h", e=EXPERTS),
                         W1.rearrange("e d h -> d e h")).then_inc(s_stage, 16)
            if n:
                sp.wait_ge(a["x_added"], BATCH * GROUPS * 2)
            sp.dma_start(stage[:, 1, :].rearrange("p (e t d) -> p e t d", e=EXPERTS, t=HT),
                         W2.rearrange("e (t p) d -> p e t d", p=P)).then_inc(s_stage2, 16)

        def act_expert_weights(act, n):
            if n:
                act.wait_ge(a["k_ready"], BATCH * GROUPS * 2 + 2)
            act.wait_ge(s_stage, 16 * (n + 1))
            act.activation(weights[:, 0, :], stage[:, 0, :], ACT.Identity).then_inc(s_hi, 1)

        FIRST_LOW = 2 * HID

        def pool_expert_weights(pool, n, cols):
            pool.wait_ge(s_hi, n + 1)
            pool.tensor_tensor(weights[:, 1, cols], stage[:, 0, cols], weights[:, 0, cols],
                               ALU.subtract).then_inc(s_lo, 1)

        def dve_expert_weights(dve, n):
            dve.wait_ge(s_stage2, 16 * (n + 1))
            dve.tensor_copy(weights[:, 2, :], stage[:, 1, :]).then_inc(s_hi2, 1)
            dve.wait_ge(s_hi2, n + 1)
            dve.tensor_tensor(weights[:, 3, :], stage[:, 1, :], weights[:, 2, :], ALU.subtract).then_inc(s_lo2, 1)

        @block.sync
        def _(sp):
            for b in range(BATCH):
                sp.dma_start(X[:, QT * b:QT * (b + 1), :],
                             x[b].rearrange("(t p) d -> p t d", p=P)).then_inc(s_x[b], 16)
            sp.dma_start(C[:], cst).then_inc(s_w, 16)
            sp.dma_start(w_in[:], W_in).then_inc(s_w, 16)
            sp.dma_start(w_gate[:], W_gate).then_inc(s_w, 16)
            sp.dma_start(b_in_col[:], b_in.rearrange("(p a) -> p a", a=1)).then_inc(s_w, 16)
            sp.dma_start(b_gate_bc[:], b_gate.partition_broadcast(P)).then_inc(s_w, 16)
            sp.dma_start(b1_rows[:], b1.rearrange("e (t p) -> (e t) p", p=P)).then_inc(s_w, 16)
            sp.dma_start(b2_rows[:], b2).then_inc(s_w, 16)
            sp.dma_start(w_out[:], W_out).then_inc(s_w, 16)
            sp.dma_start(half_b_out[:], b_out.partition_broadcast(P)).then_inc(s_w, 16)
            sp.dma_start(bo_bc[:], bo.partition_broadcast(P)).then_inc(s_w, 16)
            sp.dma_start(rel_bc[:], rel_emb.partition_broadcast(P)).then_inc(s_w, 16)
            if "f1" in phases:
                sp_expert_weights(sp, 0)
            if "at" in phases:
                sp_attention(sp)
            if "f2" in phases:
                sp_expert_weights(sp, 1)
            last = F[2] if "f2" in phases else None
            for c in range(CHUNKS):
                if last:
                    sp.wait_ge(last["x_done"], c + 1)
                else:
                    sp.wait_ge(s_in_done, 1)
                b, r = c // 2, c % 2
                sp.dma_start(out[b, CHUNK * r:CHUNK * (r + 1), :].rearrange("(t p) d -> p t d", p=P),
                             X[:, TPC * c:TPC * (c + 1), :]).then_inc(s_out, 16)
            sp.wait_ge(s_out, 16 * CHUNKS)

        N_W = 16 * 11

        def dve_ffn(dve, f, n):
            dve_stats(dve, f["stats"], f["sd"], range(TILES - 1 if n == 1 else TILES - QT, TILES))

            def tokens_copy(c, u):
                dve.wait_ge(f["tr_full"], c + 3)
                dve.wait_ge(f["h_full"], c + 1)
                dve.tensor_copy(xnT[:, u, :], bank[u]).then_inc(f["xnT_ready"], 1)

            normalise(dve, 0, 0, f["xn_ready"], f["tr_full"])
            normalise(dve, 1, 1, f["xn_ready"], f["tr_full"])
            with dve.Fori(0, CHUNKS // 2 - 1) as c2:
                for u in range(2):
                    tokens_copy(c2 * 2 + u, u)
                    normalise(dve, c2 * 2 + (u + 2), u, f["xn_ready"], f["tr_full"])
            tokens_copy(CHUNKS - 2, 0)
            tokens_copy(CHUNKS - 1, 1)
            dve_expert_weights(dve, n - 1)
            bc = [P, TILES, EXPERTS]
            ordb = order[:].unsqueeze(1).to_broadcast(bc)

            def largest(src, oh, top):
                link(dve, dve.tensor_reduce(top, src, AXX, ALU.max))
                link(dve, dve.tensor_tensor(oh, src, top.unsqueeze(2).to_broadcast(bc), ALU.is_ge))
                link(dve, dve.tensor_tensor(oh, oh, ordb, ALU.mult))
                link(dve, dve.tensor_reduce(rt1, oh, AXX, ALU.max))
                link(dve, dve.tensor_tensor(oh, ordb, rt1.unsqueeze(2).to_broadcast(bc), ALU.is_equal))

            def route_first():
                dve.wait_ge(f["lg_ready"], CHUNKS)
                link(dve, dve.tensor_tensor(logits, logits, b_gate_bc[:].unsqueeze(1).to_broadcast(bc), ALU.add))
                largest(logits, oh1, top1)

            def route_second():
                link(dve, dve.scalar_tensor_tensor(out=rtmp, in0=oh1, scalar=LOWEST, in1=logits,
                                                   op0=ALU.mult, op1=ALU.add))
                largest(rtmp, oh2, top2)
                dve.tensor_tensor(rt1, top2, top1, ALU.subtract).then_inc(f["rt_d"], 1)

            def route_weights():
                dve.wait_ge(f["rt_e"], 1)
                link(dve, dve.tensor_scalar(top1, rt2, 1.0, None, ALU.add))
                link(dve, dve.reciprocal(top2, top1))
                link(dve, dve.tensor_tensor(rt2, rt2, top2, ALU.mult))
                link(dve, dve.tensor_tensor(oh1, oh1, top2.unsqueeze(2).to_broadcast(bc), ALU.mult))
                link(dve, dve.tensor_tensor(oh2, oh2, rt2.unsqueeze(2).to_broadcast(bc), ALU.mult))
                link(dve, dve.tensor_tensor(route, oh1, oh2, ALU.add))

            dve.sem_inc(f["fa_full"], 1)
            dve.sem_inc(f["acc_chain"], 2)

            def parts(c, e):
                s = e % 2
                dve.wait_ge(f["dn_full"], c * EXPERTS + (e + 1))
                for ht in range(HT):
                    dve.wait_ge(f["mid32_ready"], c * 32 + (HT * e + ht + 1 + HT))
                    if ht % 2:
                        dve.tensor_copy(mid_hi[:, s, ht, :], mid32[:, ht, :]).then_inc(f["hi_dve"], 1)
                        dve.wait_ge(f["hi_dve"], c * 16 + (2 * e + ht // 2 + 1))
                    else:
                        dve.wait_ge(f["hi_act"], c * 16 + (2 * e + ht // 2 + 1))
                    dve.tensor_tensor(mid_lo[:, s, ht, :], mid32[:, ht, :], mid_hi[:, s, ht, :],
                                      ALU.subtract).then_inc(f["lo_done"], 1)

            def add_expert(c, d):
                dve.wait_ge(f["dn_full"], c * EXPERTS + (d + 3))
                if d == 0:
                    dve.wait_ge(f["fa_full"], c + 1)
                else:
                    dve.wait_ge(f["acc_chain"], c * EXPERTS + (d + 2))
                y = bank[4 + d % 2].rearrange("p (t d) -> p t d", t=TPC)
                for k in range(TPC):
                    r = route_c[:, k, d % EXPERTS:d % EXPERTS + 1]
                    if d == 0:
                        ins = dve.tensor_scalar(acc[:, k, :], y[:, k, :], r, None, ALU.mult)
                    else:
                        ins = dve.scalar_tensor_tensor(out=acc[:, k, :], in0=y[:, k, :], scalar=r,
                                                       in1=acc[:, k, :], op0=ALU.mult, op1=ALU.add)
                ins.then_inc(f["acc_chain"], 1)

            def add_output(c):
                Xc = X[:, bass.ds(c * TPC - TPC, TPC), :]
                dve.tensor_tensor(Xc, Xc, half_b_out[:].unsqueeze(1).to_broadcast([P, TPC, P]),
                                  ALU.add).then_inc(f["fa_chain"], 1)
                dve.wait_ge(f["fa_chain"], c)
                dve.wait_ge(f["fb_full"], c)
                dve.scalar_tensor_tensor(out=Xc, in0=bank[7].rearrange("p (t d) -> p t d", t=TPC),
                                         scalar=0.5, in1=Xc, op0=ALU.mult, op1=ALU.add).then_inc(f["x_done"], 1)

            def output_stats(c):
                dve.wait_ge(f["x_done"], c)
                for k in range(TPC):
                    t = bass.ds(c * TPC + (k - TPC), 1)
                    dve.bn_stats(bn[:, t, :].rearrange("p a s -> p (a s)"), X[:, t, :].rearrange("p a d -> p (a d)"))

            def chunk(c, first):
                for e in range(EXPERTS):
                    parts(c, e)
                    if n == 1 and e == 4 and not first:
                        output_stats(c)
                    if first and e <= 2:
                        (route_first, route_second, route_weights)[e]()
                    if e and not (first and e <= 2) or not first:
                        add_expert(c, e - 1)
                    if e == (2 if first else 0):
                        if not first:
                            dve.wait_ge(f["rT_full"], c)
                            dve.wait_ge(f["acc_chain"], c * EXPERTS + 2)
                        dve.tensor_copy(route_c, route[:, bass.ds(c * TPC, TPC), :]).then_inc(f["rc_ready"], 1)
                        dve.wait_ge(f["rc_ready"], c + 1)
                        if first:
                            add_expert(c, 0)
                            add_expert(c, 1)
                    if e == 2 and not first:
                        add_output(c)
                    if n == 1 and first and e >= 2:
                        dve_band(dve, e - 2)

            chunk(0, True)
            with dve.Fori(1, CHUNKS) as c:
                chunk(c, False)
            add_expert(CHUNKS, -1)
            add_output(CHUNKS)
            dve.wait_ge(f["x_done"], CHUNKS)

        def act_ffn(act, f, n):
            if n == 2:
                act_expert_weights(act, n - 1)
            act.wait_ge(f["stats"], 1)
            act.activation(tmp0[:], var[:], ACT.Sqrt).then_inc(f["sd"], 1)
            if n == 1:
                act_expert_weights(act, n - 1)

            def hidden_copy(c, u):
                act.wait_ge(f["h_full"], c + 3)
                act.wait_ge(f["lo_ready"], c + 1)
                act.activation(h32[:, u, :], bank[2 + u], ACT.Identity,
                               bias=b_in_col[:]).then_inc(f["h32_ready"], 1)
                act.wait_ge(f["h32_ready"], c + 1)
                act.activation(t_hi[:, bass.ds(c * CHUNK, CHUNK)], h32[:, u, :],
                               ACT.Identity).then_inc(f["hi_ready"], 1)

            def logits_copy(c, u):
                act.wait_ge(f["lg_full"], c + 1)
                act.activation(logits[:, bass.ds(c * TPC, TPC), :],
                               bank[4 + u][:, 0:TPC * EXPERTS].rearrange("p (t e) -> p t e", t=TPC),
                               ACT.Identity).then_inc(f["lg_ready"], 1)

            hidden_copy(0, 0)
            with act.Fori(0, CHUNKS // 2 - 1) as c2:
                for u in range(2):
                    c = c2 * 2 + (u + 1)
                    hidden_copy(c, 1 - u)
                    logits_copy(c2 * 2 + u, u)
            hidden_copy(CHUNKS - 1, 1)
            logits_copy(CHUNKS - 2, 0)
            logits_copy(CHUNKS - 1, 1)
            act.sem_inc(f["mid32_ready"], HT)

            def sum_copy(c):
                act.wait_ge(f["fa_full"], c + 1)
                act.activation(moT, bank[6], ACT.Identity).then_inc(f["fa_ready"], 1)

            def chunk(c, first):
                for e in range(EXPERTS):
                    s = e % 2
                    if e == 2 and not first:
                        sum_copy(c)
                    if e == 5:
                        act.wait_ge(f["rT_full"], c + 1)
                        act.wait_ge(f["fa_full"], c + 1)
                        act.activation(routeT, bank[7][0:EXPERTS, :], ACT.Identity).then_inc(f["rT_ready"], 1)
                    act.wait_ge(f["dn_full"], c * EXPERTS + (e + 1))
                    for ht in range(HT):
                        i = HT * e + ht
                        act.wait_ge(f["up_full"], c * 32 + (i + 1))
                        act.wait_ge(f["lo_done"], c * 32 + (i + 1))
                        act.activation(mid32[:, ht, :], bank[ht], ACT.Relu,
                                       bias=b1_cols[:, i:i + 1]).then_inc(f["mid32_ready"], 1)
                        if ht % 2:
                            act.wait_ge(f["mid32_ready"], c * 32 + (i + HT))
                            act.activation(mid_hi[:, s, ht - 1, :], mid32[:, ht - 1, :],
                                           ACT.Identity).then_inc(f["hi_act"], 1)
                    if e == 2 and first:
                        act.wait_ge(f["rt_d"], 1)
                        act.activation(rt2, rt1, ACT.Exp).then_inc(f["rt_e"], 1)

            chunk(0, True)
            with act.Fori(1, CHUNKS) as c:
                chunk(c, False)
            sum_copy(CHUNKS)

        def pe_transpose_chunk(pe, u, xn_ready, tr_full, c1):
            pe.wait_ge(xn_ready, c1)
            for k in range(TPC):
                ins = pe.matmul(bank[u][:, P * k:P * (k + 1)], xn[:, u, k, :], ident, start=(k == 0), stop=True,
                                is_transpose=True, skip_group_check=True)
            ins.then_inc(tr_full, 1)

        def pe_ffn(pe, f, n):
            pe.sem_inc(f["h_full"], 2)
            pe.sem_inc(f["tr_full"], 2)

            def transposes(c, u):
                pe_transpose_chunk(pe, u, f["xn_ready"], f["tr_full"], c + 1)

            def hidden(c, u):
                pe.wait_ge(f["xnT_ready"], c + 1)
                pe.matmul(bank[2 + u], w_in[:], xnT[:, u, :], start=True, stop=True).then_inc(f["h_full"], 1)

            def gate(c, u):
                pe.wait_ge(f["h32_ready"], c + 1)
                for k in range(TPC):
                    ins = pe.matmul(bank[4 + u][:, EXPERTS * k:EXPERTS * (k + 1)], h32[:, u, P * k:P * (k + 1)],
                                    w_gate[:], start=(k == 0), stop=True, skip_group_check=True)
                ins.then_inc(f["lg_full"], 1)

            transposes(0, 0)
            transposes(1, 1)
            hidden(0, 0)
            with pe.Fori(0, CHUNKS // 2 - 1) as c2:
                for u in range(2):
                    c = c2 * 2 + (u + 1)
                    transposes(c + 1, u)
                    hidden(c, 1 - u)
                    gate(c2 * 2 + u, u)
            hidden(CHUNKS - 1, 1)
            gate(CHUNKS - 2, 0)
            gate(CHUNKS - 1, 1)
            pe.wait_ge(s_lo, 2 * n - 1)
            pe.wait_ge(s_b1, 1)
            pe.wait_ge(f["lo_ready"], CHUNKS + 2)
            pe.wait_ge(f["hi_ready"], CHUNKS)
            pe.wait_ge(f["lg_ready"], CHUNKS)
            pe.sem_inc(f["lo_done"], HT)
            pe.sem_inc(f["dn_full"], 2)

            def up(c, e):
                cols = bass.ds(c * CHUNK, CHUNK)
                for ht in range(HT):
                    i = HT * e + ht
                    pe.wait_ge(f["mid32_ready"], c * 32 + (i + 1))
                    w_h, w_l = w1_hi[:, e, P * ht:P * (ht + 1)], w1_lo[:, e, P * ht:P * (ht + 1)]
                    pe.matmul(bank[ht], w_h, t_hi[:, cols], start=True, stop=False)
                    pe.matmul(bank[ht], w_h, t_lo[:, cols], start=False, stop=False)
                    pe.matmul(bank[ht], w_l, t_hi[:, cols], start=False, stop=True).then_inc(f["up_full"], 1)

            def down(c, d):
                s, w = d % 2, d % EXPERTS
                pe.wait_ge(f["hi_act"], c * 16 + (2 * d + 2))
                pe.wait_ge(f["lo_done"], c * 32 + (HT * d + 2 * HT))
                pe.wait_ge(f["acc_chain"], c * EXPERTS + (d + 1))
                for k in range(TPC):
                    tok = slice(P * k, P * (k + 1))
                    for ht in range(HT):
                        m_h, m_l = mid_hi[:, s, ht, tok], mid_lo[:, s, ht, tok]
                        o = bank[4 + s][:, tok]
                        pe.matmul(o, m_h, w2_hi[:, w, ht, :], start=(k == 0 and ht == 0), stop=False,
                                  skip_group_check=True)
                        pe.matmul(o, m_h, w2_lo[:, w, ht, :], start=False, stop=False,
                                  skip_group_check=True)
                        ins = pe.matmul(o, m_l, w2_hi[:, w, ht, :], start=False, stop=(ht == HT - 1),
                                        skip_group_check=True)
                ins.then_inc(f["dn_full"], 1)

            def transpose_sum(c):
                pe.wait_ge(f["acc_chain"], c * EXPERTS + 2)
                for k in range(TPC):
                    pe.matmul(bank[6][:, P * k:P * (k + 1)], acc[:, k, :], ident, start=(k == 0), stop=True,
                              is_transpose=True, skip_group_check=True)
                pe.wait_ge(f["rT_ready"], c)
                pe.matmul(bank[6], b2_rows[:], routeT, start=False, stop=True,
                          skip_group_check=True).then_inc(f["fa_full"], 1)

            def output(c):
                pe.wait_ge(f["fa_ready"], c)
                for k in range(TPC):
                    ins = pe.matmul(bank[7][:, P * k:P * (k + 1)], moT[:, P * k:P * (k + 1)], w_out[:],
                                    start=(k == 0), stop=True, skip_group_check=True)
                ins.then_inc(f["fb_full"], 1)

            def chunk(c, first):
                for e in range(EXPERTS):
                    if first and e == 2:
                        pe.wait_ge(s_lo, 2 * n)
                    up(c, e)
                    if e == 1 and not first:
                        transpose_sum(c)
                    if e == 2 and not first:
                        output(c)
                    if e or not first:
                        if e == 0 or (e == 1 and first):
                            pe.wait_ge(s_lo2, n)
                        down(c, e - 1)
                    if e == 4:
                        pe.wait_ge(f["rc_ready"], c + 1)
                        if not first:
                            pe.wait_ge(f["x_done"], c)
                        for k in range(TPC):
                            ins = pe.matmul(bank[7][0:EXPERTS, P * k:P * (k + 1)], route_c[:, k, :], ident,
                                            start=(k == 0), stop=True, is_transpose=True, skip_group_check=True)
                        ins.then_inc(f["rT_full"], 1)

            chunk(0, True)
            with pe.Fori(1, CHUNKS) as c:
                chunk(c, False)
            down(CHUNKS, -1)
            transpose_sum(CHUNKS)
            output(CHUNKS)

        def pool_ffn(pool, f, n):
            pool_expert_weights(pool, n - 1, slice(0, FIRST_LOW))
            pool.sem_inc(f["lo_ready"], 2)
            with pool.Fori(0, CHUNKS // 2) as c2:
                for u in range(2):
                    pool.wait_ge(f["hi_ready"], c2 * 2 + (u + 1))
                    cols = bass.ds(c2 * (2 * CHUNK) + u * CHUNK, CHUNK)
                    pool.tensor_tensor(t_lo[:, cols], h32[:, u, :], t_hi[:, cols],
                                       ALU.subtract).then_inc(f["lo_ready"], 1)
            pool_expert_weights(pool, n - 1, slice(FIRST_LOW, W_PART))

        @block.gpsimd
        def _(pool):
            for e in range(EXPERTS):
                ins = pool.memset(order[:, e:e + 1], float(EXPERTS - e))
            ins.then_inc(s_cst, 1)
            pool.memset(M4, 0.0)
            pool.memset(E, 0.0)
            pool.memset(mxp, LOWEST)
            pool.memset(vaug, 0.0).then_inc(s_zero, 1)
            pool.wait_ge(s_zero, 1)
            pool.memset(vaug[:, :, :, HD:HD + 1], 1.0).then_inc(s_zero, 1)
            if "f1" in phases:
                pool_ffn(pool, F[1], 1)
            if "at" in phases:
                pool_attention(pool)
            if "f2" in phases:
                pool_ffn(pool, F[2], 2)

        @block.vector
        def _(dve):
            for b in range(BATCH):
                dve.wait_ge(s_x[b], 16)
                link(dve, tile_stats(dve, range(QT * b, QT * (b + 1))))
            dve.wait_ge(s_w, N_W)
            dve.tensor_copy(ident_bf[:], ident)
            dve.tensor_copy(neg_bf[:], C[:, C_NEG:C_NEG + P])
            link(dve, dve.tensor_scalar(half_b_out[:], half_b_out[:], 0.5, None, ALU.mult))
            dve.wait_ge(s_b1T, 1)
            dve.tensor_copy(b1_cols[:], bank[6][:, 0:EXPERTS * HT]).then_inc(s_b1, 1)
            dve.wait_ge(s_cst, 1)
            if "f1" in phases:
                dve_ffn(dve, F[1], 1)
            if "at" in phases:
                dve_attention(dve)
            if "f2" in phases:
                dve_ffn(dve, F[2], 2)
            dve.sem_inc(s_in_done, 1)

        @block.scalar
        def _(act):
            act.wait_ge(s_w, N_W)
            if "f1" in phases:
                act_ffn(act, F[1], 1)
            if "at" in phases:
                act_attention(act)
            if "f2" in phases:
                act_ffn(act, F[2], 2)

        @block.tensor
        def _(pe):
            pe.wait_ge(s_w, N_W)
            pe.transpose(bank[6][:, 0:EXPERTS * HT], b1_rows[:], C[0:EXPERTS * HT, C_ID:C_ID + EXPERTS * HT]).then_inc(s_b1T, 1)
            if "f1" in phases:
                pe_ffn(pe, F[1], 1)
            if "at" in phases:
                pe_attention(pe)
            if "f2" in phases:
                pe_ffn(pe, F[2], 2)


_INS = ["L0_attn_x", "L0_attn_Wq", "L0_attn_Wk", "L0_attn_Wv", "L0_attn_Wo", "L0_attn_bo", "L0_attn_rel_emb",
        "L0_ffn_W_in", "L0_ffn_b_in", "L0_ffn_W_gate", "L0_ffn_b_gate", "L0_ffn_W1", "L0_ffn_b1", "L0_ffn_W2",
        "L0_ffn_b2", "L0_ffn_W_out", "L0_ffn_b_out"]


def kernel(**inputs):
    import numpy as _np
    import concourse.bacc as _bacc
    from concourse import mybir as _mybir
    from concourse.bass_utils import run_bass_kernel_spmd as _run

    nc = _bacc.Bacc("TRN2", target_bir_lowering=False, num_devices=1)
    arrays, args = {}, []
    for name in _INS:
        a = _np.ascontiguousarray(inputs[name])
        arrays[f"in_{name}"] = a
        args.append(nc.dram_tensor(f"in_{name}", a.shape, _mybir.dt.from_np(a.dtype), kind="ExternalInput").ap())
    c = consts()
    arrays["consts"] = c
    args.append(nc.dram_tensor("consts", c.shape, _mybir.dt.float32, kind="ExternalInput").ap())
    args.append(nc.dram_tensor("out_0", (BATCH, SEQ, P), _mybir.dt.float32, kind="ExternalOutput").ap())
    build(nc, *args)
    r = _run(nc, [arrays], core_ids=[0])
    return r.results[0]["out_0"]
```
